# Optimizing a Trainium2 kernel written in Bass

```python
import numpy as np
import jax
import jax.numpy as jnp

def _softmax(x, axis=-1):
    return jax.nn.softmax(x, axis=axis)

def _gelu(x):
    return jax.nn.gelu(x, approximate=True)

def _silu(x):
    return jax.nn.silu(x)

def _sigmoid(x):
    return jax.nn.sigmoid(x)

def _layernorm(x, axis=-1, eps=1e-05):
    m = jnp.mean(x, axis=axis, keepdims=True)
    v = jnp.var(x, axis=axis, keepdims=True)
    return (x - m) / jnp.sqrt(v + eps)

def _scatter_add(tgt, idx, src, axis=0):
    return tgt.at[idx].add(src)

def _segment_sum(src, seg, n):
    return jax.ops.segment_sum(src, seg, n)
kernel_name = 'mk_gnn_ffn_d1_gnn_r8_ffdf5d'

def setup_inputs(seed: int=0):
    np.random.seed(seed)
    _w = jnp.asarray

    def _rec_inputs():
        import jax
        import jax.numpy as jnp
        _gk = jax.random.key(seed)
        x = -0.0003713 + 1 * jax.random.normal(jax.random.fold_in(_gk, 1), (6250, 256), jnp.float32)
        _s = jax.random.randint(jax.random.fold_in(_gk, 2), (50000,), 0, 6250, jnp.int32)
        _d = jax.random.randint(jax.random.fold_in(_gk, 3), (50000,), 0, 6250, jnp.int32)
        _loop = jnp.arange(6250, dtype=jnp.int32)
        src = jnp.concatenate([_s, _d, _loop])
        dst = jnp.concatenate([_d, _s, _loop])
        _o = jnp.argsort(dst, stable=True)
        src = src[_o]
        dst = dst[_o]
        node_type_24 = jax.random.randint(jax.random.fold_in(_gk, 12), (6250,), 0, 24, jnp.int32)
        return (x, src, dst, node_type_24)
    x, src, dst, node_type_24 = _rec_inputs()

    def _L0_gnn_setup():
        import jax, jax.numpy as jnp
        import numpy as np
        N = 6250
        E = 100000
        F_IN = 256
        HID = 64
        H = 4
        NC = 23
        NEG_SLOPE = 0.2

        def _gat_layer(h, W, attn_l, attn_r, bias, src, dst):
            feat = (h @ W.T).reshape(-1, H, HID)
            el = jnp.einsum('nhd,hd->nh', feat, attn_l)
            er = jnp.einsum('nhd,hd->nh', feat, attn_r)
            e = jax.nn.leaky_relu(el[src] + er[dst], NEG_SLOPE)
            m = jax.ops.segment_max(e, dst, num_segments=N)
            m = jnp.where(jnp.isfinite(m), m, 0.0)
            ex = jnp.exp(e - m[dst])
            den = jax.ops.segment_sum(ex, dst, num_segments=N)
            a = ex / jnp.maximum(den[dst], 1e-09)
            out = jax.ops.segment_sum(a[:, :, None] * feat[src], dst, num_segments=N)
            out = out + bias.reshape(1, H, HID)
            return jax.nn.relu(out).reshape(-1, H * HID)
        key = jax.random.key(seed)
        ks = jax.random.split(key, 18)
        s = 0.05
        emb = jax.random.normal(ks[4], (NC + 1, F_IN), jnp.float32) * s
        emb = emb.at[NC].set(0.0)
        return {'features': jax.random.normal(ks[0], (N, F_IN), jnp.float32), 'input_labels': jax.random.randint(ks[1], (N,), 0, NC + 1), 'src': jax.random.randint(ks[2], (E,), 0, N), 'dst': jax.random.randint(ks[3], (E,), 0, N), 'emb': emb, 'le_W1': jax.random.normal(ks[5], (4 * F_IN, 2 * F_IN), jnp.float32) * s, 'le_b1': jnp.zeros((4 * F_IN,), jnp.float32), 'ln_g': jnp.ones((4 * F_IN,), jnp.float32), 'ln_b': jnp.zeros((4 * F_IN,), jnp.float32), 'le_W2': jax.random.normal(ks[6], (F_IN, 4 * F_IN), jnp.float32) * s, 'le_b2': jnp.zeros((F_IN,), jnp.float32), 'W1': jax.random.normal(ks[7], (H * HID, F_IN), jnp.float32) * s, 'al1': jax.random.normal(ks[8], (H, HID), jnp.float32) * s, 'ar1': jax.random.normal(ks[9], (H, HID), jnp.float32) * s, 'b1': jnp.zeros((H * HID,), jnp.float32), 'W2': jax.random.normal(ks[10], (H * HID, H * HID), jnp.float32) * s, 'al2': jax.random.normal(ks[11], (H, HID), jnp.float32) * s, 'ar2': jax.random.normal(ks[12], (H, HID), jnp.float32) * s, 'b2': jnp.zeros((H * HID,), jnp.float32)}
    _L0_gnn_all = _L0_gnn_setup()
    _L0_gnn_in = {k: v for k, v in _L0_gnn_all.items() if k in ('emb', 'le_W1', 'le_b1', 'ln_g', 'ln_b', 'le_W2', 'le_b2', 'W1', 'al1', 'ar1', 'b1', 'W2', 'al2', 'ar2', 'b2')}
    del _L0_gnn_all

    def _L0_ffn_setup():
        import jax, jax.numpy as jnp
        import numpy as np
        DIM = 256
        H = 8
        D = 64
        G = 64
        INNER = H * D
        SCALE = D ** (-0.5)
        key = jax.random.key(seed)
        ks = jax.random.split(key, 12)
        B, N = (4, 2048)
        x = jax.random.normal(ks[0], (B, N, DIM), dtype=jnp.float32)
        s = lambda fan_in: 1.0 / np.sqrt(fan_in)
        W_fx = jax.random.normal(ks[1], (DIM, INNER), dtype=jnp.float32) * s(DIM)
        b_fx = jnp.zeros((INNER,), dtype=jnp.float32)
        W_x = jax.random.normal(ks[2], (DIM, INNER), dtype=jnp.float32) * s(DIM)
        b_x = jnp.zeros((INNER,), dtype=jnp.float32)
        A = jax.random.normal(ks[3], (G, D), dtype=jnp.float32)
        Q, _ = jnp.linalg.qr(A.T)
        W_slice = Q[:, :G].astype(jnp.float32)
        b_slice = jnp.zeros((G,), dtype=jnp.float32)
        W_q = jax.random.normal(ks[4], (D, D), dtype=jnp.float32) * s(D)
        W_k = jax.random.normal(ks[5], (D, D), dtype=jnp.float32) * s(D)
        W_v = jax.random.normal(ks[6], (D, D), dtype=jnp.float32) * s(D)
        W_out = jax.random.normal(ks[7], (INNER, DIM), dtype=jnp.float32) * s(INNER)
        b_out = jnp.zeros((DIM,), dtype=jnp.float32)
        temperature = jnp.ones((1, H, 1, 1), dtype=jnp.float32) * 0.5
        return {'x': x, 'W_fx': W_fx, 'b_fx': b_fx, 'W_x': W_x, 'b_x': b_x, 'W_slice': W_slice, 'b_slice': b_slice, 'W_q': W_q, 'W_k': W_k, 'W_v': W_v, 'W_out': W_out, 'b_out': b_out, 'temperature': temperature}
    _L0_ffn_all = _L0_ffn_setup()
    _L0_ffn_in = {k: v for k, v in _L0_ffn_all.items() if k in ('W_fx', 'b_fx', 'W_x', 'b_x', 'W_slice', 'b_slice', 'W_q', 'W_k', 'W_v', 'W_out', 'b_out', 'temperature')}
    del _L0_ffn_all
    return {'x': x, 'src': src, 'dst': dst, 'node_type_24': node_type_24, 'L0_gnn_emb': _L0_gnn_in['emb'], 'L0_gnn_le_W1': _L0_gnn_in['le_W1'], 'L0_gnn_le_b1': _L0_gnn_in['le_b1'], 'L0_gnn_ln_g': _L0_gnn_in['ln_g'], 'L0_gnn_ln_b': _L0_gnn_in['ln_b'], 'L0_gnn_le_W2': _L0_gnn_in['le_W2'], 'L0_gnn_le_b2': _L0_gnn_in['le_b2'], 'L0_gnn_W1': _L0_gnn_in['W1'], 'L0_gnn_al1': _L0_gnn_in['al1'], 'L0_gnn_ar1': _L0_gnn_in['ar1'], 'L0_gnn_b1': _L0_gnn_in['b1'], 'L0_gnn_W2': _L0_gnn_in['W2'], 'L0_gnn_al2': _L0_gnn_in['al2'], 'L0_gnn_ar2': _L0_gnn_in['ar2'], 'L0_gnn_b2': _L0_gnn_in['b2'], 'L0_ffn_W_fx': _L0_ffn_in['W_fx'], 'L0_ffn_b_fx': _L0_ffn_in['b_fx'], 'L0_ffn_W_x': _L0_ffn_in['W_x'], 'L0_ffn_b_x': _L0_ffn_in['b_x'], 'L0_ffn_W_slice': _L0_ffn_in['W_slice'], 'L0_ffn_b_slice': _L0_ffn_in['b_slice'], 'L0_ffn_W_q': _L0_ffn_in['W_q'], 'L0_ffn_W_k': _L0_ffn_in['W_k'], 'L0_ffn_W_v': _L0_ffn_in['W_v'], 'L0_ffn_W_out': _L0_ffn_in['W_out'], 'L0_ffn_b_out': _L0_ffn_in['b_out'], 'L0_ffn_temperature': _L0_ffn_in['temperature']}

def reference(x, src, dst, node_type_24, L0_gnn_emb, L0_gnn_le_W1, L0_gnn_le_b1, L0_gnn_ln_g, L0_gnn_ln_b, L0_gnn_le_W2, L0_gnn_le_b2, L0_gnn_W1, L0_gnn_al1, L0_gnn_ar1, L0_gnn_b1, L0_gnn_W2, L0_gnn_al2, L0_gnn_ar2, L0_gnn_b2, L0_ffn_W_fx, L0_ffn_b_fx, L0_ffn_W_x, L0_ffn_b_x, L0_ffn_W_slice, L0_ffn_b_slice, L0_ffn_W_q, L0_ffn_W_k, L0_ffn_W_v, L0_ffn_W_out, L0_ffn_b_out, L0_ffn_temperature):
    import jax
    import jax.numpy as jnp

    def _L0_gnn_ref(features, emb, le_W1, le_b1, ln_g, ln_b, le_W2, le_b2, W1, al1, ar1, b1, W2, al2, ar2, b2, input_labels, src, dst):
        import jax, jax.numpy as jnp
        import numpy as np
        N = 6250
        E = 100000
        F_IN = 256
        HID = 64
        H = 4
        NC = 23
        NEG_SLOPE = 0.2

        def _gat_layer(h, W, attn_l, attn_r, bias, src, dst):
            feat = (h @ W.T).reshape(-1, H, HID)
            el = jnp.einsum('nhd,hd->nh', feat, attn_l)
            er = jnp.einsum('nhd,hd->nh', feat, attn_r)
            e = jax.nn.leaky_relu(el[src] + er[dst], NEG_SLOPE)
            m = jax.ops.segment_max(e, dst, num_segments=N)
            m = jnp.where(jnp.isfinite(m), m, 0.0)
            ex = jnp.exp(e - m[dst])
            den = jax.ops.segment_sum(ex, dst, num_segments=N)
            a = ex / jnp.maximum(den[dst], 1e-09)
            out = jax.ops.segment_sum(a[:, :, None] * feat[src], dst, num_segments=N)
            out = out + bias.reshape(1, H, HID)
            return jax.nn.relu(out).reshape(-1, H * HID)
        lab = emb[input_labels]
        x = jnp.concatenate([features, lab], axis=-1)
        x = x @ le_W1.T + le_b1
        mu = jnp.mean(x, axis=-1, keepdims=True)
        var = jnp.var(x, axis=-1, keepdims=True)
        x = (x - mu) * jax.lax.rsqrt(var + 1e-05) * ln_g + ln_b
        x = jax.nn.relu(x)
        h = x @ le_W2.T + le_b2
        h = _gat_layer(h, W1, al1, ar1, b1, src, dst)
        h = _gat_layer(h, W2, al2, ar2, b2, src, dst)
        return h

    def _L0_ffn_ref(x, W_fx, b_fx, W_x, b_x, W_slice, b_slice, W_q, W_k, W_v, W_out, b_out, temperature):
        import jax, jax.numpy as jnp
        import numpy as np
        DIM = 256
        H = 8
        D = 64
        G = 64
        INNER = H * D
        SCALE = D ** (-0.5)
        B, N, _ = x.shape
        fx_mid = (x @ W_fx + b_fx).reshape(B, N, H, D).transpose(0, 2, 1, 3)
        x_mid = (x @ W_x + b_x).reshape(B, N, H, D).transpose(0, 2, 1, 3)
        temp = jnp.clip(temperature, 0.1, 5.0)
        slice_weights = jax.nn.softmax((x_mid @ W_slice + b_slice) / temp, axis=-1)
        slice_norm = slice_weights.sum(axis=2)
        slice_token = jnp.einsum('bhnc,bhng->bhgc', fx_mid, slice_weights)
        slice_token = slice_token / (slice_norm[..., None] + 1e-05)
        q = slice_token @ W_q
        k = slice_token @ W_k
        v = slice_token @ W_v
        attn = jax.nn.softmax(jnp.einsum('bhgc,bhkc->bhgk', q, k) * SCALE, axis=-1)
        out_slice = jnp.einsum('bhgk,bhkc->bhgc', attn, v)
        out_x = jnp.einsum('bhgc,bhng->bhnc', out_slice, slice_weights)
        out_x = out_x.transpose(0, 2, 1, 3).reshape(B, N, INNER)
        return out_x @ W_out + b_out
    x = x + _L0_gnn_ref(_layernorm(x, axis=-1), L0_gnn_emb, L0_gnn_le_W1, L0_gnn_le_b1, L0_gnn_ln_g, L0_gnn_ln_b, L0_gnn_le_W2, L0_gnn_le_b2, L0_gnn_W1, L0_gnn_al1, L0_gnn_ar1, L0_gnn_b1, L0_gnn_W2, L0_gnn_al2, L0_gnn_ar2, L0_gnn_b2, node_type_24, src, dst)
    x = x + _L0_ffn_ref(_layernorm(x, axis=-1)[None], L0_ffn_W_fx, L0_ffn_b_fx, L0_ffn_W_x, L0_ffn_b_x, L0_ffn_W_slice, L0_ffn_b_slice, L0_ffn_W_q, L0_ffn_W_k, L0_ffn_W_v, L0_ffn_W_out, L0_ffn_b_out, L0_ffn_temperature)[0]
    return x

_drawn_inputs = setup_inputs


def setup_inputs(seed=0):
    import zlib

    import numpy as np

    out = dict(_drawn_inputs(seed))
    spreads = {'L0_gnn_le_b1': (0.0, 0.1),
     'L0_gnn_ln_g': (1.0, 0.2),
     'L0_gnn_ln_b': (0.0, 0.1),
     'L0_gnn_le_b2': (0.0, 0.1),
     'L0_gnn_b1': (0.0, 0.1),
     'L0_gnn_b2': (0.0, 0.1),
     'L0_ffn_b_fx': (0.0, 0.1),
     'L0_ffn_b_x': (0.0, 0.8),
     'L0_ffn_b_slice': (0.0, 2.0),
     'L0_ffn_b_out': (0.0, 0.1),
     'L0_ffn_temperature': (0.5, 0.6)}
    factors = {'L0_gnn_emb': 8.0,
     'L0_gnn_al1': 4.371,
     'L0_gnn_ar1': 8.0,
     'L0_gnn_al2': 8.0,
     'L0_gnn_ar2': 64.0,
     'L0_ffn_W_x': 8.0,
     'L0_ffn_W_slice': 8.0,
     'L0_ffn_W_q': 8.0,
     'L0_ffn_W_k': 8.0}
    for name, (base, spread) in spreads.items():
        noise = np.random.default_rng([zlib.crc32(name.encode()), seed]).standard_normal(out[name].shape)
        drawn = base * np.exp(spread * noise) if base else spread * noise
        out[name] = jnp.asarray(drawn.astype(out[name].dtype))
    for name, factor in factors.items():
        out[name] = (out[name] * factor).astype(out[name].dtype)
    return out
```

```python
from contextlib import ExitStack

import concourse.bass as bass
from concourse import mybir

ALU = mybir.AluOpType
ACT = mybir.ActivationFunctionType
AX = mybir.AxisListType
F32 = mybir.dt.float32
BF16 = mybir.dt.bfloat16
I32 = mybir.dt.int32
DVE_ONLY = (mybir.EngineType.DVE,)
ACT_ONLY = (mybir.EngineType.Activation,)

P = 128
N, E, D = 6250, 106250, 256
HEADS, HID = 4, 64
CLASSES = 24
FF = 1024
NT = -(-N // P)
TAIL = N - (NT - 1) * P
TPB = 32
ET = 832
EP = ET * P
NB = ET // TPB
PAIRS = NB // 2
EPP = EP // P
ROW = D + 2 * HEADS
NW = NT * P + P
BIG = 1e30
LN_EPS = 1e-5
SLOPE = 0.2
RING = 4
SH, SD, SG = 8, 64, 64
INNER = SH * SD
RESERVED = 2 * TPB


class Core:

    def __init__(self, nc, ctx, dram):
        self.nc, self.ctx, self.d = nc, ctx, dram

    def sem(self, name):
        return self.ctx.enter_context(self.nc.semaphore(name))

    def sb(self, name, shape, dt=F32):
        return self.ctx.enter_context(self.nc.sbuf_tensor(name, shape, dt))


def sems(nc, ctx, *names):
    return [ctx.enter_context(nc.semaphore(n)) for n in names]


def over_tiles(eng, body):
    body(0, 0)
    with eng.Fori(0, (NT - 1) // 2) as k:
        body(2 * k + 1, 1)
        body(2 * k + 2, 0)


def bcast_rows(ap, parts, n):
    return bass.AP(ap.tensor, ap.offset, [[0, parts], [1, n]])


def constants_and_weights(c):
    nc, d = c.nc, c.d
    with ExitStack() as ctx:
        def sb(name, shape, dt=F32):
            return ctx.enter_context(nc.sbuf_tensor(name, shape, dt))

        emb3 = sb("emb3", [P, 2, 3, 32])
        w1b = sb("w1b", [P, 2, FF])
        b1_bc = sb("b1_bc", [96, FF])
        table = sb("table", [96, FF])
        rest = sb("rest", [96, FF])
        parts = sb("parts", [96, 3, FF], BF16)
        gw = [sb(f"gw{i}", [P, 2, D]) for i in range(2)]
        attn = [sb(f"attn{i}", [P, 2, 2 * HEADS]) for i in range(2)]
        gext1 = sb("gext1", [P, 2, ROW])
        le2 = sb("le2", [P, 2, FF])
        le2_b = sb("le2_b", [P, 2])
        le2_bw = sb("le2_bw", [P, 2, P])
        wxT = sb("wxT", [SD, SH, D])
        wsl = sb("wsl", [SD, SG])
        bx = sb("bx", [SD, SH])
        bx_w = sb("bx_w", [SD, SH, P])
        bsl = sb("bsl", [P, SG])
        temp = sb("temp", [P, SH])
        src_i = sb("src_i", [P, 7, P], I32)
        dst_i = sb("dst_i", [P, 7, P], I32)
        src_f = sb("src_f", [P, 7, P])
        dst_f = sb("dst_f", [P, 7, P])
        rel_f = sb("rel_f", [P, 7, P])
        base_f = sb("base_f", [1, ET])
        ends = sb("ends", [HEADS, 3, ET], I32)
        same = sb("same", [HEADS, 3, ET])
        one_row = sb("one_row", [1, P])
        iota_i = sb("iota_i", [P, P], I32)
        nid_i = sb("nid_i", [P, NT + 1], I32)
        seq = sb("seq", [P, EPP + 1], I32)
        zeros = sb("zeros", [P, 2048])
        pm = [ctx.enter_context(nc.psum_tensor(f"pm{i}", [P, 512], F32)) for i in range(8)]

        (loaded, weights_in, attn_in, pool_done, v_step, p_step, a_step, zeroed) = sems(
            nc, ctx, "loaded", "weights_in", "attn_in", "pool_done", "v_step", "p_step", "a_step", "zeroed")
        n_loaded = [0]

        PE = ["table", "attn1", "attn2", "fused0", "fused1", "fused2", "fused3", "fused4", "fused5", "fused6",
              "fused7", "bias1", "slices0", "slices1", "slice_bias", "base"] + [f"idx{g}" for g in range(7)]
        pe_at = {n: i + 1 for i, n in enumerate(PE)}

        with nc.Block() as block:
            @block.sync
            def _(sp):
                def load(dst, src):
                    sp.dma_start(dst, src).then_inc(loaded, 16)
                    n_loaded[0] += 16

                with nc.allow_non_contiguous_dma(reason="short vectors"):
                    for k in range(2):
                        load(w1b[:, k, :], d["le_W1T"][D + k * P:D + (k + 1) * P, :])
                        load(le2[:, k, :], d["le_W2"][k * P:(k + 1) * P, :])
                        load(c.w1a[:, k, :], d["le_W1T"][k * P:(k + 1) * P, :])
                        for i in range(2):
                            load(gw[i][:, k, :], d[f"W{i + 1}"][k * P:(k + 1) * P, :])
                            load((gext1, c.gext2)[i][:, k, 0:D], d[f"W{i + 1}T"][k * P:(k + 1) * P, :])
                    load(b1_bc[:], bcast_rows(d["le_b1"], 96, FF))
                    load(le2_b[:], d["le_b2"].rearrange("(k p) -> p k", p=P))
                    load(c.ln_g[:], d["ln_g"].rearrange("(k p) -> p k", p=P))
                    load(c.ln_b[:], d["ln_b"].rearrange("(k p) -> p k", p=P))
                    for i in range(2):
                        load(c.gat_b[:, i, :], d[f"b{i + 1}"].rearrange("(k p) -> p k", p=P))
                    load(wxT[:], d["W_xT"].rearrange("(h c) n -> c h n", c=SD))
                    load(wsl[:], d["W_slice"])
                    load(bx[:], d["b_x"].rearrange("(h c) -> c h", c=SD))
                    load(bsl[:], bcast_rows(d["b_slice"], P, SG))
                    load(temp[:], bcast_rows(d["temperature"], P, SH))
                    load(c.b_out[:], bcast_rows(d["b_out"], P, D))
                    for g in range(7):
                        rows = min(P, ET - g * P)
                        load(src_i[0:rows, g, :], d["src"][g * P:g * P + rows, :])
                        load(dst_i[0:rows, g, :], d["dst"][g * P:g * P + rows, :])
                    dst_at = d["dst_seq"]
                    load(c.base[:], bass.AP(dst_at.tensor, dst_at.offset + 1, [[0, 1], [P, ET]]))
                    for i, at in enumerate((1, 0, P)):
                        load(ends[:, i, :], bass.AP(dst_at.tensor, dst_at.offset + at, [[0, HEADS], [P, ET]]))
                    load(seq[:], bass.AP(dst_at.tensor, dst_at.offset, [[EPP, P], [1, EPP + 1]]))
                    sp.wait_ge(pool_done, 2)
                    for i in range(2):
                        for h in range(HEADS):
                            for j, a in enumerate(("al", "ar")):
                                lo = HID * (h % 2)
                                sp.dma_start(attn[i][lo:lo + HID, h // 2, j * HEADS + h:j * HEADS + h + 1],
                                             d[f"{a}{i + 1}"][h, :].rearrange("(p o) -> p o", o=1)).then_inc(attn_in, 16)
                    for k in range(2):
                        for r in range(3):
                            sp.dma_start(emb3[:, k, r, 0:CLASSES], d["embT"][k * P:(k + 1) * P, :]).then_inc(attn_in, 16)
                sp.wait_ge(v_step, 1)
                flat = EP * HEADS // P
                for e in (d["er_start1"], d["er_start2"]):
                    v = e.rearrange("(p a) h -> p (a h)", p=P)
                    for o in range(0, flat, 2048):
                        w = min(2048, flat - o)
                        sp.dma_start(v[:, o:o + w], zeros[:, 0:w]).then_inc(zeroed, 16)
                sp.wait_ge(zeroed, 16 * 2 * -(-flat // 2048))

            @block.gpsimd
            def _(pool):
                nc.gpsimd.memset(emb3[:], 0.0).then_inc(pool_done, 1)
                nc.gpsimd.memset(attn[0][:], 0.0)
                nc.gpsimd.memset(attn[1][:], 0.0).then_inc(pool_done, 1)
                nc.gpsimd.memset(c.ident[:], 0.0).then_inc(pool_done, 1)
                pool.wait_ge(pool_done, 3)
                nc.gpsimd.affine_select(out=c.ident[:], in_=c.ident[:], compare_op=ALU.not_equal, fill=1.0, base=0,
                                        pattern=[[-1, P]], channel_multiplier=1).then_inc(pool_done, 1)
                nc.gpsimd.iota(iota_i[:], [[1, P]], base=0, channel_multiplier=0).then_inc(pool_done, 1)
                nc.gpsimd.iota(nid_i[:], [[P, NT + 1]], base=0, channel_multiplier=1).then_inc(pool_done, 1)

            @block.vector
            def _(dve):
                n = [0]

                def link(ins):
                    n[0] += 1
                    ins.then_inc(v_step, 1)
                    dve.wait_ge(v_step, n[0])

                V = nc.vector
                link(V.memset(zeros[:], 0.0))
                V.memset(c.eps[:], LN_EPS)
                V.memset(one_row[:], 1.0).then_inc(v_step, 1)
                n[0] += 1
                dve.wait_ge(pool_done, 6)
                link(V.tensor_copy(c.iota[:], iota_i[:]))
                link(V.tensor_copy(c.nid[:], nid_i[:, 0:NT]))
                link(V.tensor_copy(c.klass[:, 0:1], nid_i[:, 0:1]))
                for r in range(1, 3):
                    link(V.tensor_scalar(c.klass[32 * r:32 * r + 32, :], c.klass[32 * r:32 * r + 32, :], -32.0 * r,
                                         None, ALU.add))
                link(V.tensor_reduce(c.is_head[:], c.ident[:].rearrange("p (t h) -> p h t", h=HEADS), AX.X, ALU.add))
                link(V.tensor_reduce(c.is_tile[:], c.ident[:].rearrange("p (t h) -> p t h", h=HEADS), AX.X, ALU.add))
                link(V.memset(c.to_rows[:], 0.0))
                link(V.tensor_copy(c.to_rows[:, 0:2, :].rearrange("p a (b f) -> p (a b) f", b=2),
                                   c.is_head[:].unsqueeze(2).broadcast_to([P, HEADS, HID])))
                link(V.tensor_copy(c.to_rows[:, 2, 0:HEADS], c.is_head[:]))
                link(V.tensor_copy(c.head_rows[:].rearrange("p (h f) -> p h f", h=HEADS),
                                   c.ident[0:HEADS, 0:HEADS].unsqueeze(2).broadcast_to([HEADS, HEADS, HID])))
                link(V.tensor_copy(c.head_parts[:].rearrange("p (t h) -> p t h", h=HEADS),
                                   c.ident[0:HEADS, 0:HEADS].unsqueeze(1).broadcast_to([HEADS, TPB, HEADS])))
                assert n[0] == 14
                dve.wait_ge(loaded, n_loaded[0])
                link(V.tensor_copy(base_f[:], c.base[:]))
                for g in range(7):
                    rows = min(P, ET - g * P)
                    link(V.tensor_copy(src_f[0:rows, g, :], src_i[0:rows, g, :]))
                    link(V.tensor_copy(dst_f[0:rows, g, :], dst_i[0:rows, g, :]))
                    link(V.tensor_scalar(rel_f[0:rows, g, :], dst_f[0:rows, g, :], dst_f[0:rows, g, 0:1], None,
                                         ALU.subtract))
                assert n[0] == 36
                link(V.tensor_tensor(same[:, 0, :], ends[:, 0, :], ends[:, 1, :], ALU.is_equal))
                link(V.tensor_tensor(same[:, 1, :], ends[:, 0, :], ends[:, 2, :], ALU.is_equal))
                link(V.tensor_tensor(same[:, 2, :], same[:, 0, :], same[:, 1, :], ALU.mult))
                link(V.tensor_scalar(c.go_on[:], same[:, 0, :], -1.0, BIG, ALU.add, ALU.mult))
                link(V.tensor_scalar(c.pass_on[:], same[:, 2, :], -1.0, BIG, ALU.add, ALU.mult))
                link(V.tensor_tensor(c.not_start[:], seq[:, 1:EPP + 1], seq[:, 0:EPP], ALU.is_equal))
                link(V.tensor_copy(le2_bw[:], le2_b[:].unsqueeze(2).broadcast_to([P, 2, P])))
                link(V.tensor_copy(bx_w[:], bx[:].unsqueeze(2).broadcast_to([SD, SH, P])))
                link(V.tensor_scalar(temp[:], temp[:], 0.1, 5.0, ALU.max, ALU.min))
                link(V.reciprocal(c.inv_temp[:], temp[:]))
                dve.wait_ge(p_step, pe_at["table"])
                for h in range(2):
                    link(V.tensor_tensor(table[:, h * 512:(h + 1) * 512], pm[h][0:96, :],
                                         b1_bc[:, h * 512:(h + 1) * 512], ALU.add))
                link(V.tensor_copy(parts[:, 0, :], table[:]))
                link(V.tensor_tensor(rest[:], table[:], parts[:, 0, :], ALU.subtract))
                link(V.tensor_copy(parts[:, 1, :], rest[:]))
                link(V.tensor_tensor(table[:], rest[:], parts[:, 1, :], ALU.subtract))
                link(V.tensor_copy(parts[:, 2, :], table[:]))
                for r in range(3):
                    link(V.tensor_copy(c.label_rows[32 * r:32 * r + 32, :], parts[32 * r:32 * r + 32, r, :]))
                assert n[0] == 56
                for i, g in enumerate((gext1, c.gext2)):
                    dve.wait_ge(p_step, pe_at[f"attn{i + 1}"])
                    link(V.tensor_copy(g[:, :, D:ROW],
                                       pm[2 + i][:, 0:16].rearrange("p (k a) -> p k a", k=2)))
                for k in range(8):
                    dve.wait_ge(p_step, pe_at[f"fused{k}"])
                    link(V.tensor_copy(c.fused[:, k, :], pm[4 + k % 2][:, 0:ROW]))
                dve.wait_ge(p_step, pe_at["bias1"])
                link(V.tensor_copy(c.bias1[:], pm[6][:, 0:ROW]))
                inv = c.inv_temp[:].unsqueeze(2).broadcast_to([P, SH, SG])
                for k in range(2):
                    dve.wait_ge(p_step, pe_at[f"slices{k}"])
                    link(V.tensor_tensor(c.wc[:, k, :].rearrange("p (h g) -> p h g", h=SH),
                                         pm[k][:].rearrange("p (h g) -> p h g", h=SH), inv, ALU.mult))
                dve.wait_ge(p_step, pe_at["slice_bias"])
                cb = c.wc_bias[:].rearrange("p (h g) -> p h g", h=SH)
                link(V.tensor_tensor(cb, pm[7][:].rearrange("p (h g) -> p h g", h=SH),
                                     bsl[:].unsqueeze(1).broadcast_to([P, SH, SG]), ALU.add))
                link(V.tensor_tensor(cb, cb, inv, ALU.mult))
                dve.wait_ge(p_step, pe_at["base"])
                link(V.tensor_copy(c.base_bc[:, 0:512], pm[2][:]))
                link(V.tensor_copy(c.base_bc[:, 512:ET], pm[3][:, 0:ET - 512]))
                for g in range(7):
                    rows = min(P, ET - g * P)
                    dve.wait_ge(p_step, pe_at[f"idx{g}"])
                    q = pm[4 + g % 2]
                    link(V.tensor_copy(c.idx[:, g * P:g * P + rows], q[:, 0:rows]))
                    link(V.tensor_copy(c.rel[:, g * P:g * P + rows], q[:, 256:256 + rows]))

            @block.tensor
            def _(pe):
                M, T = nc.tensor.matmul, nc.tensor.transpose

                def done(ins):
                    ins.then_inc(p_step, 1)

                pe.wait_ge(attn_in, 16 * (16 + 6))
                pe.wait_ge(loaded, n_loaded[0])
                for h in range(2):
                    for k in range(2):
                        m = M(pm[h][0:96, :], emb3[:, k].rearrange("p r q -> p (r q)"), w1b[:, k, h * 512:(h + 1) * 512],
                              start=k == 0, stop=k == 1)
                done(m)
                for i in range(2):
                    for k in range(2):
                        for o in range(2):
                            m = M(pm[2 + i][:, 8 * k:8 * k + 8], gw[i][:, o, k * P:(k + 1) * P], attn[i][:, o, :],
                                  start=o == 0, stop=o == 1)
                    done(m)
                pe.wait_ge(v_step, 57)
                for k in range(8):
                    if k >= 2:
                        pe.wait_ge(v_step, 59 + k - 2)
                    for cc in range(2):
                        m = M(pm[4 + k % 2][:, 0:ROW], le2[:, cc, k * P:(k + 1) * P], gext1[:, cc, :],
                              start=cc == 0, stop=cc == 1)
                    done(m)
                for cc in range(2):
                    m = M(pm[6][:, 0:ROW], le2_bw[:, cc, :], gext1[:, cc, :], start=cc == 0, stop=cc == 1)
                done(m)
                for k in range(2):
                    for h in range(SH):
                        m = M(pm[k][:, h * SG:(h + 1) * SG], wxT[:, h, k * P:(k + 1) * P], wsl[:], start=True, stop=True)
                    done(m)
                for h in range(SH):
                    m = M(pm[7][:, h * SG:(h + 1) * SG], bx_w[:, h, :], wsl[:], start=True, stop=True)
                done(m)
                M(pm[2][:], one_row[:], base_f[0:1, 0:512], start=True, stop=True)
                m = M(pm[3][:, 0:ET - 512], one_row[:], base_f[0:1, 512:ET], start=True, stop=True)
                done(m)
                for g in range(7):
                    rows = min(P, ET - g * P)
                    pe.wait_ge(v_step, 73 if g < 2 else 75 + 2 * (g - 2))
                    q = pm[4 + g % 2]
                    T(q[:, 0:rows], src_f[0:rows, g, :], c.ident[0:rows, 0:rows])
                    m = T(q[:, 256:256 + rows], rel_f[0:rows, g, :], c.ident[0:rows, 0:rows])
                    done(m)


def encode(c):
    nc, d = c.nc, c.d
    with ExitStack() as ctx:
        def sb(name, shape, dt=F32):
            return ctx.enter_context(nc.sbuf_tensor(name, shape, dt))

        x = [sb(f"x{i}", [P, D]) for i in range(2)]
        lab = [sb(f"lab{i}", [96, P], I32) for i in range(2)]
        hot = [sb(f"hot{i}", [96, P], BF16) for i in range(2)]
        xn = [sb(f"xn{i}", [P, D]) for i in range(2)]
        xnT = [sb(f"xnT{i}", [P, D]) for i in range(2)]
        zn = [sb(f"zn{i}", [P, FF]) for i in range(2)]
        yT = [sb(f"yT{i}", [P, FF]) for i in range(2)]
        fe = [sb(f"fe{i}", [P, ROW]) for i in range(2)]
        st = [sb(f"st{i}", [P, 32]) for i in range(2)]
        junk = sb("junk", [P, ET])
        tile_f = [sb(f"tile_f{i}", [P, 1]) for i in range(2)]
        tile_i = [sb(f"tile_i{i}", [P, 1], I32) for i in range(2)]
        rows = [sb(f"rows{i}", [P, P], I32) for i in range(2)]
        cnt = [sb(f"cnt{i}", [P, 1]) for i in range(2)]
        start_f = [sb(f"start_f{i}", [P, 1]) for i in range(2)]
        start_i = [sb(f"start_i{i}", [P, 1], I32) for i in range(2)]
        p_xT = ctx.enter_context(nc.psum_tensor("p_xT", [P, 512], F32))
        p_z = [ctx.enter_context(nc.psum_tensor(f"p_z{i}", [P, 2, 512], F32)) for i in range(2)]
        p_zT = ctx.enter_context(nc.psum_tensor("p_zT", [P, 2, 512], F32))
        p_fe = ctx.enter_context(nc.psum_tensor("p_fe", [P, 512], F32))

        in_ = sems(nc, ctx, "x_in0", "x_in1")
        stored = sems(nc, ctx, "fe_stored0", "fe_stored1")
        scattered = sems(nc, ctx, "er_scattered0", "er_scattered1")
        found = sems(nc, ctx, "rows_in0", "rows_in1")
        (chain, xn_ready, hot_ready, z_half, xT_done, xT_ready, z_done, var_x, std_x, var_z, std_z, scale_z, zn_ready,
         zT_done, yT_ready, fe_done, fe_ready, tile_ready, start_ready) = sems(
            nc, ctx, "chain", "xn_ready", "hot_ready", "z_half", "xT_done", "xT_ready", "z_done", "var_x", "std_x",
            "var_z", "std_z", "scale_z", "zn_ready", "zT_done", "yT_ready", "fe_done", "fe_ready", "tile_ready",
            "start_ready")
        free_x, counted = sems(nc, ctx, "free_x", "counted")

        with nc.Block() as block:
            @block.sync
            def _(sp):
                def store(j, q):
                    sp.wait_ge(fe_ready, j + 1)
                    sp.dma_start(d["table1"][bass.ds(j * P, P), :], fe[q][:]).then_inc(stored[q], 16)

                def load(j, q, n=P):
                    sp.wait_ge(free_x, j + 1)
                    sp.dma_start(x[q][0:n, :], d["x"][bass.ds(j * P, n), :]).then_inc(in_[q], 16)
                    at = d["labels"]
                    sp.dma_start(lab[q][:], at[bass.ds(j * P, P)].unsqueeze(0).broadcast_to([96, P])).then_inc(in_[q], 16)

                sp.sem_inc(free_x, 2)
                load(0, 0)
                load(1, 1)
                with sp.Fori(0, (NT - 3) // 2) as k:
                    load(2 * k + 2, 0)
                    store(2 * k, 0)
                    load(2 * k + 3, 1)
                    store(2 * k + 1, 1)
                load(NT - 1, 0, TAIL)
                for j in range(NT - 3, NT):
                    store(j, j % 2)
                for q in range(2):
                    sp.wait_ge(stored[q], 16 * len(range(q, NT, 2)))

            @block.gpsimd
            def _(pool):
                def fetch(j, q):
                    pool.wait_ge(tile_ready, j + 1)
                    pool.nop(nofuse=True)
                    nc.gpsimd.indirect_dma_start(
                        out=rows[q][:], out_offset=None, in_=d["dst"],
                        in_offset=bass.IndirectOffsetOnAxis(ap=tile_i[q][:], axis=0)).then_inc(found[q], 16)

                def scatter(j, q, n=P):
                    pool.wait_ge(fe_ready, j + 1)
                    pool.wait_ge(start_ready, j + 1)
                    pool.nop(nofuse=True)
                    nc.gpsimd.indirect_dma_start(
                        out=d["er_start1"], out_offset=bass.IndirectOffsetOnAxis(ap=start_i[q][0:n, :], axis=0),
                        in_=fe[q][0:n, D + HEADS:ROW], in_offset=None).then_inc(scattered[q], 16)

                fetch(0, 0)
                with pool.Fori(0, (NT - 1) // 2) as k:
                    fetch(2 * k + 1, 1)
                    scatter(2 * k, 0)
                    fetch(2 * k + 2, 0)
                    scatter(2 * k + 1, 1)
                scatter(NT - 1, 0, TAIL)
                for q in range(2):
                    pool.wait_ge(scattered[q], 16 * len(range(q, NT, 2)))

            @block.vector
            def _(dve):
                V = nc.vector

                def norm_x(j, q):
                    dve.wait_ge(in_[q], 16 * (2 * (j // 2) + 2) if isinstance(j, int) else (j + 2 - q) * 16)
                    s = st[q]
                    V.bn_stats(s[:, 0:6], x[q][:]).then_inc(chain, 1)
                    V.tensor_scalar(hot[q][:], lab[q][:], c.klass[0:96, :], None, ALU.is_equal).then_inc(hot_ready, 1)
                    dve.wait_ge(chain, 4 * j + 1)
                    dve.nop(nofuse=True)
                    V.bn_aggr(s[:, 6:8], s[:, 0:6]).then_inc(var_x, 1)
                    V.tensor_scalar(junk[:], c.base_bc[:], c.nid[:, bass.ds(j, 1)], 0.0, ALU.is_lt, ALU.add,
                                    accum_out=tile_f[q][:]).then_inc(chain, 1)
                    dve.wait_ge(chain, 4 * j + 2)
                    V.tensor_scalar(tile_f[q][:], tile_f[q][:], -1.0, 0.0, ALU.add, ALU.max).then_inc(chain, 1)
                    dve.wait_ge(chain, 4 * j + 3)
                    V.tensor_copy(tile_i[q][:], tile_f[q][:]).then_inc(tile_ready, 1)
                    dve.wait_ge(std_x, j + 1)
                    V.reciprocal(s[:, 9:10], s[:, 8:9]).then_inc(chain, 1)
                    dve.wait_ge(chain, 4 * j + 4)
                    V.tensor_scalar(xn[q][:], x[q][:], s[:, 6:7], s[:, 9:10], ALU.subtract,
                                    ALU.mult).then_inc(xn_ready, 1)
                    dve.wait_ge(xn_ready, j + 1)
                    dve.sem_inc(free_x, 1)

                def norm_z(j, q):
                    s = st[q]
                    dve.wait_ge(z_done, j + 1)
                    V.bn_stats(s[:, 10:16], p_z[q][:, 0, :])
                    V.bn_stats(s[:, 16:22], p_z[q][:, 1, :]).then_inc(z_half, 1)
                    dve.wait_ge(z_half, 2 * j + 1)
                    dve.nop(nofuse=True)
                    V.bn_aggr(s[:, 22:24], s[:, 10:22]).then_inc(var_z, 1)
                    dve.wait_ge(std_z, j + 1)
                    V.reciprocal(s[:, 25:26], s[:, 24:25]).then_inc(z_half, 1)
                    dve.wait_ge(z_half, 2 * j + 2)
                    V.scalar_tensor_tensor(out=s[:, 26:27], in0=s[:, 22:23], scalar=-1.0, in1=s[:, 25:26],
                                           op0=ALU.mult, op1=ALU.mult).then_inc(scale_z, 1)
                    dve.wait_ge(scale_z, j + 1)
                    V.tensor_scalar(zn[q][:, 0:512], p_z[q][:, 0, :], s[:, 25:26], s[:, 26:27], ALU.mult,
                                    ALU.add).then_inc(zn_ready, 1)

                def edge_start(j, q):
                    if not (isinstance(j, int) and j < 2):
                        dve.wait_ge(scattered[q], (j - q) * 8)
                    dve.wait_ge(found[q], 16 * (j // 2 + 1) if isinstance(j, int) else (j + 2 - q) * 8)
                    V.tensor_scalar(junk[:, 0:P], rows[q][:], c.nid[:, bass.ds(j, 1)], 0.0, ALU.is_lt, ALU.add,
                                    accum_out=cnt[q][:]).then_inc(counted, 1)
                    dve.wait_ge(counted, 2 * j + 1)
                    V.scalar_tensor_tensor(out=start_f[q][:], in0=tile_f[q][:], scalar=float(P), in1=cnt[q][:],
                                           op0=ALU.mult, op1=ALU.add).then_inc(counted, 1)
                    dve.wait_ge(counted, 2 * j + 2)
                    V.tensor_copy(start_i[q][:], start_f[q][:]).then_inc(start_ready, 1)
                    V.tensor_copy(c.start[:, bass.ds(j, 1)], start_f[q][:])

                def features(j, q):
                    if not (isinstance(j, int) and j < 2):
                        dve.wait_ge(stored[q], (j - q) * 8)
                        dve.wait_ge(scattered[q], (j - q) * 8)
                    dve.wait_ge(fe_done, j + 1)
                    V.tensor_tensor(fe[q][:], p_fe[:, 0:ROW], c.bias1[:], ALU.add).then_inc(fe_ready, 1)

                def tile(j, q, ahead=True, behind=True):
                    norm_z(j, q)
                    if ahead:
                        norm_x(j + 1, 1 - q)
                    edge_start(j, q)
                    if behind:
                        features(j - 1, 1 - q)

                norm_x(0, 0)
                tile(0, 0, behind=False)
                tile(1, 1)
                tile(2, 0)
                with dve.Fori(1, (NT - 3) // 2) as k:
                    tile(2 * k + 1, 1)
                    tile(2 * k + 2, 0)
                tile(NT - 2, 1)
                tile(NT - 1, 0, ahead=False)
                features(NT - 1, 0)

            @block.scalar
            def _(act):
                A = nc.scalar.activation

                def head(j, q):
                    s = st[q]
                    act.wait_ge(var_x, j + 1)
                    A(s[:, 8:9], s[:, 7:8], ACT.Sqrt, bias=c.eps[:]).then_inc(std_x, 1)
                    act.wait_ge(xT_done, j + 1)
                    A(xnT[q][:], p_xT[:, 0:D], ACT.Copy).then_inc(xT_ready, 1)

                def mid(j, q):
                    s = st[q]
                    act.wait_ge(var_z, j + 1)
                    A(s[:, 24:25], s[:, 23:24], ACT.Sqrt, bias=c.eps[:]).then_inc(std_z, 1)
                    act.wait_ge(scale_z, j + 1)
                    A(zn[q][:, 512:1024], p_z[q][:, 1, :], ACT.Identity, bias=s[:, 26:27],
                      scale=s[:, 25:26]).then_inc(zn_ready, 1)

                def tail(j, q):
                    for h in range(2):
                        act.wait_ge(zT_done, 2 * j + h + 1)
                        for i in range(4):
                            k = 4 * h + i
                            a = A(yT[q][:, k * P:(k + 1) * P], p_zT[:, h, i * P:(i + 1) * P], ACT.Relu,
                                  bias=c.ln_b[:, k:k + 1], scale=c.ln_g[:, k:k + 1])
                        a.then_inc(yT_ready, 1)

                def tile(j, q, ahead=True):
                    mid(j, q)
                    if ahead:
                        head(j + 1, 1 - q)
                    tail(j, q)

                head(0, 0)
                with act.Fori(0, (NT - 1) // 2) as k:
                    tile(2 * k, 0)
                    tile(2 * k + 1, 1)
                tile(NT - 1, 0, ahead=False)

            @block.tensor
            def _(pe):
                M, T = nc.tensor.matmul, nc.tensor.transpose

                def xT(j, q):
                    pe.wait_ge(xn_ready, j + 1)
                    for k in range(2):
                        t = T(p_xT[:, k * P:(k + 1) * P], xn[q][:, k * P:(k + 1) * P], c.ident[:])
                    t.then_inc(xT_done, 1)

                def z(j, q):
                    pe.wait_ge(xT_ready, j + 1)
                    pe.wait_ge(hot_ready, j + 1)
                    for h in range(2):
                        cols = slice(h * 512, (h + 1) * 512)
                        for k in range(2):
                            M(p_z[q][:, h, :], xnT[q][:, k * P:(k + 1) * P], c.w1a[:, k, cols], start=k == 0, stop=False)
                        m = M(p_z[q][:, h, :], hot[q][:], c.label_rows[:, cols], start=False, stop=True)
                    m.then_inc(z_done, 1)

                def zT(j, q):
                    pe.wait_ge(zn_ready, 2 * j + 2)
                    for h in range(2):
                        for i in range(4):
                            k = 4 * h + i
                            t = T(p_zT[:, h, i * P:(i + 1) * P], zn[q][:, k * P:(k + 1) * P], c.ident[:])
                        t.then_inc(zT_done, 1)

                def fe_mm(j, q):
                    pe.wait_ge(yT_ready, 2 * j + 2)
                    if not (isinstance(j, int) and j == 0):
                        pe.wait_ge(fe_ready, j)
                    for k in range(8):
                        m = M(p_fe[:, 0:ROW], yT[q][:, k * P:(k + 1) * P], c.fused[:, k, :], start=k == 0, stop=k == 7)
                    m.then_inc(fe_done, 1)

                xT(0, 0)
                z(0, 0)
                with pe.Fori(0, (NT - 1) // 2) as k:
                    xT(2 * k + 1, 1)
                    zT(2 * k, 0)
                    z(2 * k + 1, 1)
                    fe_mm(2 * k, 0)
                    xT(2 * k + 2, 0)
                    zT(2 * k + 1, 1)
                    z(2 * k + 2, 0)
                    fe_mm(2 * k + 1, 1)
                zT(NT - 1, 0)
                fe_mm(NT - 1, 0)


def spread_er(c, layer):
    nc, d = c.nc, c.d
    with ExitStack() as ctx:
        def sb(name, shape, dt=F32):
            return ctx.enter_context(nc.sbuf_tensor(f"{name}_{layer}", shape, dt))

        er = sb("er", [P, EPP, HEADS])
        spread = sb("spread", [P, HEADS, EPP])
        first_id = sb("first_id", [P, 1], I32)
        first_row = sb("first_row", [P, ROW])
        er_in, id_in, row_in, scanned, out_done, acc_zero = sems(
            nc, ctx, *(f"{n}_{layer}" for n in ("er_in", "id_in", "row_in", "scanned", "out_done", "acc_zero")))
        with nc.Block() as block:
            @block.sync
            def _(sp):
                at = d["dst_seq"]
                with nc.allow_non_contiguous_dma(reason="one id per partition"):
                    sp.dma_start(first_id[:], bass.AP(at.tensor, at.offset + 1, [[EPP, P], [1, 1]])).then_inc(id_in, 16)
                sp.dma_start(er[:], d[f"er_start{layer}"].rearrange("(p a) h -> p a h", p=P)).then_inc(er_in, 16)
                for h in range(HEADS):
                    sp.wait_ge(scanned, h + 1)
                    sp.dma_start(d[f"er_edge{layer}"][h].rearrange("(p a) -> p a", p=P), spread[:, h, :]).then_inc(out_done, 16)
                sp.wait_ge(out_done, 16 * HEADS)

            @block.gpsimd
            def _(pool):
                pool.wait_ge(id_in, 16)
                nc.gpsimd.indirect_dma_start(
                    out=first_row[:], out_offset=None, in_=d[f"table{layer}"],
                    in_offset=bass.IndirectOffsetOnAxis(ap=first_id[:], axis=0)).then_inc(row_in, 16)

            @block.vector
            def _(dve):
                if layer == 1:
                    nc.vector.memset(c.acc[:], 0.0).then_inc(acc_zero, 1)
                    dve.wait_ge(acc_zero, 1)
                dve.wait_ge(er_in, 16)
                dve.wait_ge(row_in, 16)
                for h in range(HEADS):
                    nc.vector.tensor_tensor_scan(spread[:, h, :], c.not_start[:], er[:, :, h],
                                                 first_row[:, D + HEADS + h:D + HEADS + h + 1],
                                                 ALU.mult, ALU.add).then_inc(scanned, 1)


def edges(c, layer):
    nc, d = c.nc, c.d
    with ExitStack() as ctx:
        def sb(name, shape, dt=F32):
            return ctx.enter_context(nc.sbuf_tensor(f"{name}_{layer}", shape, dt))

        def two(name, shape, dt=F32):
            return [sb(f"{name}{i}", shape, dt) for i in range(2)]

        rows = two("rows", [P, TPB, ROW])
        scaled = sb("scaled", [P, RING, D])
        window = sb("window", [P, RING, P])
        idx_now = two("idx_now", [P, TPB], I32)
        er = two("er", [P, P])
        el = sb("el", [P, P])
        dst_i = two("dst_i", [P, P + 2], I32)
        cut = sb("cut", [P, P + 1])
        fst = sb("fst", [P, P])
        e0 = sb("e0", [P, P])
        e = sb("e", [P, P])
        run_max = sb("run_max", [P, P])
        node_max = sb("node_max", [P, P])
        full_max = sb("full_max", [P, P])
        down = sb("down", [P, P])
        prob = sb("prob", [P, P])
        last_max = sb("last_max", [P, TPB])
        carried = sb("carried", [HEADS, NB * TPB + 1])
        brought = sb("brought", [HEADS, TPB])
        spread_junk = sb("spread_junk", [P, TPB])
        carry = sb("carry", [P, 1])
        fade = sb("fade", [P, 1])
        fade_t = sb("fade_t", [P, TPB])
        wt = two("wt", [P, P])
        fades = two("fades", [P, 3, TPB])
        kept = sb("kept", [P, 2, 3])
        p_part = [ctx.enter_context(nc.psum_tensor(f"p_part{i}_{layer}", [P, 512], F32)) for i in range(RING)]
        p_e = ctx.enter_context(nc.psum_tensor(f"p_e_{layer}", [P, 512], F32))
        p_carry = ctx.enter_context(nc.psum_tensor(f"p_carry_{layer}", [P, 512], F32))
        p_w = ctx.enter_context(nc.psum_tensor(f"p_w_{layer}", [P, 512], F32))
        p_fade = ctx.enter_context(nc.psum_tensor(f"p_fade_{layer}", [P, 512], F32))

        names = ["idx_ready", "el_ready", "slot_free", "eT_done", "link", "last_ready", "last_done", "brought_ready",
                 "brought_done", "down_ready", "carry_ready", "exp_done", "fade_done", "fade_ready", "w_done",
                 "fadeT_done", "w_ready", "scaled_ready", "mm_done", "kept_ready", "fixed", "copied", "psum_zero"]
        S = dict(zip(names, sems(nc, ctx, *(f"{n}_{layer}" for n in names))))
        gathered = sems(nc, ctx, *(f"gathered{i}_{layer}" for i in range(2)))
        loaded = sems(nc, ctx, *(f"batch_in{i}_{layer}" for i in range(2)))
        TWO = 2 * TPB

        with nc.Block() as block:
            @block.sync
            def _(sp):
                def load(b, q):
                    sp.wait_ge(S["down_ready"], b + 1)
                    ee, dd = d[f"er_edge{layer}"], d["dst_seq"]
                    sp.dma_start(er[q][:], ee.rearrange("h (b t e) -> b t h e", t=TPB, e=P)[bass.ds(b, 1)].rearrange(
                        "b t h e -> (b t) h e")).then_inc(loaded[q], 16)
                    sp.dma_start(dst_i[q][:], d["dst_over"][bass.ds(b * TPB, TPB), :].unsqueeze(1).broadcast_to(
                        [TPB, HEADS, P + 2])).then_inc(loaded[q], 16)

                sp.sem_inc(S["down_ready"], 2)
                with sp.Fori(0, PAIRS) as k:
                    load(2 * k, 0)
                    load(2 * k + 1, 1)

            @block.gpsimd
            def _(pool):
                with pool.Fori(0, PAIRS) as k:
                    for q in range(2):
                        b = 2 * k + q
                        pool.wait_ge(S["idx_ready"], b + 1)
                        for s in range(TPB):
                            if s % 4 == 0:
                                pool.wait_ge(S["scaled_ready"], b * TPB + s + 4)
                            pool.nop(nofuse=True)
                            nc.gpsimd.indirect_dma_start(
                                out=rows[q][:, s, :], out_offset=None, in_=d[f"table{layer}"],
                                in_offset=bass.IndirectOffsetOnAxis(ap=idx_now[q][:, s:s + 1], axis=0)
                            ).then_inc(gathered[q], 16)

            @block.vector
            def _(dve):
                V = nc.vector
                LINKS = 7

                def index(b, q):
                    V.tensor_copy(idx_now[q][:], c.idx[:, bass.ds(b * TPB, TPB)]).then_inc(S["idx_ready"], 1)

                def prep(b, q):
                    def links(k):
                        dve.wait_ge(S["link"], b * LINKS + k)

                    def logits():
                        dve.wait_ge(loaded[q], (b + 2 - q) * 16)
                        V.tensor_tensor(cut[:], dst_i[q][:, 1:P + 2], dst_i[q][:, 0:P + 1],
                                        ALU.not_equal).then_inc(S["link"], 1)
                        V.tensor_scalar(fst[:], dst_i[q][:, 1:P + 1], dst_i[q][:, 1:2], -BIG, ALU.not_equal, ALU.mult)
                        links(1)
                        V.tensor_scalar(cut[:], cut[:], -BIG, None, ALU.mult).then_inc(S["link"], 1)
                        dve.wait_ge(S["eT_done"], b + 1)
                        V.tensor_tensor(e0[:], p_e[:, 0:P], er[q][:], ALU.add).then_inc(S["link"], 1)
                        links(3)
                        V.scalar_tensor_tensor(out=e[:], in0=e0[:], scalar=SLOPE, in1=e0[:], op0=ALU.mult,
                                               op1=ALU.max).then_inc(S["link"], 1)
                        links(4)
                        V.tensor_tensor_scan(run_max[:], cut[:, 0:P], e[:], -BIG, ALU.add, ALU.max).then_inc(S["link"], 1)
                        links(5)
                        V.tensor_tensor_scan(node_max[:, ::-1], cut[:, :0:-1], run_max[:, ::-1], -BIG, ALU.add,
                                             ALU.max).then_inc(S["link"], 1)
                        links(6)
                        V.tensor_scalar(last_max[:], c.is_tile[:], node_max[:, P - 1:P], None,
                                        ALU.mult).then_inc(S["last_ready"], 1)

                    def carries():
                        dve.wait_ge(S["last_done"], b + 1)
                        V.tensor_tensor_scan(carried[:, bass.ds(b * TPB + 1, TPB)], c.pass_on[:, bass.ds(b * TPB, TPB)],
                                             p_carry[0:HEADS, 0:TPB], carried[:, bass.ds(b * TPB, 1)], ALU.add,
                                             ALU.max).then_inc(S["link"], 1)
                        links(7)
                        V.tensor_tensor(brought[:], carried[:, bass.ds(b * TPB, TPB)], c.go_on[:, bass.ds(b * TPB, TPB)],
                                        ALU.add).then_inc(S["brought_ready"], 1)

                    def shift():
                        dve.wait_ge(S["brought_done"], b + 1)
                        V.tensor_tensor_reduce(spread_junk[:], p_carry[:, 64:64 + TPB], c.is_tile[:], 1.0, 0.0,
                                               ALU.mult, ALU.add, carry[:]).then_inc(S["carry_ready"], 1)
                        dve.wait_ge(S["carry_ready"], 2 * b + 1)
                        V.scalar_tensor_tensor(out=full_max[:], in0=fst[:], scalar=carry[:], in1=node_max[:],
                                               op0=ALU.add, op1=ALU.max).then_inc(S["carry_ready"], 1)
                        dve.wait_ge(S["carry_ready"], 2 * b + 2)
                        V.tensor_tensor(down[:], e[:], full_max[:], ALU.subtract).then_inc(S["down_ready"], 1)

                    def fade_():
                        dve.wait_ge(S["fade_done"], b + 1)
                        V.tensor_scalar(fade_t[:], c.is_tile[:], fade[:], None, ALU.mult).then_inc(S["fade_ready"], 1)

                    return {4: logits, 8: carries, 12: shift, 16: fade_}

                def scale(i, b, q, s):
                    r = s % RING
                    dve.wait_ge(S["mm_done"], i + 1)
                    V.tensor_scalar(window[:, r, :], c.iota[:], c.rel[:, bass.ds(i, 1)], None, ALU.is_equal)
                    V.tensor_tensor(scaled[:, r, :].rearrange("p (h f) -> p h f", h=HEADS),
                                    rows[q][:, s, 0:D].rearrange("p (h f) -> p h f", h=HEADS),
                                    wt[q][:, HEADS * s:HEADS * s + HEADS].unsqueeze(2).broadcast_to([P, HEADS, HID]),
                                    ALU.mult).then_inc(S["scaled_ready"], 1)

                def fix(i, q, s, at):
                    col = c.acc[:, :, bass.ds(at, 1)]
                    k = kept[:, s % 2, :].unsqueeze(2)
                    dve.wait_ge(S["copied"], i + RING)
                    V.tensor_tensor(k, col, fades[q][:, :, s:s + 1], ALU.mult).then_inc(S["kept_ready"], 1)
                    dve.wait_ge(S["mm_done"], i + RING + 1)
                    dve.wait_ge(S["kept_ready"], i + 1)
                    part = p_part[s % RING][:, 0:3 * P].rearrange("p (a n) -> p a n", a=3)[:, :, 0:1]
                    V.tensor_tensor(col, k, part, ALU.add).then_inc(S["fixed"], 1)

                def batch(b, q, ahead, more=False):
                    steps = prep(b + 1, 1 - q) if ahead else {}
                    dve.wait_ge(S["w_ready"], 2 * b + 2)
                    if more:
                        dve.wait_ge(gathered[q], (b + 2 - q) * 8 * TPB)
                        index(b + 2, q)
                    scale(b * TPB, b, q, 0)
                    for s in range(TPB):
                        i = b * TPB + s
                        if s % 8 == 0:
                            at = nc.values_load_multi_w_load_instructions(
                                c.base[0:1, bass.ds(i, 8)], engines=DVE_ONLY, min_val=0, max_val=N,
                                skip_runtime_bounds_check_because="a node's number")[1]
                        if s + 1 < TPB:
                            scale(i + 1, b, q, s + 1)
                        fix(i, q, s, at[s % 8])
                        if s in steps:
                            steps[s]()

                V.memset(carried[:, 0:1], -BIG).then_inc(S["psum_zero"], 1)
                for r in range(RING):
                    V.memset(p_part[r][:], 0.0).then_inc(S["psum_zero"], 1)
                dve.wait_ge(S["psum_zero"], RING + 1)
                index(0, 0)
                index(1, 1)
                for _, step in sorted(prep(0, 0).items()):
                    step()
                with dve.Fori(0, PAIRS - 1) as k:
                    batch(2 * k, 0, True, more=True)
                    batch(2 * k + 1, 1, True, more=True)
                batch(NB - 2, 0, True)
                batch(NB - 1, 1, False)

            @block.scalar
            def _(act):
                A = nc.scalar.activation

                def prep(b, q):
                    def pick():
                        act.wait_ge(gathered[q], (b + 2 - q) * 8 * TPB)
                        A(el[:].rearrange("p (t h) -> p t h", h=HEADS), rows[q][:, :, D:D + HEADS],
                          ACT.Copy).then_inc(S["el_ready"], 1)

                    def probs():
                        act.wait_ge(S["down_ready"], b + 3)
                        A(prob[:], down[:], ACT.Exp).then_inc(S["exp_done"], 1)
                        A(fade[:], full_max[:, 0:1], ACT.Exp, bias=carry[:], scale=-1.0).then_inc(S["fade_done"], 1)

                    def copy_out():
                        act.wait_ge(S["w_done"], b + 1)
                        A(wt[q][:], p_w[:, 0:P], ACT.Copy).then_inc(S["w_ready"], 1)
                        act.wait_ge(S["fadeT_done"], b + 1)
                        A(fades[q][:].rearrange("p a t -> p (a t)"), p_fade[:, 0:3 * TPB],
                          ACT.Copy).then_inc(S["w_ready"], 1)
                    return {2: pick, 14: probs, 20: copy_out}

                def batch(b, q, ahead):
                    steps = prep(b + 1, 1 - q) if ahead else {}
                    for s in range(TPB):
                        i = b * TPB + s
                        if s % 8 == 0:
                            at = nc.values_load_multi_w_load_instructions(
                                c.base[0:1, bass.ds(i, 8)], engines=ACT_ONLY, min_val=0, max_val=N,
                                skip_runtime_bounds_check_because="a node's number")[1]
                        act.wait_ge(S["fixed"], i + 1)
                        A(c.acc[:, :, bass.ds(at[s % 8] + 1, P - 1)],
                          p_part[s % RING][:, 0:3 * P].rearrange("p (a n) -> p a n", a=3)[:, :, 1:P],
                          ACT.Copy).then_inc(S["copied"], 1)
                        if s in steps:
                            steps[s]()

                act.sem_inc(S["copied"], RING)
                for _, step in sorted(prep(0, 0).items()):
                    step()
                with act.Fori(0, PAIRS - 1) as k:
                    batch(2 * k, 0, True)
                    batch(2 * k + 1, 1, True)
                batch(NB - 2, 0, True)
                batch(NB - 1, 1, False)

            @block.tensor
            def _(pe):
                M, T = nc.tensor.matmul, nc.tensor.transpose

                def prep(b, q):
                    def eT():
                        pe.wait_ge(S["el_ready"], b + 1)
                        T(p_e[:, 0:P], el[:], c.ident[:]).then_inc(S["eT_done"], 1)

                    def last():
                        pe.wait_ge(S["last_ready"], b + 1)
                        M(p_carry[0:HEADS, 0:TPB], c.is_head[:], last_max[:], start=True,
                          stop=True).then_inc(S["last_done"], 1)

                    def bring():
                        pe.wait_ge(S["brought_ready"], b + 1)
                        M(p_carry[:, 64:64 + TPB], c.head_parts[:], brought[:], start=True,
                          stop=True).then_inc(S["brought_done"], 1)

                    def turn():
                        pe.wait_ge(S["exp_done"], b + 1)
                        T(p_w[:, 0:P], prob[:], c.ident[:]).then_inc(S["w_done"], 1)

                    def fades_():
                        pe.wait_ge(S["fade_ready"], b + 1)
                        for a in range(3):
                            m = M(p_fade[:, a * TPB:(a + 1) * TPB], c.to_rows[:, a, :], fade_t[:], start=True, stop=True)
                        m.then_inc(S["fadeT_done"], 1)
                    return {3: eT, 7: last, 11: bring, 15: turn, 18: fades_}

                def batch(b, q, ahead):
                    steps = prep(b + 1, 1 - q) if ahead else {}
                    for s in range(TPB):
                        i = b * TPB + s
                        r = s % RING
                        pe.wait_ge(S["scaled_ready"], i + RESERVED + 1)
                        pe.wait_ge(S["copied"], i + 1)
                        for a in range(2):
                            M(p_part[r][:, a * P:(a + 1) * P], scaled[:, r, a * P:(a + 1) * P], window[:, r, :],
                              start=True, stop=True)
                        M(p_part[r][0:HEADS, 2 * P:3 * P], wt[q][:, HEADS * s:HEADS * s + HEADS], window[:, r, :],
                          start=True, stop=True).then_inc(S["mm_done"], 1)
                        if s in steps:
                            steps[s]()

                pe.sem_inc(S["mm_done"], RING)
                pe.sem_inc(S["scaled_ready"], RESERVED)
                pe.wait_ge(S["psum_zero"], RING + 1)
                for _, step in sorted(prep(0, 0).items()):
                    step()
                with pe.Fori(0, PAIRS - 1) as k:
                    batch(2 * k, 0, True)
                    batch(2 * k + 1, 1, True)
                batch(NB - 2, 0, True)
                batch(NB - 1, 1, False)


def end_of_layer(c, ctx, tag, block_bias):
    nc = c.nc

    def sb(name, shape):
        return ctx.enter_context(nc.sbuf_tensor(f"{name}_{tag}", shape, F32))

    den = [sb(f"den{i}", [HEADS, P]) for i in range(2)]
    inv = [sb(f"inv{i}", [HEADS, P]) for i in range(2)]
    avg = [sb(f"avg{i}", [P, 2, P]) for i in range(2)]
    hT = [sb(f"hT{i}", [P, 2, P]) for i in range(2)]
    p_inv = [ctx.enter_context(nc.psum_tensor(f"p_inv{i}_{tag}", [P, 512], F32)) for i in range(2)]
    den_ready, inv_ready, inv_done, avg_ready, hT_ready = sems(
        nc, ctx, *(f"{n}_{tag}" for n in ("den_ready", "inv_ready", "inv_done", "avg_ready", "hT_ready")))

    def invert(dve, j, q):
        V = nc.vector
        V.tensor_scalar(den[q][:], c.acc[0:HEADS, 2, bass.ds(j * P, P)], 1e-9, None, ALU.max).then_inc(den_ready, 1)
        dve.wait_ge(den_ready, j + 1)
        V.reciprocal(inv[q][:], den[q][:]).then_inc(inv_ready, 1)

    def spread(pe, j, q):
        pe.wait_ge(inv_ready, j + 1)
        for a in range(2):
            m = nc.tensor.matmul(p_inv[q][:, a * P:(a + 1) * P], c.head_rows[:, a * P:(a + 1) * P], inv[q][:],
                                 start=True, stop=True)
        m.then_inc(inv_done, 1)

    def average(dve, j, q):
        dve.wait_ge(inv_done, j + 1)
        nc.vector.tensor_tensor(avg[q][:], c.acc[:, 0:2, bass.ds(j * P, P)],
                                p_inv[q][:, 0:2 * P].rearrange("p (a n) -> p a n", a=2), ALU.mult).then_inc(avg_ready, 1)

    def relu(act, j, q):
        act.wait_ge(avg_ready, j + 1)
        for a in range(2):
            i = nc.scalar.activation(hT[q][:, a, :], avg[q][:, a, :], ACT.Relu,
                                     bias=c.gat_b[:, block_bias, a:a + 1])
        i.then_inc(hT_ready, 1)
    return hT, hT_ready, invert, spread, average, relu


def second_features(c):
    nc, d = c.nc, c.d
    with ExitStack() as ctx:
        fe = [ctx.enter_context(nc.sbuf_tensor(f"fe2_{i}", [P, ROW], F32)) for i in range(2)]
        start_i = [ctx.enter_context(nc.sbuf_tensor(f"start2_{i}", [P, 1], I32)) for i in range(2)]
        p_fe = [ctx.enter_context(nc.psum_tensor(f"p_fe2_{i}", [P, 512], F32)) for i in range(2)]
        hT, hT_ready, invert, spread, average, relu = end_of_layer(c, ctx, "one", 0)
        stored = sems(nc, ctx, "fe2_stored0", "fe2_stored1")
        scattered = sems(nc, ctx, "er2_scattered0", "er2_scattered1")
        fe_done, fe_ready = sems(nc, ctx, "fe2_done", "fe2_ready")

        with nc.Block() as block:
            @block.sync
            def _(sp):
                def store(j, q):
                    sp.wait_ge(fe_ready, j + 1)
                    sp.dma_start(d["table2"][bass.ds(j * P, P), :], fe[q][:]).then_inc(stored[q], 16)
                over_tiles(sp, store)
                for q in range(2):
                    sp.wait_ge(stored[q], 16 * len(range(q, NT, 2)))

            @block.gpsimd
            def _(pool):
                def scatter(j, q, n=P):
                    pool.wait_ge(fe_ready, j + 1)
                    pool.nop(nofuse=True)
                    nc.gpsimd.indirect_dma_start(
                        out=d["er_start2"], out_offset=bass.IndirectOffsetOnAxis(ap=start_i[q][0:n, :], axis=0),
                        in_=fe[q][0:n, D + HEADS:ROW], in_offset=None).then_inc(scattered[q], 16)
                with pool.Fori(0, (NT - 1) // 2) as k:
                    scatter(2 * k, 0)
                    scatter(2 * k + 1, 1)
                scatter(NT - 1, 0, TAIL)
                for q in range(2):
                    pool.wait_ge(scattered[q], 16 * len(range(q, NT, 2)))

            @block.vector
            def _(dve):
                def features(j, q):
                    if not (isinstance(j, int) and j < 2):
                        dve.wait_ge(stored[q], (j - q) * 8)
                        dve.wait_ge(scattered[q], (j - q) * 8)
                    nc.vector.tensor_copy(start_i[q][:], c.start[:, bass.ds(j, 1)])
                    dve.wait_ge(fe_done, j + 1)
                    nc.vector.tensor_copy(fe[q][:], p_fe[q][:, 0:ROW]).then_inc(fe_ready, 1)

                def tile(j, q, ahead=True):
                    if ahead:
                        invert(dve, j + 1, 1 - q)
                        average(dve, j + 1, 1 - q)
                    features(j, q)
                invert(dve, 0, 0)
                average(dve, 0, 0)
                tile(0, 0)
                tile(1, 1)
                with dve.Fori(1, (NT - 1) // 2) as k:
                    tile(2 * k, 0)
                    tile(2 * k + 1, 1)
                tile(NT - 1, 0, ahead=False)

            @block.scalar
            def _(act):
                over_tiles(act, lambda j, q: relu(act, j, q))

            @block.tensor
            def _(pe):
                def features(j, q):
                    pe.wait_ge(hT_ready, j + 1)
                    for k in range(2):
                        m = nc.tensor.matmul(p_fe[q][:, 0:ROW], hT[q][:, k, :], c.gext2[:, k, :], start=k == 0, stop=k == 1)
                    m.then_inc(fe_done, 1)
                spread(pe, 0, 0)
                with pe.Fori(0, (NT - 1) // 2) as k:
                    spread(pe, 2 * k + 1, 1)
                    features(2 * k, 0)
                    spread(pe, 2 * k + 2, 0)
                    features(2 * k + 1, 1)
                features(NT - 1, 0)


def join(c):
    nc, d = c.nc, c.d
    with ExitStack() as ctx:
        def two(name, shape):
            return [ctx.enter_context(nc.sbuf_tensor(f"{name}{i}", shape, F32)) for i in range(2)]

        x = two("jx", [P, D])
        x2 = two("jx2", [P, D])
        st = two("jst", [P, 10])
        p_h = [ctx.enter_context(nc.psum_tensor(f"p_h{i}", [P, 512], F32)) for i in range(2)]
        hT, hT_ready, invert, spread, average, relu = end_of_layer(c, ctx, "two", 1)
        in_ = sems(nc, ctx, "jx_in0", "jx_in1")
        stored = sems(nc, ctx, "x2_stored0", "x2_stored1")
        h_done, x2_ready, stat, var_ready, std_ready, mean_ready = sems(
            nc, ctx, "h_done", "x2_ready", "stat", "jvar_ready", "jstd_ready", "mean_ready")

        with nc.Block() as block:
            @block.sync
            def _(sp):
                def load(j, q, n=P):
                    sp.dma_start(x[q][0:n, :], d["x"][bass.ds(j * P, n), :]).then_inc(in_[q], 16)

                def store(j, q):
                    sp.wait_ge(x2_ready, j + 1)
                    sp.dma_start(d["x2"][bass.ds(j * P, P), :], x2[q][:]).then_inc(stored[q], 16)

                load(0, 0)
                load(1, 1)
                with sp.Fori(0, (NT - 3) // 2) as k:
                    for q in range(2):
                        store(2 * k + q, q)
                        load(2 * k + 2 + q, q)
                store(NT - 3, 0)
                load(NT - 1, 0, TAIL)
                store(NT - 2, 1)
                store(NT - 1, 0)
                for q in range(2):
                    sp.wait_ge(stored[q], 16 * len(range(q, NT, 2)))

            @block.vector
            def _(dve):
                V = nc.vector

                def add(j, q):
                    s = st[q]
                    if not (isinstance(j, int) and j < 2):
                        dve.wait_ge(stored[q], (j - q) * 8)
                    dve.wait_ge(in_[q], (j - q) * 8 + 16)
                    dve.wait_ge(h_done, j + 1)
                    V.tensor_tensor(x2[q][:], p_h[q][:, 0:D], x[q][:], ALU.add).then_inc(x2_ready, 1)
                    dve.wait_ge(x2_ready, j + 1)
                    V.bn_stats(s[:, 0:6], x2[q][:]).then_inc(stat, 1)
                    dve.wait_ge(stat, 2 * j + 1)
                    dve.nop(nofuse=True)
                    V.bn_aggr(s[:, 6:8], s[:, 0:6]).then_inc(var_ready, 1)
                    dve.wait_ge(std_ready, j + 1)
                    V.reciprocal(s[:, 9:10], s[:, 8:9]).then_inc(stat, 1)
                    dve.wait_ge(stat, 2 * j + 2)
                    V.tensor_copy(c.mean[:, bass.ds(j, 1)], s[:, 6:7])
                    V.tensor_copy(c.rstd[:, bass.ds(j, 1)], s[:, 9:10])

                def tile(j, q, ahead=True):
                    if ahead:
                        invert(dve, j + 1, 1 - q)
                        average(dve, j + 1, 1 - q)
                    add(j, q)
                invert(dve, 0, 0)
                average(dve, 0, 0)
                tile(0, 0)
                tile(1, 1)
                with dve.Fori(1, (NT - 1) // 2) as k:
                    tile(2 * k, 0)
                    tile(2 * k + 1, 1)
                tile(NT - 1, 0, ahead=False)

            @block.scalar
            def _(act):
                def std(j, q):
                    act.wait_ge(var_ready, j + 1)
                    nc.scalar.activation(st[q][:, 8:9], st[q][:, 7:8], ACT.Sqrt, bias=c.eps[:]).then_inc(std_ready, 1)
                relu(act, 0, 0)
                with act.Fori(0, (NT - 1) // 2) as k:
                    relu(act, 2 * k + 1, 1)
                    std(2 * k, 0)
                    relu(act, 2 * k + 2, 0)
                    std(2 * k + 1, 1)
                std(NT - 1, 0)

            @block.tensor
            def _(pe):
                def turn(j, q):
                    pe.wait_ge(hT_ready, j + 1)
                    for k in range(2):
                        t = nc.tensor.transpose(p_h[q][:, k * P:(k + 1) * P], hT[q][:, k, :], c.ident[:])
                    t.then_inc(h_done, 1)
                spread(pe, 0, 0)
                with pe.Fori(0, (NT - 1) // 2) as k:
                    spread(pe, 2 * k + 1, 1)
                    turn(2 * k, 0)
                    spread(pe, 2 * k + 2, 0)
                    turn(2 * k + 1, 1)
                turn(NT - 1, 0)


def slice_block(c):
    nc, d = c.nc, c.d
    with ExitStack() as ctx:
        def sb(name, shape, dt=F32):
            return ctx.enter_context(nc.sbuf_tensor(name, shape, dt))

        def two(name, shape):
            return [sb(f"{name}{i}", shape) for i in range(2)]

        x2 = sb("x2", [P, NT, D])
        swT = sb("swT", [P, 4, NT * P])
        vp = sb("vp", [P, 4, D])
        with ExitStack() as inner:
            ctx_outer, ctx_in = ctx, inner
            p_sum = [inner.enter_context(nc.psum_tensor(f"p_sum{i}", [P, 512], F32)) for i in range(4)]
            bank = [inner.enter_context(nc.psum_tensor(f"bank{i}", [P, 512], F32)) for i in range(4)]
            slice_weights(c, x2, swT, p_sum, bank)
            slice_attention(c, vp, p_sum, bank)
        output(c, x2, swT, vp)


def slice_weights(c, x2, swT, p_sum, bank):
    nc, d = c.nc, c.d
    with ExitStack() as ctx:
        def two(name, shape):
            return [ctx.enter_context(nc.sbuf_tensor(f"{name}{i}", shape, F32)) for i in range(2)]

        xn = two("sxn", [P, D + 1])
        xnT = two("sxnT", [P, 2, P])
        logit = two("logit", [P, SH, SG])
        top = two("top", [P, SH])
        low = two("low", [P, SH, SG])
        ex = two("ex", [P, SH, SG])
        total = two("total", [P, SH])
        inv = two("sinv", [P, SH])
        sw = two("sw", [P, INNER])
        p_xT, p_l, p_t = bank[0], bank[1:3], bank[3]
        in_ = sems(nc, ctx, "x2_in0", "x2_in1")
        (ones, xn_ready, xT_done, xT_ready, l_done, logit_ready, top_ready, low_ready, ex_ready, total_ready, inv_ready,
         sw_ready, t_done, swT_ready) = sems(
            nc, ctx, "ones", "sxn_ready", "sxT_done", "sxT_ready", "l_done", "logit_ready", "top_ready", "low_ready",
            "ex_ready", "total_ready", "sinv_ready", "sw_ready", "t_done", "swT_ready")

        def wide(v):
            return v.unsqueeze(2).broadcast_to([P, SH, SG])

        with nc.Block() as block:
            @block.sync
            def _(sp):
                def load(j, q):
                    if not (isinstance(j, int) and j < 2):
                        sp.wait_ge(in_[q], (j - q) * 8)
                    sp.dma_start(x2[:, bass.ds(j, 1), :].rearrange("p a n -> p (a n)"),
                                 d["x2"][bass.ds(j * P, P), :]).then_inc(in_[q], 16)
                load(0, 0)
                load(1, 1)
                with sp.Fori(1, (NT - 1) // 2) as k:
                    load(2 * k, 0)
                    load(2 * k + 1, 1)
                load(NT - 1, 0)
                for q in range(2):
                    sp.wait_ge(in_[q], 16 * len(range(q, NT, 2)))

            @block.vector
            def _(dve):
                V = nc.vector

                def norm(j, q):
                    dve.wait_ge(in_[q], (j - q) * 8 + 16)
                    V.tensor_scalar(xn[q][:, 0:D], x2[:, bass.ds(j, 1), :].rearrange("p a n -> p (a n)"),
                                    c.mean[:, bass.ds(j, 1)], c.rstd[:, bass.ds(j, 1)], ALU.subtract,
                                    ALU.mult).then_inc(xn_ready, 1)

                def biased(j, q):
                    dve.wait_ge(l_done, j + 1)
                    V.tensor_tensor(logit[q][:].rearrange("p h g -> p (h g)"), p_l[q][:], c.wc_bias[:],
                                    ALU.add).then_inc(logit_ready, 1)
                    dve.wait_ge(logit_ready, j + 1)
                    V.tensor_reduce(top[q][:], logit[q][:], AX.X, ALU.max).then_inc(top_ready, 1)

                def sums(j, q):
                    dve.wait_ge(ex_ready, j + 1)
                    V.tensor_reduce(total[q][:], ex[q][:], AX.X, ALU.add).then_inc(total_ready, 1)
                    dve.wait_ge(total_ready, j + 1)
                    V.reciprocal(inv[q][:], total[q][:]).then_inc(inv_ready, 1)

                def tile(j, q, ahead=2):
                    if ahead > 0:
                        biased(j + 1, 1 - q)
                    sums(j, q)
                    if ahead > 1:
                        dve.wait_ge(t_done, j + 1)
                        norm(j + 2, q)

                V.memset(xn[0][:, D:D + 1], 1.0)
                V.memset(xn[1][:, D:D + 1], 1.0).then_inc(ones, 1)
                norm(0, 0)
                norm(1, 1)
                biased(0, 0)
                with dve.Fori(0, (NT - 3) // 2) as k:
                    tile(2 * k, 0)
                    tile(2 * k + 1, 1)
                tile(NT - 3, 0)
                tile(NT - 2, 1, ahead=1)
                tile(NT - 1, 0, ahead=0)

            @block.gpsimd
            def _(pool):
                def lower(j, q):
                    pool.wait_ge(top_ready, j + 1)
                    nc.gpsimd.tensor_tensor(low[q][:], logit[q][:], wide(top[q][:]), ALU.subtract).then_inc(low_ready, 1)

                def weigh(j, q):
                    pool.wait_ge(inv_ready, j + 1)
                    nc.gpsimd.tensor_tensor(sw[q][:].rearrange("p (h g) -> p h g", h=SH), ex[q][:], wide(inv[q][:]),
                                            ALU.mult).then_inc(sw_ready, 1)
                lower(0, 0)
                with pool.Fori(0, (NT - 1) // 2) as k:
                    lower(2 * k + 1, 1)
                    weigh(2 * k, 0)
                    lower(2 * k + 2, 0)
                    weigh(2 * k + 1, 1)
                weigh(NT - 1, 0)

            @block.scalar
            def _(act):
                A = nc.scalar.activation

                def copy_x(j, q):
                    act.wait_ge(xT_done, j + 1)
                    A(xnT[q][:].rearrange("p k n -> p (k n)"), p_xT[:, 0:D], ACT.Copy).then_inc(xT_ready, 1)

                def exp(j, q):
                    act.wait_ge(low_ready, j + 1)
                    A(ex[q][:], low[q][:], ACT.Exp).then_inc(ex_ready, 1)

                def keep(j, q):
                    act.wait_ge(t_done, j + 1)
                    A(swT[:, :, bass.ds(j * P, P)], p_t[:].rearrange("p (k n) -> p k n", k=4),
                      ACT.Copy).then_inc(swT_ready, 1)

                def tile(j, q, ahead=2):
                    if ahead > 0:
                        exp(j + 1, 1 - q)
                    if ahead > 1:
                        copy_x(j + 2, q)
                    keep(j, q)
                copy_x(0, 0)
                copy_x(1, 1)
                exp(0, 0)
                with act.Fori(0, (NT - 3) // 2) as k:
                    tile(2 * k, 0)
                    tile(2 * k + 1, 1)
                tile(NT - 3, 0)
                tile(NT - 2, 1, ahead=1)
                tile(NT - 1, 0, ahead=0)

            @block.tensor
            def _(pe):
                M, T = nc.tensor.matmul, nc.tensor.transpose

                def turn_x(j, q):
                    pe.wait_ge(xn_ready, j + 1)
                    if not (isinstance(j, int) and j == 0):
                        pe.wait_ge(xT_ready, j)
                    for k in range(2):
                        t = T(p_xT[:, k * P:(k + 1) * P], xn[q][:, k * P:(k + 1) * P], c.ident[:])
                    t.then_inc(xT_done, 1)

                def logits(j, q):
                    pe.wait_ge(xT_ready, j + 1)
                    if not (isinstance(j, int) and j < 2):
                        pe.wait_ge(logit_ready, j - 1)
                    for k in range(2):
                        m = M(p_l[q][:], xnT[q][:, k, :], c.wc[:, k, :], start=k == 0, stop=k == 1)
                    m.then_inc(l_done, 1)

                def slices(j, q, first=False, last=False):
                    pe.wait_ge(sw_ready, j + 1)
                    n = TAIL if last else P
                    for s in range(4):
                        M(p_sum[s][:, 0:D + 1], sw[q][0:n, s * P:(s + 1) * P], xn[q][0:n, :], start=first, stop=last)
                    if not first:
                        pe.wait_ge(swT_ready, j)
                    for s in range(4):
                        t = T(p_t[:, s * P:(s + 1) * P], sw[q][:, s * P:(s + 1) * P], c.ident[:])
                    t.then_inc(t_done, 1)

                def tile(j, q, first=False, ahead=2):
                    if ahead > 0:
                        logits(j + 1, 1 - q)
                    slices(j, q, first)
                    if ahead > 1:
                        turn_x(j + 2, q)
                pe.wait_ge(ones, 1)
                turn_x(0, 0)
                logits(0, 0)
                turn_x(1, 1)
                tile(0, 0, first=True)
                tile(1, 1)
                with pe.Fori(1, (NT - 3) // 2) as k:
                    tile(2 * k, 0)
                    tile(2 * k + 1, 1)
                tile(NT - 3, 0)
                tile(NT - 2, 1, ahead=1)
                slices(NT - 1, 0, last=True)


def slice_attention(c, vp, p_sum, bank):
    nc, d = c.nc, c.d
    with ExitStack() as ctx:
        def sb(name, shape, dt=F32):
            return ctx.enter_context(nc.sbuf_tensor(name, shape, dt))

        wfx = sb("wfx", [P, 2, INNER])
        bfx = sb("bfx", [1, INNER])
        wq, wk, wv = (sb(n, [SD, SD]) for n in ("wq", "wk", "wv"))
        wo = sb("wo", [SD, SH, D])
        soft = sb("soft", [P, 4, 1])
        inv = sb("ainv", [P, 4, 1])
        mean = sb("amean", [P, 4, D + 1])
        meanT = sb("ameanT", [P, 2, INNER])
        share = sb("share", [1, INNER])
        tokT, qT, kT, v, lg, ex, pr, prT, oT = (sb(n, [SD, INNER]) for n in
                                                ("tokT", "qT", "kT", "v", "lg", "aex", "pr", "prT", "oT"))
        top, tot, itot = (sb(n, [SG, SH]) for n in ("atop", "atot", "aitot"))
        loaded, v_step, p_step, exp_done = sems(nc, ctx, "a_loaded", "a_v", "a_p", "a_exp")

        DV = ["soft", "inv", "mean", "meanT", "share", "tokT", "qT", "kT", "v", "top", "low", "tot", "itot", "pr",
              "prT", "oT", "vp"]
        PE = ["meanT", "tokT", "qT", "kT", "v", "lg", "prT", "oT", "vp"]

        def dv(n):
            return DV.index(n) + 1

        def pp(n):
            return PE.index(n) + 1

        def heads(t):
            return t[:].rearrange("p (h g) -> p h g", h=SH)

        with nc.Block() as block:
            @block.sync
            def _(sp):
                for k in range(2):
                    sp.dma_start(wfx[:, k, :], d["W_fx"][k * P:(k + 1) * P, :]).then_inc(loaded, 16)
                sp.dma_start(bfx[:], d["b_fx"].unsqueeze(0)).then_inc(loaded, 16)
                for t, n in ((wq, "W_q"), (wk, "W_k"), (wv, "W_v")):
                    sp.dma_start(t[:], d[n]).then_inc(loaded, 16)
                sp.dma_start(wo[:], d["W_out"].rearrange("(h c) n -> c h n", c=SD)).then_inc(loaded, 16)

            @block.vector
            def _(dve):
                V = nc.vector

                def step(name, ins):
                    ins.then_inc(v_step, 1)
                    dve.wait_ge(v_step, dv(name))

                for s in range(4):
                    i = V.tensor_scalar(soft[:, s, :], p_sum[s][:, D:D + 1], 1e-5, None, ALU.add)
                step("soft", i)
                step("inv", V.reciprocal(inv[:, :, 0], soft[:, :, 0]))
                for s in range(4):
                    i = V.tensor_scalar(mean[:, s, :], p_sum[s][:, 0:D + 1], inv[:, s, :], None, ALU.mult)
                step("mean", i)
                dve.wait_ge(p_step, pp("meanT"))
                V.tensor_copy(meanT[:, 0, :], bank[0][:])
                step("meanT", V.tensor_copy(meanT[:, 1, :], bank[1][:]))
                step("share", V.tensor_copy(share[:], bank[2][0:1, :]))
                for name, t, b in (("tokT", tokT, 3), ("qT", qT, 0), ("kT", kT, 1), ("v", v, 2)):
                    dve.wait_ge(p_step, pp(name))
                    step(name, V.tensor_copy(t[:], bank[b][0:SD, :]))
                dve.wait_ge(p_step, pp("lg"))
                step("top", V.tensor_reduce(top[:], bank[3][0:SD, :].rearrange("p (h g) -> p h g", h=SH), AX.X, ALU.max))
                step("low", V.tensor_tensor(heads(lg), bank[3][0:SD, :].rearrange("p (h g) -> p h g", h=SH),
                                            top[:].unsqueeze(2).broadcast_to([SG, SH, SG]), ALU.subtract))
                dve.wait_ge(exp_done, 1)
                step("tot", V.tensor_reduce(tot[:], heads(ex), AX.X, ALU.add))
                step("itot", V.reciprocal(itot[:], tot[:]))
                step("pr", V.tensor_tensor(heads(pr), heads(ex), itot[:].unsqueeze(2).broadcast_to([SG, SH, SG]), ALU.mult))
                dve.wait_ge(p_step, pp("prT"))
                step("prT", V.tensor_copy(prT[:], bank[0][0:SD, :]))
                dve.wait_ge(p_step, pp("oT"))
                step("oT", V.tensor_copy(oT[:], bank[1][0:SD, :]))
                dve.wait_ge(p_step, pp("vp"))
                for h in range(SH):
                    i = V.tensor_copy(vp[64 * (h % 2):64 * (h % 2) + 64, h // 2, :],
                                      p_sum[h // 2][0:SG, (h % 2) * D:(h % 2 + 1) * D])
                step("vp", i)

            @block.scalar
            def _(act):
                act.wait_ge(v_step, dv("low"))
                nc.scalar.activation(ex[:], lg[:], ACT.Exp, scale=float(SD) ** -0.5).then_inc(exp_done, 1)

            @block.tensor
            def _(pe):
                M, T = nc.tensor.matmul, nc.tensor.transpose
                at = [slice(h * SG, (h + 1) * SG) for h in range(SH)]
                pe.wait_ge(v_step, dv("mean"))
                for s in range(4):
                    for k in range(2):
                        T(bank[k][:, s * P:(s + 1) * P], mean[:, s, k * P:(k + 1) * P], c.ident[:])
                    i = T(bank[2][0:1, s * P:(s + 1) * P], mean[:, s, D:D + 1], c.ident[:])
                i.then_inc(p_step, 1)
                pe.wait_ge(loaded, 16 * 7)
                pe.wait_ge(v_step, dv("share"))
                for h in range(SH):
                    for k in range(2):
                        M(bank[3][0:SD, at[h]], wfx[:, k, at[h]], meanT[:, k, at[h]], start=k == 0, stop=False)
                    i = M(bank[3][0:SD, at[h]], bfx[:, at[h]], share[:, at[h]], start=False, stop=True)
                i.then_inc(p_step, 1)
                pe.wait_ge(v_step, dv("tokT"))
                M(bank[0][0:SD, :], wq[:], tokT[:], start=True, stop=True).then_inc(p_step, 1)
                M(bank[1][0:SD, :], wk[:], tokT[:], start=True, stop=True).then_inc(p_step, 1)
                for h in range(SH):
                    i = M(bank[2][0:SG, at[h]], tokT[:, at[h]], wv[:], start=True, stop=True)
                i.then_inc(p_step, 1)
                pe.wait_ge(v_step, dv("kT"))
                for h in range(SH):
                    i = M(bank[3][0:SG, at[h]], qT[:, at[h]], kT[:, at[h]], start=True, stop=True)
                i.then_inc(p_step, 1)
                pe.wait_ge(v_step, dv("pr"))
                for h in range(SH):
                    i = T(bank[0][0:SG, at[h]], pr[:, at[h]], c.ident[0:SG, 0:SG])
                i.then_inc(p_step, 1)
                pe.wait_ge(v_step, dv("prT"))
                for h in range(SH):
                    i = M(bank[1][0:SD, at[h]], v[:, at[h]], prT[:, at[h]], start=True, stop=True)
                i.then_inc(p_step, 1)
                pe.wait_ge(v_step, dv("oT"))
                for h in range(SH):
                    i = M(p_sum[h // 2][0:SG, (h % 2) * D:(h % 2 + 1) * D], oT[:, at[h]], wo[:, h, :], start=True, stop=True)
                i.then_inc(p_step, 1)


def output(c, x2, swT, vp):
    nc, d = c.nc, c.d
    with ExitStack() as ctx:
        def two(name, shape):
            return [ctx.enter_context(nc.sbuf_tensor(f"{name}{i}", shape, F32)) for i in range(2)]

        w = two("w_now", [P, 4, P])
        xb = two("xb", [P, D])
        y = two("y", [P, D])
        p_y = [ctx.enter_context(nc.psum_tensor(f"p_y{i}", [P, 512], F32)) for i in range(2)]
        w_ready, xb_ready, y_done, y_ready = sems(nc, ctx, "w_now_ready", "xb_ready", "y_done", "y_ready")
        stored = sems(nc, ctx, "y_stored0", "y_stored1")
        with nc.Block() as block:
            @block.scalar
            def _(act):
                def copy(j, q):
                    if not (isinstance(j, int) and j < 2):
                        act.wait_ge(y_done, j - 1)
                    nc.scalar.activation(w[q][:], swT[:, :, bass.ds(j * P, P)], ACT.Copy).then_inc(w_ready, 1)
                copy(0, 0)
                copy(1, 1)
                with act.Fori(1, (NT - 1) // 2) as k:
                    copy(2 * k, 0)
                    copy(2 * k + 1, 1)
                copy(NT - 1, 0)

            @block.gpsimd
            def _(pool):
                def add(j, q):
                    if not (isinstance(j, int) and j < 2):
                        pool.wait_ge(y_ready, j - 1)
                    nc.gpsimd.tensor_tensor(xb[q][:], x2[:, bass.ds(j, 1), :].rearrange("p a n -> p (a n)"), c.b_out[:],
                                            ALU.add).then_inc(xb_ready, 1)
                add(0, 0)
                add(1, 1)
                with pool.Fori(1, (NT - 1) // 2) as k:
                    add(2 * k, 0)
                    add(2 * k + 1, 1)
                add(NT - 1, 0)

            @block.tensor
            def _(pe):
                def mm(j, q):
                    pe.wait_ge(w_ready, j + 1)
                    if not (isinstance(j, int) and j < 2):
                        pe.wait_ge(y_ready, j - 1)
                    for s in range(4):
                        m = nc.tensor.matmul(p_y[q][:, 0:D], w[q][:, s, :], vp[:, s, :], start=s == 0, stop=s == 3)
                    m.then_inc(y_done, 1)
                mm(0, 0)
                mm(1, 1)
                with pe.Fori(1, (NT - 1) // 2) as k:
                    mm(2 * k, 0)
                    mm(2 * k + 1, 1)
                mm(NT - 1, 0)

            @block.vector
            def _(dve):
                def add(j, q):
                    if not (isinstance(j, int) and j < 2):
                        dve.wait_ge(stored[q], (j - q) * 8)
                    dve.wait_ge(xb_ready, j + 1)
                    dve.wait_ge(y_done, j + 1)
                    nc.vector.tensor_tensor(y[q][:], p_y[q][:, 0:D], xb[q][:], ALU.add).then_inc(y_ready, 1)
                add(0, 0)
                add(1, 1)
                with dve.Fori(1, (NT - 1) // 2) as k:
                    add(2 * k, 0)
                    add(2 * k + 1, 1)
                add(NT - 1, 0)

            @block.sync
            def _(sp):
                def store(j, q, n=P):
                    sp.wait_ge(y_ready, j + 1)
                    sp.dma_start(d["out"][bass.ds(j * P, n), :], y[q][0:n, :]).then_inc(stored[q], 16)
                with sp.Fori(0, (NT - 1) // 2) as k:
                    store(2 * k, 0)
                    store(2 * k + 1, 1)
                store(NT - 1, 0, TAIL)
                for q in range(2):
                    sp.wait_ge(stored[q], 16 * len(range(q, NT, 2)))


def build(nc, dram):
    with ExitStack() as ctx:
        c = Core(nc, ctx, dram)
        seq = dram["dst_seq"]
        dram["dst_over"] = bass.AP(seq.tensor, seq.offset, [[P, ET], [1, P + 2]])
        c.ident = c.sb("ident", [P, P])
        c.iota = c.sb("iota", [P, P])
        c.eps = c.sb("eps", [P, 1])
        c.wc = c.sb("wc", [P, 2, INNER])
        c.wc_bias = c.sb("wc_bias", [P, INNER])
        c.inv_temp = c.sb("inv_temp", [P, SH])
        c.b_out = c.sb("b_out", [P, D])
        c.mean = c.sb("mean", [P, NT])
        c.rstd = c.sb("rstd", [P, NT])
        c.start = c.sb("start", [P, NT])
        with ExitStack() as gnn:
            c.ctx = gnn
            c.idx = c.sb("idx", [P, ET], I32)
            c.rel = c.sb("rel", [P, ET])
            c.base = c.sb("base", [1, ET], I32)
            c.not_start = c.sb("not_start", [P, EPP])
            c.go_on = c.sb("go_on", [HEADS, ET])
            c.pass_on = c.sb("pass_on", [HEADS, ET])
            c.is_head = c.sb("is_head", [P, HEADS])
            c.is_tile = c.sb("is_tile", [P, TPB])
            c.to_rows = c.sb("to_rows", [P, 3, P])
            c.head_rows = c.sb("head_rows", [HEADS, D])
            c.head_parts = c.sb("head_parts", [HEADS, P])
            c.gext2 = c.sb("gext2", [P, 2, ROW])
            c.gat_b = c.sb("gat_b", [P, 2, 2])
            with ExitStack() as enc:
                c.ctx = enc
                c.w1a = c.sb("w1a", [P, 2, FF])
                c.label_rows = c.sb("label_rows", [96, FF], BF16)
                c.klass = c.sb("klass", [P, 1])
                c.fused = c.sb("fused", [P, 8, ROW])
                c.bias1 = c.sb("bias1", [P, ROW])
                c.ln_g = c.sb("ln_g", [P, 8])
                c.ln_b = c.sb("ln_b", [P, 8])
                c.nid = c.sb("nid", [P, NT])
                c.base_bc = c.sb("base_bc", [P, ET])
                constants_and_weights(c)
                encode(c)
            c.ctx = gnn
            c.acc = c.sb("acc", [P, 3, NW])
            spread_er(c, 1)
            edges(c, 1)
            second_features(c)
            spread_er(c, 2)
            edges(c, 2)
            join(c)
        slice_block(c)


_GNN = ["emb", "le_W1", "le_b1", "ln_g", "ln_b", "le_W2", "le_b2", "W1", "al1", "ar1", "b1", "W2", "al2", "ar2", "b2"]
_FFN = ["W_fx", "b_fx", "W_x", "b_x", "W_slice", "b_slice", "W_q", "W_k", "W_v", "W_out", "b_out", "temperature"]
_OUT_OF_PLACE = {"emb": "embT", "le_W1": "le_W1T", "W_x": "W_xT"}


def kernel(**inputs):
    import numpy as np
    import concourse.bacc as bacc
    from concourse.bass_utils import run_bass_kernel_spmd

    pad = EP - E
    src, dst = np.asarray(inputs["src"]), np.asarray(inputs["dst"])
    arrays = {
        "x": inputs["x"],
        "src": np.concatenate([src, np.zeros(pad, src.dtype)]).reshape(ET, P),
        "dst": np.concatenate([dst, np.full(pad, N, dst.dtype)]).reshape(ET, P),
        "dst_seq": np.concatenate([np.full(1, -1, dst.dtype), dst, np.full(pad + 1, N, dst.dtype)]),
        "labels": np.concatenate([np.asarray(inputs["node_type_24"]), np.zeros(NT * P - N, np.int32)]),
    }
    for n in _GNN:
        arrays[_OUT_OF_PLACE.get(n, n)] = np.asarray(inputs["L0_gnn_" + n])
    for n in _FFN:
        arrays[_OUT_OF_PLACE.get(n, n)] = np.asarray(inputs["L0_ffn_" + n])
    for n in _OUT_OF_PLACE.values():
        arrays[n] = arrays[n].T
    arrays["W1T"], arrays["W2T"] = arrays["W1"].T, arrays["W2"].T
    arrays["temperature"] = arrays["temperature"].reshape(-1)
    arrays = {f"in_{n}": np.ascontiguousarray(a) for n, a in arrays.items()}

    nc = bacc.Bacc("TRN2", target_bir_lowering=False, num_devices=1)
    dram = {n[3:]: nc.dram_tensor(n, a.shape, mybir.dt.from_np(a.dtype), kind="ExternalInput").ap()
            for n, a in arrays.items()}
    for i in (1, 2):
        dram[f"table{i}"] = nc.dram_tensor(f"table{i}", [NT * P, ROW], F32, kind="Internal").ap()
        dram[f"er_start{i}"] = nc.dram_tensor(f"er_start{i}", [EP, HEADS], F32, kind="Internal").ap()
        dram[f"er_edge{i}"] = nc.dram_tensor(f"er_edge{i}", [HEADS, EP], F32, kind="Internal").ap()
    dram["x2"] = nc.dram_tensor("x2_rows", [NT * P, D], F32, kind="Internal").ap()
    dram["out"] = nc.dram_tensor("out_0", [N, D], F32, kind="ExternalOutput").ap()
    build(nc, dram)
    return run_bass_kernel_spmd(nc, [arrays], core_ids=[0]).results[0]["out_0"]
```

```python
from contextlib import ExitStack

import concourse.bass as bass
from concourse import mybir

ALU = mybir.AluOpType
ACT = mybir.ActivationFunctionType
AX = mybir.AxisListType
F32 = mybir.dt.float32
BF16 = mybir.dt.bfloat16
I32 = mybir.dt.int32
DVE_ONLY = (mybir.EngineType.DVE,)
ACT_ONLY = (mybir.EngineType.Activation,)

P = 128
N, E, D = 6250, 106250, 256
HEADS, HID = 4, 64
CLASSES = 24
FF = 1024
NT = -(-N // P)
TAIL = N - (NT - 1) * P
TPB = 26
BP = TPB * HEADS
ET = 832
EP = ET * P
NB = ET // TPB
PAIRS = NB // 2
EPP = EP // P
ROW = D + 2 * HEADS
NW = NT * P + P
BIG = 1e30
LN_EPS = 1e-5
SLOPE = 0.2
RING = 4
SH, SD, SG = 8, 64, 64
INNER = SH * SD
RESERVED = 2 * TPB


class Core:

    def __init__(self, nc, ctx, dram):
        self.nc, self.ctx, self.d = nc, ctx, dram

    def sem(self, name):
        return self.ctx.enter_context(self.nc.semaphore(name))

    def sb(self, name, shape, dt=F32):
        return self.ctx.enter_context(self.nc.sbuf_tensor(name, shape, dt))


def sems(nc, ctx, *names):
    return [ctx.enter_context(nc.semaphore(n)) for n in names]


def over_tiles(eng, body):
    body(0, 0)
    with eng.Fori(0, (NT - 1) // 2) as k:
        body(2 * k + 1, 1)
        body(2 * k + 2, 0)


def bcast_rows(ap, parts, n):
    return bass.AP(ap.tensor, ap.offset, [[0, parts], [1, n]])


def constants_and_weights(c):
    nc, d = c.nc, c.d
    with ExitStack() as ctx:
        def sb(name, shape, dt=F32):
            return ctx.enter_context(nc.sbuf_tensor(name, shape, dt))

        emb3 = sb("emb3", [P, 2, 3, 32])
        w1b = sb("w1b", [P, 2, FF])
        b1_bc = sb("b1_bc", [96, FF])
        table = sb("table", [96, FF])
        rest = sb("rest", [96, FF])
        parts = sb("parts", [96, 3, FF], BF16)
        gw = [sb(f"gw{i}", [P, 2, D]) for i in range(2)]
        attn = [sb(f"attn{i}", [P, 2, 2 * HEADS]) for i in range(2)]
        gext1 = sb("gext1", [P, 2, ROW])
        le2 = sb("le2", [P, 2, FF])
        le2_b = sb("le2_b", [P, 2])
        le2_bw = sb("le2_bw", [P, 2, P])
        wxT = sb("wxT", [SD, SH, D])
        wsl = sb("wsl", [SD, SG])
        bx = sb("bx", [SD, SH])
        bx_w = sb("bx_w", [SD, SH, P])
        bsl = sb("bsl", [P, SG])
        temp = sb("temp", [P, SH])
        src_i = sb("src_i", [P, 7, P], I32)
        dst_i = sb("dst_i", [P, 7, P], I32)
        src_f = sb("src_f", [P, 7, P])
        dst_f = sb("dst_f", [P, 7, P])
        rel_f = sb("rel_f", [P, 7, P])
        base_f = sb("base_f", [1, ET])
        ends = sb("ends", [HEADS, 3, ET], I32)
        same = sb("same", [HEADS, 3, ET])
        one_row = sb("one_row", [1, P])
        iota_i = sb("iota_i", [P, P], I32)
        nid_i = sb("nid_i", [P, NT + 1], I32)
        seq = sb("seq", [P, EPP + 1], I32)
        zeros = sb("zeros", [P, 2048])
        pm = [ctx.enter_context(nc.psum_tensor(f"pm{i}", [P, 512], F32)) for i in range(8)]

        (loaded, weights_in, attn_in, pool_done, v_step, p_step, a_step, zeroed) = sems(
            nc, ctx, "loaded", "weights_in", "attn_in", "pool_done", "v_step", "p_step", "a_step", "zeroed")
        n_loaded = [0]

        PE = ["table", "attn1", "attn2", "fused0", "fused1", "fused2", "fused3", "fused4", "fused5", "fused6",
              "fused7", "bias1", "slices0", "slices1", "slice_bias", "base"] + [f"idx{g}" for g in range(7)]
        pe_at = {n: i + 1 for i, n in enumerate(PE)}

        with nc.Block() as block:
            @block.sync
            def _(sp):
                def load(dst, src):
                    sp.dma_start(dst, src).then_inc(loaded, 16)
                    n_loaded[0] += 16

                with nc.allow_non_contiguous_dma(reason="short vectors"):
                    for k in range(2):
                        load(w1b[:, k, :], d["le_W1T"][D + k * P:D + (k + 1) * P, :])
                        load(le2[:, k, :], d["le_W2"][k * P:(k + 1) * P, :])
                        load(c.w1a[:, k, :], d["le_W1T"][k * P:(k + 1) * P, :])
                        for i in range(2):
                            load(gw[i][:, k, :], d[f"W{i + 1}"][k * P:(k + 1) * P, :])
                            load((gext1, c.gext2)[i][:, k, 0:D], d[f"W{i + 1}T"][k * P:(k + 1) * P, :])
                    load(b1_bc[:], bcast_rows(d["le_b1"], 96, FF))
                    load(le2_b[:], d["le_b2"].rearrange("(k p) -> p k", p=P))
                    load(c.ln_g[:], d["ln_g"].rearrange("(k p) -> p k", p=P))
                    load(c.ln_b[:], d["ln_b"].rearrange("(k p) -> p k", p=P))
                    for i in range(2):
                        load(c.gat_b[:, i, :], d[f"b{i + 1}"].rearrange("(k p) -> p k", p=P))
                    load(wxT[:], d["W_xT"].rearrange("(h c) n -> c h n", c=SD))
                    load(wsl[:], d["W_slice"])
                    load(bx[:], d["b_x"].rearrange("(h c) -> c h", c=SD))
                    load(bsl[:], bcast_rows(d["b_slice"], P, SG))
                    load(temp[:], bcast_rows(d["temperature"], P, SH))
                    load(c.b_out[:], bcast_rows(d["b_out"], P, D))
                    for g in range(7):
                        rows = min(P, ET - g * P)
                        load(src_i[0:rows, g, :], d["src"][g * P:g * P + rows, :])
                        load(dst_i[0:rows, g, :], d["dst"][g * P:g * P + rows, :])
                    dst_at = d["dst_seq"]
                    load(c.base[:], bass.AP(dst_at.tensor, dst_at.offset + 1, [[0, 1], [P, ET]]))
                    for i, at in enumerate((1, 0, P)):
                        load(ends[:, i, :], bass.AP(dst_at.tensor, dst_at.offset + at, [[0, HEADS], [P, ET]]))
                    load(seq[:], bass.AP(dst_at.tensor, dst_at.offset, [[EPP, P], [1, EPP + 1]]))
                    sp.wait_ge(pool_done, 2)
                    for i in range(2):
                        for h in range(HEADS):
                            for j, a in enumerate(("al", "ar")):
                                lo = HID * (h % 2)
                                sp.dma_start(attn[i][lo:lo + HID, h // 2, j * HEADS + h:j * HEADS + h + 1],
                                             d[f"{a}{i + 1}"][h, :].rearrange("(p o) -> p o", o=1)).then_inc(attn_in, 16)
                    for k in range(2):
                        for r in range(3):
                            sp.dma_start(emb3[:, k, r, 0:CLASSES], d["embT"][k * P:(k + 1) * P, :]).then_inc(attn_in, 16)
                sp.wait_ge(v_step, 1)
                flat = EP * HEADS // P
                for e in (d["er_start1"], d["er_start2"]):
                    v = e.rearrange("(p a) h -> p (a h)", p=P)
                    for o in range(0, flat, 2048):
                        w = min(2048, flat - o)
                        sp.dma_start(v[:, o:o + w], zeros[:, 0:w]).then_inc(zeroed, 16)
                sp.wait_ge(zeroed, 16 * 2 * -(-flat // 2048))

            @block.gpsimd
            def _(pool):
                nc.gpsimd.memset(emb3[:], 0.0).then_inc(pool_done, 1)
                nc.gpsimd.memset(attn[0][:], 0.0)
                nc.gpsimd.memset(attn[1][:], 0.0).then_inc(pool_done, 1)
                nc.gpsimd.memset(c.ident[:], 0.0).then_inc(pool_done, 1)
                pool.wait_ge(pool_done, 3)
                nc.gpsimd.affine_select(out=c.ident[:], in_=c.ident[:], compare_op=ALU.not_equal, fill=1.0, base=0,
                                        pattern=[[-1, P]], channel_multiplier=1).then_inc(pool_done, 1)
                nc.gpsimd.iota(iota_i[:], [[1, P]], base=0, channel_multiplier=0).then_inc(pool_done, 1)
                nc.gpsimd.iota(nid_i[:], [[P, NT + 1]], base=0, channel_multiplier=1).then_inc(pool_done, 1)

            @block.vector
            def _(dve):
                n = [0]

                def link(ins):
                    n[0] += 1
                    ins.then_inc(v_step, 1)
                    dve.wait_ge(v_step, n[0])

                V = nc.vector
                link(V.memset(zeros[:], 0.0))
                V.memset(c.eps[:], LN_EPS)
                V.memset(one_row[:], 1.0).then_inc(v_step, 1)
                n[0] += 1
                dve.wait_ge(pool_done, 6)
                link(V.tensor_copy(c.iota[:], iota_i[:]))
                link(V.tensor_copy(c.nid[:], nid_i[:, 0:NT]))
                link(V.tensor_copy(c.klass[:, 0:1], nid_i[:, 0:1]))
                for r in range(1, 3):
                    link(V.tensor_scalar(c.klass[32 * r:32 * r + 32, :], c.klass[32 * r:32 * r + 32, :], -32.0 * r,
                                         None, ALU.add))
                link(V.tensor_reduce(c.is_head[:], c.ident[:].rearrange("p (t h) -> p h t", h=HEADS), AX.X, ALU.add))
                link(V.tensor_reduce(c.is_tile[:], c.ident[:, 0:BP].rearrange("p (t h) -> p t h", h=HEADS), AX.X, ALU.add))
                link(V.memset(c.to_rows[:], 0.0))
                link(V.tensor_copy(c.to_rows[:, 0:2, :].rearrange("p a (b f) -> p (a b) f", b=2),
                                   c.is_head[:].unsqueeze(2).broadcast_to([P, HEADS, HID])))
                link(V.tensor_copy(c.to_rows[:, 2, 0:HEADS], c.is_head[:]))
                link(V.tensor_copy(c.head_rows[:].rearrange("p (h f) -> p h f", h=HEADS),
                                   c.ident[0:HEADS, 0:HEADS].unsqueeze(2).broadcast_to([HEADS, HEADS, HID])))
                link(V.tensor_copy(c.head_parts[:].rearrange("p (t h) -> p t h", h=HEADS),
                                   c.ident[0:HEADS, 0:HEADS].unsqueeze(1).broadcast_to([HEADS, TPB, HEADS])))
                assert n[0] == 14
                dve.wait_ge(loaded, n_loaded[0])
                link(V.tensor_copy(base_f[:], c.base[:]))
                for g in range(7):
                    rows = min(P, ET - g * P)
                    link(V.tensor_copy(src_f[0:rows, g, :], src_i[0:rows, g, :]))
                    link(V.tensor_copy(dst_f[0:rows, g, :], dst_i[0:rows, g, :]))
                    link(V.tensor_scalar(rel_f[0:rows, g, :], dst_f[0:rows, g, :], dst_f[0:rows, g, 0:1], None,
                                         ALU.subtract))
                assert n[0] == 36
                link(V.tensor_tensor(same[:, 0, :], ends[:, 0, :], ends[:, 1, :], ALU.is_equal))
                link(V.tensor_tensor(same[:, 1, :], ends[:, 0, :], ends[:, 2, :], ALU.is_equal))
                link(V.tensor_tensor(same[:, 2, :], same[:, 0, :], same[:, 1, :], ALU.mult))
                link(V.tensor_scalar(c.go_on[:], same[:, 0, :], -1.0, BIG, ALU.add, ALU.mult))
                link(V.tensor_scalar(c.pass_on[:], same[:, 2, :], -1.0, BIG, ALU.add, ALU.mult))
                link(V.tensor_tensor(c.not_start[:], seq[:, 1:EPP + 1], seq[:, 0:EPP], ALU.is_equal))
                link(V.tensor_copy(le2_bw[:], le2_b[:].unsqueeze(2).broadcast_to([P, 2, P])))
                link(V.tensor_copy(bx_w[:], bx[:].unsqueeze(2).broadcast_to([SD, SH, P])))
                link(V.tensor_scalar(temp[:], temp[:], 0.1, 5.0, ALU.max, ALU.min))
                link(V.reciprocal(c.inv_temp[:], temp[:]))
                dve.wait_ge(p_step, pe_at["table"])
                for h in range(2):
                    link(V.tensor_tensor(table[:, h * 512:(h + 1) * 512], pm[h][0:96, :],
                                         b1_bc[:, h * 512:(h + 1) * 512], ALU.add))
                link(V.tensor_copy(parts[:, 0, :], table[:]))
                link(V.tensor_tensor(rest[:], table[:], parts[:, 0, :], ALU.subtract))
                link(V.tensor_copy(parts[:, 1, :], rest[:]))
                link(V.tensor_tensor(table[:], rest[:], parts[:, 1, :], ALU.subtract))
                link(V.tensor_copy(parts[:, 2, :], table[:]))
                for r in range(3):
                    link(V.tensor_copy(c.label_rows[32 * r:32 * r + 32, :], parts[32 * r:32 * r + 32, r, :]))
                assert n[0] == 56
                for i, g in enumerate((gext1, c.gext2)):
                    dve.wait_ge(p_step, pe_at[f"attn{i + 1}"])
                    link(V.tensor_copy(g[:, :, D:ROW],
                                       pm[2 + i][:, 0:16].rearrange("p (k a) -> p k a", k=2)))
                for k in range(8):
                    dve.wait_ge(p_step, pe_at[f"fused{k}"])
                    link(V.tensor_copy(c.fused[:, k, :], pm[4 + k % 2][:, 0:ROW]))
                dve.wait_ge(p_step, pe_at["bias1"])
                link(V.tensor_copy(c.bias1[:], pm[6][:, 0:ROW]))
                inv = c.inv_temp[:].unsqueeze(2).broadcast_to([P, SH, SG])
                for k in range(2):
                    dve.wait_ge(p_step, pe_at[f"slices{k}"])
                    link(V.tensor_tensor(c.wc[:, k, :].rearrange("p (h g) -> p h g", h=SH),
                                         pm[k][:].rearrange("p (h g) -> p h g", h=SH), inv, ALU.mult))
                dve.wait_ge(p_step, pe_at["slice_bias"])
                cb = c.wc_bias[:].rearrange("p (h g) -> p h g", h=SH)
                link(V.tensor_tensor(cb, pm[7][:].rearrange("p (h g) -> p h g", h=SH),
                                     bsl[:].unsqueeze(1).broadcast_to([P, SH, SG]), ALU.add))
                link(V.tensor_tensor(cb, cb, inv, ALU.mult))
                dve.wait_ge(p_step, pe_at["base"])
                link(V.tensor_copy(c.base_bc[:, 0:512], pm[2][:]))
                link(V.tensor_copy(c.base_bc[:, 512:ET], pm[3][:, 0:ET - 512]))
                for g in range(7):
                    rows = min(P, ET - g * P)
                    dve.wait_ge(p_step, pe_at[f"idx{g}"])
                    q = pm[4 + g % 2]
                    link(V.tensor_copy(c.idx[:, g * P:g * P + rows], q[:, 0:rows]))
                    link(V.tensor_copy(c.rel[:, g * P:g * P + rows], q[:, 256:256 + rows]))

            @block.tensor
            def _(pe):
                M, T = nc.tensor.matmul, nc.tensor.transpose

                def done(ins):
                    ins.then_inc(p_step, 1)

                pe.wait_ge(attn_in, 16 * (16 + 6))
                pe.wait_ge(loaded, n_loaded[0])
                for h in range(2):
                    for k in range(2):
                        m = M(pm[h][0:96, :], emb3[:, k].rearrange("p r q -> p (r q)"), w1b[:, k, h * 512:(h + 1) * 512],
                              start=k == 0, stop=k == 1)
                done(m)
                for i in range(2):
                    for k in range(2):
                        for o in range(2):
                            m = M(pm[2 + i][:, 8 * k:8 * k + 8], gw[i][:, o, k * P:(k + 1) * P], attn[i][:, o, :],
                                  start=o == 0, stop=o == 1)
                    done(m)
                pe.wait_ge(v_step, 57)
                for k in range(8):
                    if k >= 2:
                        pe.wait_ge(v_step, 59 + k - 2)
                    for cc in range(2):
                        m = M(pm[4 + k % 2][:, 0:ROW], le2[:, cc, k * P:(k + 1) * P], gext1[:, cc, :],
                              start=cc == 0, stop=cc == 1)
                    done(m)
                for cc in range(2):
                    m = M(pm[6][:, 0:ROW], le2_bw[:, cc, :], gext1[:, cc, :], start=cc == 0, stop=cc == 1)
                done(m)
                for k in range(2):
                    for h in range(SH):
                        m = M(pm[k][:, h * SG:(h + 1) * SG], wxT[:, h, k * P:(k + 1) * P], wsl[:], start=True, stop=True)
                    done(m)
                for h in range(SH):
                    m = M(pm[7][:, h * SG:(h + 1) * SG], bx_w[:, h, :], wsl[:], start=True, stop=True)
                done(m)
                M(pm[2][:], one_row[:], base_f[0:1, 0:512], start=True, stop=True)
                m = M(pm[3][:, 0:ET - 512], one_row[:], base_f[0:1, 512:ET], start=True, stop=True)
                done(m)
                for g in range(7):
                    rows = min(P, ET - g * P)
                    pe.wait_ge(v_step, 73 if g < 2 else 75 + 2 * (g - 2))
                    q = pm[4 + g % 2]
                    T(q[:, 0:rows], src_f[0:rows, g, :], c.ident[0:rows, 0:rows])
                    m = T(q[:, 256:256 + rows], rel_f[0:rows, g, :], c.ident[0:rows, 0:rows])
                    done(m)


def encode(c):
    nc, d = c.nc, c.d
    with ExitStack() as ctx:
        def sb(name, shape, dt=F32):
            return ctx.enter_context(nc.sbuf_tensor(name, shape, dt))

        x = [sb(f"x{i}", [P, D]) for i in range(2)]
        lab = [sb(f"lab{i}", [96, P], I32) for i in range(2)]
        hot = [sb(f"hot{i}", [96, P], BF16) for i in range(2)]
        xn = [sb(f"xn{i}", [P, D]) for i in range(2)]
        xnT = [sb(f"xnT{i}", [P, D]) for i in range(2)]
        zn = [sb(f"zn{i}", [P, FF]) for i in range(2)]
        yT = [sb(f"yT{i}", [P, FF]) for i in range(2)]
        fe = [sb(f"fe{i}", [P, ROW]) for i in range(2)]
        st = [sb(f"st{i}", [P, 32]) for i in range(2)]
        junk = sb("junk", [P, ET])
        tile_f = [sb(f"tile_f{i}", [P, 1]) for i in range(2)]
        tile_i = [sb(f"tile_i{i}", [P, 1], I32) for i in range(2)]
        rows = [sb(f"rows{i}", [P, P], I32) for i in range(2)]
        cnt = [sb(f"cnt{i}", [P, 1]) for i in range(2)]
        start_f = [sb(f"start_f{i}", [P, 1]) for i in range(2)]
        start_i = [sb(f"start_i{i}", [P, 1], I32) for i in range(2)]
        p_xT = ctx.enter_context(nc.psum_tensor("p_xT", [P, 512], F32))
        p_z = [ctx.enter_context(nc.psum_tensor(f"p_z{i}", [P, 2, 512], F32)) for i in range(2)]
        p_zT = ctx.enter_context(nc.psum_tensor("p_zT", [P, 2, 512], F32))
        p_fe = ctx.enter_context(nc.psum_tensor("p_fe", [P, 512], F32))

        in_ = sems(nc, ctx, "x_in0", "x_in1")
        stored = sems(nc, ctx, "fe_stored0", "fe_stored1")
        scattered = sems(nc, ctx, "er_scattered0", "er_scattered1")
        found = sems(nc, ctx, "rows_in0", "rows_in1")
        (chain, xn_ready, hot_ready, z_half, xT_done, xT_ready, z_done, var_x, std_x, var_z, std_z, scale_z, zn_ready,
         zT_done, yT_ready, fe_done, fe_ready, tile_ready, start_ready) = sems(
            nc, ctx, "chain", "xn_ready", "hot_ready", "z_half", "xT_done", "xT_ready", "z_done", "var_x", "std_x",
            "var_z", "std_z", "scale_z", "zn_ready", "zT_done", "yT_ready", "fe_done", "fe_ready", "tile_ready",
            "start_ready")
        free_x, counted = sems(nc, ctx, "free_x", "counted")

        with nc.Block() as block:
            @block.sync
            def _(sp):
                def store(j, q):
                    sp.wait_ge(fe_ready, j + 1)
                    sp.dma_start(d["table1"][bass.ds(j * P, P), :], fe[q][:]).then_inc(stored[q], 16)

                def load(j, q, n=P):
                    sp.wait_ge(free_x, j + 1)
                    sp.dma_start(x[q][0:n, :], d["x"][bass.ds(j * P, n), :]).then_inc(in_[q], 16)
                    at = d["labels"]
                    sp.dma_start(lab[q][:], at[bass.ds(j * P, P)].unsqueeze(0).broadcast_to([96, P])).then_inc(in_[q], 16)

                sp.sem_inc(free_x, 2)
                load(0, 0)
                load(1, 1)
                with sp.Fori(0, (NT - 3) // 2) as k:
                    load(2 * k + 2, 0)
                    store(2 * k, 0)
                    load(2 * k + 3, 1)
                    store(2 * k + 1, 1)
                load(NT - 1, 0, TAIL)
                for j in range(NT - 3, NT):
                    store(j, j % 2)
                for q in range(2):
                    sp.wait_ge(stored[q], 16 * len(range(q, NT, 2)))

            @block.gpsimd
            def _(pool):
                def fetch(j, q):
                    pool.wait_ge(tile_ready, j + 1)
                    pool.nop(nofuse=True)
                    nc.gpsimd.indirect_dma_start(
                        out=rows[q][:], out_offset=None, in_=d["dst"],
                        in_offset=bass.IndirectOffsetOnAxis(ap=tile_i[q][:], axis=0)).then_inc(found[q], 16)

                def scatter(j, q, n=P):
                    pool.wait_ge(fe_ready, j + 1)
                    pool.wait_ge(start_ready, j + 1)
                    pool.nop(nofuse=True)
                    nc.gpsimd.indirect_dma_start(
                        out=d["er_start1"], out_offset=bass.IndirectOffsetOnAxis(ap=start_i[q][0:n, :], axis=0),
                        in_=fe[q][0:n, D + HEADS:ROW], in_offset=None).then_inc(scattered[q], 16)

                fetch(0, 0)
                with pool.Fori(0, (NT - 1) // 2) as k:
                    fetch(2 * k + 1, 1)
                    scatter(2 * k, 0)
                    fetch(2 * k + 2, 0)
                    scatter(2 * k + 1, 1)
                scatter(NT - 1, 0, TAIL)
                for q in range(2):
                    pool.wait_ge(scattered[q], 16 * len(range(q, NT, 2)))

            @block.vector
            def _(dve):
                V = nc.vector

                def norm_x(j, q):
                    dve.wait_ge(in_[q], 16 * (2 * (j // 2) + 2) if isinstance(j, int) else (j + 2 - q) * 16)
                    s = st[q]
                    V.bn_stats(s[:, 0:6], x[q][:]).then_inc(chain, 1)
                    V.tensor_scalar(hot[q][:], lab[q][:], c.klass[0:96, :], None, ALU.is_equal).then_inc(hot_ready, 1)
                    dve.wait_ge(chain, 4 * j + 1)
                    dve.nop(nofuse=True)
                    V.bn_aggr(s[:, 6:8], s[:, 0:6]).then_inc(var_x, 1)
                    V.tensor_scalar(junk[:], c.base_bc[:], c.nid[:, bass.ds(j, 1)], 0.0, ALU.is_lt, ALU.add,
                                    accum_out=tile_f[q][:]).then_inc(chain, 1)
                    dve.wait_ge(chain, 4 * j + 2)
                    V.tensor_scalar(tile_f[q][:], tile_f[q][:], -1.0, 0.0, ALU.add, ALU.max).then_inc(chain, 1)
                    dve.wait_ge(chain, 4 * j + 3)
                    V.tensor_copy(tile_i[q][:], tile_f[q][:]).then_inc(tile_ready, 1)
                    dve.wait_ge(std_x, j + 1)
                    V.reciprocal(s[:, 9:10], s[:, 8:9]).then_inc(chain, 1)
                    dve.wait_ge(chain, 4 * j + 4)
                    V.tensor_scalar(xn[q][:], x[q][:], s[:, 6:7], s[:, 9:10], ALU.subtract,
                                    ALU.mult).then_inc(xn_ready, 1)
                    dve.wait_ge(xn_ready, j + 1)
                    dve.sem_inc(free_x, 1)

                def norm_z(j, q):
                    s = st[q]
                    dve.wait_ge(z_done, j + 1)
                    V.bn_stats(s[:, 10:16], p_z[q][:, 0, :])
                    V.bn_stats(s[:, 16:22], p_z[q][:, 1, :]).then_inc(z_half, 1)
                    dve.wait_ge(z_half, 2 * j + 1)
                    dve.nop(nofuse=True)
                    V.bn_aggr(s[:, 22:24], s[:, 10:22]).then_inc(var_z, 1)
                    dve.wait_ge(std_z, j + 1)
                    V.reciprocal(s[:, 25:26], s[:, 24:25]).then_inc(z_half, 1)
                    dve.wait_ge(z_half, 2 * j + 2)
                    V.scalar_tensor_tensor(out=s[:, 26:27], in0=s[:, 22:23], scalar=-1.0, in1=s[:, 25:26],
                                           op0=ALU.mult, op1=ALU.mult).then_inc(scale_z, 1)
                    dve.wait_ge(scale_z, j + 1)
                    V.tensor_scalar(zn[q][:, 0:512], p_z[q][:, 0, :], s[:, 25:26], s[:, 26:27], ALU.mult,
                                    ALU.add).then_inc(zn_ready, 1)

                def edge_start(j, q):
                    if not (isinstance(j, int) and j < 2):
                        dve.wait_ge(scattered[q], (j - q) * 8)
                    dve.wait_ge(found[q], 16 * (j // 2 + 1) if isinstance(j, int) else (j + 2 - q) * 8)
                    V.tensor_scalar(junk[:, 0:P], rows[q][:], c.nid[:, bass.ds(j, 1)], 0.0, ALU.is_lt, ALU.add,
                                    accum_out=cnt[q][:]).then_inc(counted, 1)
                    dve.wait_ge(counted, 2 * j + 1)
                    V.scalar_tensor_tensor(out=start_f[q][:], in0=tile_f[q][:], scalar=float(P), in1=cnt[q][:],
                                           op0=ALU.mult, op1=ALU.add).then_inc(counted, 1)
                    dve.wait_ge(counted, 2 * j + 2)
                    V.tensor_copy(start_i[q][:], start_f[q][:]).then_inc(start_ready, 1)
                    V.tensor_copy(c.start[:, bass.ds(j, 1)], start_f[q][:])

                def features(j, q):
                    if not (isinstance(j, int) and j < 2):
                        dve.wait_ge(stored[q], (j - q) * 8)
                        dve.wait_ge(scattered[q], (j - q) * 8)
                    dve.wait_ge(fe_done, j + 1)
                    V.tensor_tensor(fe[q][:], p_fe[:, 0:ROW], c.bias1[:], ALU.add).then_inc(fe_ready, 1)

                def tile(j, q, ahead=True, behind=True):
                    norm_z(j, q)
                    if ahead:
                        norm_x(j + 1, 1 - q)
                    edge_start(j, q)
                    if behind:
                        features(j - 1, 1 - q)

                norm_x(0, 0)
                tile(0, 0, behind=False)
                tile(1, 1)
                tile(2, 0)
                with dve.Fori(1, (NT - 3) // 2) as k:
                    tile(2 * k + 1, 1)
                    tile(2 * k + 2, 0)
                tile(NT - 2, 1)
                tile(NT - 1, 0, ahead=False)
                features(NT - 1, 0)

            @block.scalar
            def _(act):
                A = nc.scalar.activation

                def head(j, q):
                    s = st[q]
                    act.wait_ge(var_x, j + 1)
                    A(s[:, 8:9], s[:, 7:8], ACT.Sqrt, bias=c.eps[:]).then_inc(std_x, 1)
                    act.wait_ge(xT_done, j + 1)
                    A(xnT[q][:], p_xT[:, 0:D], ACT.Copy).then_inc(xT_ready, 1)

                def mid(j, q):
                    s = st[q]
                    act.wait_ge(var_z, j + 1)
                    A(s[:, 24:25], s[:, 23:24], ACT.Sqrt, bias=c.eps[:]).then_inc(std_z, 1)
                    act.wait_ge(scale_z, j + 1)
                    A(zn[q][:, 512:1024], p_z[q][:, 1, :], ACT.Identity, bias=s[:, 26:27],
                      scale=s[:, 25:26]).then_inc(zn_ready, 1)

                def tail(j, q):
                    for h in range(2):
                        act.wait_ge(zT_done, 2 * j + h + 1)
                        for i in range(4):
                            k = 4 * h + i
                            a = A(yT[q][:, k * P:(k + 1) * P], p_zT[:, h, i * P:(i + 1) * P], ACT.Relu,
                                  bias=c.ln_b[:, k:k + 1], scale=c.ln_g[:, k:k + 1])
                        a.then_inc(yT_ready, 1)

                def tile(j, q, ahead=True):
                    mid(j, q)
                    if ahead:
                        head(j + 1, 1 - q)
                    tail(j, q)

                head(0, 0)
                with act.Fori(0, (NT - 1) // 2) as k:
                    tile(2 * k, 0)
                    tile(2 * k + 1, 1)
                tile(NT - 1, 0, ahead=False)

            @block.tensor
            def _(pe):
                M, T = nc.tensor.matmul, nc.tensor.transpose

                def xT(j, q):
                    pe.wait_ge(xn_ready, j + 1)
                    for k in range(2):
                        t = T(p_xT[:, k * P:(k + 1) * P], xn[q][:, k * P:(k + 1) * P], c.ident[:])
                    t.then_inc(xT_done, 1)

                def z(j, q):
                    pe.wait_ge(xT_ready, j + 1)
                    pe.wait_ge(hot_ready, j + 1)
                    for h in range(2):
                        cols = slice(h * 512, (h + 1) * 512)
                        for k in range(2):
                            M(p_z[q][:, h, :], xnT[q][:, k * P:(k + 1) * P], c.w1a[:, k, cols], start=k == 0, stop=False)
                        m = M(p_z[q][:, h, :], hot[q][:], c.label_rows[:, cols], start=False, stop=True)
                    m.then_inc(z_done, 1)

                def zT(j, q):
                    pe.wait_ge(zn_ready, 2 * j + 2)
                    for h in range(2):
                        for i in range(4):
                            k = 4 * h + i
                            t = T(p_zT[:, h, i * P:(i + 1) * P], zn[q][:, k * P:(k + 1) * P], c.ident[:])
                        t.then_inc(zT_done, 1)

                def fe_mm(j, q):
                    pe.wait_ge(yT_ready, 2 * j + 2)
                    if not (isinstance(j, int) and j == 0):
                        pe.wait_ge(fe_ready, j)
                    for k in range(8):
                        m = M(p_fe[:, 0:ROW], yT[q][:, k * P:(k + 1) * P], c.fused[:, k, :], start=k == 0, stop=k == 7)
                    m.then_inc(fe_done, 1)

                xT(0, 0)
                z(0, 0)
                with pe.Fori(0, (NT - 1) // 2) as k:
                    xT(2 * k + 1, 1)
                    zT(2 * k, 0)
                    z(2 * k + 1, 1)
                    fe_mm(2 * k, 0)
                    xT(2 * k + 2, 0)
                    zT(2 * k + 1, 1)
                    z(2 * k + 2, 0)
                    fe_mm(2 * k + 1, 1)
                zT(NT - 1, 0)
                fe_mm(NT - 1, 0)


def edges(c, layer):
    nc, d = c.nc, c.d
    with ExitStack() as ctx:
        def sb(name, shape, dt=F32):
            return ctx.enter_context(nc.sbuf_tensor(f"{name}_{layer}", shape, dt))

        def two(name, shape, dt=F32):
            return [sb(f"{name}{i}", shape, dt) for i in range(2)]

        rows = two("rows", [P, TPB, ROW])
        scaled = sb("scaled", [P, RING, D])
        window = sb("window", [P, RING, P])
        idx_now = two("idx_now", [P, TPB], I32)
        er = two("er_now", [BP, P])
        el = sb("el", [P, BP])
        dst_i = two("dst_i", [BP, P + 2], I32)
        cut = sb("cut", [BP, P + 1])
        fst = sb("fst", [BP, P])
        e0 = sb("e0", [BP, P])
        e = sb("e", [BP, P])
        run_max = sb("run_max", [BP, P])
        node_max = sb("node_max", [BP, P])
        full_max = sb("full_max", [BP, P])
        down = sb("down", [BP, P])
        prob = sb("prob", [BP, P])
        last_max = sb("last_max", [BP, TPB])
        carried = sb("carried", [HEADS, NB * TPB + 1])
        brought = sb("brought", [HEADS, TPB])
        spread_junk = sb("spread_junk", [BP, TPB])
        carry = sb("carry", [BP, 1])
        fade = sb("fade", [BP, 1])
        fade_t = sb("fade_t", [BP, TPB])
        wt = two("wt", [P, BP])
        fades = two("fades", [P, 3, TPB])
        kept = sb("kept", [P, 2, 3])
        er_at = sb("er_at", [P, EPP, HEADS])
        spread = sb("spread", [P, HEADS, EPP])
        first_id = sb("first_id", [P, 1], I32)
        first_row = sb("first_row", [P, ROW])
        first = sb("first", [P, RING, 3])
        p_part = [ctx.enter_context(nc.psum_tensor(f"p_part{i}_{layer}", [P, 512], F32)) for i in range(RING)]
        p_e = ctx.enter_context(nc.psum_tensor(f"p_e_{layer}", [P, 512], F32))
        p_carry = ctx.enter_context(nc.psum_tensor(f"p_carry_{layer}", [P, 512], F32))
        p_w = ctx.enter_context(nc.psum_tensor(f"p_w_{layer}", [P, 512], F32))
        p_fade = ctx.enter_context(nc.psum_tensor(f"p_fade_{layer}", [P, 512], F32))

        names = ["idx_ready", "el_ready", "eT_done", "link", "last_ready", "last_done", "brought_ready",
                 "brought_done", "down_ready", "carry_ready", "exp_done", "fade_done", "fade_ready", "w_done",
                 "fadeT_done", "w_ready", "scaled_ready", "mm_done", "kept_ready", "taken", "fixed",
                 "copied", "psum_zero"]
        S = dict(zip(names, sems(nc, ctx, *(f"{n}_{layer}" for n in names))))
        moved, row_in, scanned = sems(nc, ctx, *(f"{n}_{layer}" for n in ("er_moved", "row_in", "scanned")))
        gathered = sems(nc, ctx, *(f"gathered{i}_{layer}" for i in range(2)))
        loaded = sems(nc, ctx, *(f"batch_in{i}_{layer}" for i in range(2)))

        PREP = TPB - 23
        ZEROED = RING + (2 if layer == 1 else 1)
        LEAD = RING - 1

        def ring(q, s):
            return (q * TPB + s) % RING

        with nc.Block() as block:
            @block.sync
            def _(sp):
                def load(b, q):
                    sp.wait_ge(S["down_ready"], b + 1)
                    ee, dd = d[f"er_edge{layer}"], d["dst_seq"]
                    sp.dma_start(er[q][:], ee.rearrange("h (b t e) -> b t h e", t=TPB, e=P)[bass.ds(b, 1)].rearrange(
                        "b t h e -> (b t) h e")).then_inc(loaded[q], 16)
                    sp.dma_start(dst_i[q][:], d["dst_over"][bass.ds(b * TPB, TPB), :].unsqueeze(1).broadcast_to(
                        [TPB, HEADS, P + 2])).then_inc(loaded[q], 16)

                at = d["dst_seq"]
                with nc.allow_non_contiguous_dma(reason="one id per partition"):
                    sp.dma_start(first_id[:], bass.AP(at.tensor, at.offset + 1, [[EPP, P], [1, 1]])).then_inc(moved, 16)
                sp.wait_ge(moved, 16)
                sp.dma_start(er_at[:], d[f"er_start{layer}"].rearrange("(p a) h -> p a h", p=P)).then_inc(moved, 16)
                for h in range(HEADS):
                    sp.wait_ge(scanned, h + 1)
                    sp.dma_start(d[f"er_edge{layer}"][h].rearrange("(p a) -> p a", p=P), spread[:, h, :]).then_inc(moved, 16)
                sp.wait_ge(moved, 16 * (2 + HEADS))
                sp.sem_inc(S["down_ready"], 2)
                with sp.Fori(0, PAIRS) as k:
                    load(2 * k, 0)
                    load(2 * k + 1, 1)

            @block.gpsimd
            def _(pool):
                pool.wait_ge(moved, 16)
                nc.gpsimd.indirect_dma_start(
                    out=first_row[:], out_offset=None, in_=d[f"table{layer}"],
                    in_offset=bass.IndirectOffsetOnAxis(ap=first_id[:], axis=0)).then_inc(row_in, 16)
                with pool.Fori(0, PAIRS) as k:
                    for q in range(2):
                        b = 2 * k + q
                        pool.wait_ge(S["idx_ready"], b + 1)
                        for s in range(TPB):
                            if s % 4 == 0:
                                pool.wait_ge(S["scaled_ready"], b * TPB + s + 4)
                            pool.nop(nofuse=True)
                            nc.gpsimd.indirect_dma_start(
                                out=rows[q][:, s, :], out_offset=None, in_=d[f"table{layer}"],
                                in_offset=bass.IndirectOffsetOnAxis(ap=idx_now[q][:, s:s + 1], axis=0)
                            ).then_inc(gathered[q], 16)

            @block.vector
            def _(dve):
                V = nc.vector
                LINKS = 7

                def index(b, q):
                    V.tensor_copy(idx_now[q][:], c.idx[:, bass.ds(b * TPB, TPB)]).then_inc(S["idx_ready"], 1)

                def prep(b, q):
                    def links(k):
                        dve.wait_ge(S["link"], b * LINKS + k)

                    def borders():
                        dve.wait_ge(loaded[q], (b + 2 - q) * 16)
                        V.tensor_tensor(cut[:], dst_i[q][:, 1:P + 2], dst_i[q][:, 0:P + 1],
                                        ALU.not_equal).then_inc(S["link"], 1)
                        V.tensor_scalar(fst[:], dst_i[q][:, 1:P + 1], dst_i[q][:, 1:2], -BIG, ALU.not_equal, ALU.mult)

                    def sum_():
                        links(1)
                        V.tensor_scalar(cut[:], cut[:], -BIG, None, ALU.mult).then_inc(S["link"], 1)
                        dve.wait_ge(S["eT_done"], b + 1)
                        V.tensor_tensor(e0[:], p_e[0:BP, 0:P], er[q][:], ALU.add).then_inc(S["link"], 1)

                    def leak():
                        links(3)
                        V.scalar_tensor_tensor(out=e[:], in0=e0[:], scalar=SLOPE, in1=e0[:], op0=ALU.mult,
                                               op1=ALU.max).then_inc(S["link"], 1)

                    def forth():
                        links(4)
                        V.tensor_tensor_scan(run_max[:], cut[:, 0:P], e[:], -BIG, ALU.add, ALU.max).then_inc(S["link"], 1)

                    def back():
                        links(5)
                        V.tensor_tensor_scan(node_max[:, ::-1], cut[:, :0:-1], run_max[:, ::-1], -BIG, ALU.add,
                                             ALU.max).then_inc(S["link"], 1)

                    def last():
                        links(6)
                        V.tensor_scalar(last_max[:], c.is_tile[0:BP, :], node_max[:, P - 1:P], None,
                                        ALU.mult).then_inc(S["last_ready"], 1)

                    def carries():
                        dve.wait_ge(S["last_done"], b + 1)
                        V.tensor_tensor_scan(carried[:, bass.ds(b * TPB + 1, TPB)], c.pass_on[:, bass.ds(b * TPB, TPB)],
                                             p_carry[0:HEADS, 0:TPB], carried[:, bass.ds(b * TPB, 1)], ALU.add,
                                             ALU.max).then_inc(S["link"], 1)

                    def bring():
                        links(7)
                        V.tensor_tensor(brought[:], carried[:, bass.ds(b * TPB, TPB)], c.go_on[:, bass.ds(b * TPB, TPB)],
                                        ALU.add).then_inc(S["brought_ready"], 1)

                    def own():
                        dve.wait_ge(S["brought_done"], b + 1)
                        V.tensor_tensor_reduce(spread_junk[:], p_carry[0:BP, 64:64 + TPB], c.is_tile[0:BP, :], 1.0, 0.0,
                                               ALU.mult, ALU.add, carry[:]).then_inc(S["carry_ready"], 1)

                    def full():
                        dve.wait_ge(S["carry_ready"], 2 * b + 1)
                        V.scalar_tensor_tensor(out=full_max[:], in0=fst[:], scalar=carry[:], in1=node_max[:],
                                               op0=ALU.add, op1=ALU.max).then_inc(S["carry_ready"], 1)

                    def shift():
                        dve.wait_ge(S["carry_ready"], 2 * b + 2)
                        V.tensor_tensor(down[:], e[:], full_max[:], ALU.subtract).then_inc(S["down_ready"], 1)

                    def fade_():
                        dve.wait_ge(S["fade_done"], b + 1)
                        V.tensor_scalar(fade_t[:], c.is_tile[0:BP, :], fade[:], None, ALU.mult).then_inc(S["fade_ready"], 1)

                    return {PREP + 1: borders, PREP + 3: sum_, PREP + 4: leak, PREP + 5: forth, PREP + 6: back,
                            PREP + 7: last, PREP + 10: carries, PREP + 11: bring, PREP + 13: own, PREP + 14: full,
                            PREP + 15: shift, PREP + 17: fade_}

                def make_window(i, q, s):
                    dve.wait_ge(S["mm_done"], i + 1)
                    V.tensor_scalar(window[:, ring(q, s), :], c.iota[:], c.rel[:, bass.ds(i, 1)], None, ALU.is_equal)

                def scale(q, s):
                    V.tensor_tensor(scaled[:, ring(q, s), :].rearrange("p (h f) -> p h f", h=HEADS),
                                    rows[q][:, s, 0:D].rearrange("p (h f) -> p h f", h=HEADS),
                                    wt[q][:, HEADS * s:HEADS * s + HEADS].unsqueeze(2).broadcast_to([P, HEADS, HID]),
                                    ALU.mult).then_inc(S["scaled_ready"], 1)

                def take(i, q, s):
                    dve.wait_ge(S["mm_done"], i + RING + 1)
                    V.tensor_copy(first[:, ring(q, s), :].unsqueeze(2), p_part[ring(q, s)][:, 0:3 * P].rearrange(
                        "p (a n) -> p a n", a=3)[:, :, 0:1]).then_inc(S["taken"], 1)

                def keep(i, q, s, at):
                    dve.wait_ge(S["copied"], i + RING)
                    dve.wait_ge(S["fixed"], i + 1)
                    V.tensor_tensor(kept[:, s % 2, :].unsqueeze(2), c.acc[:, :, bass.ds(at, 1)], fades[q][:, :, s:s + 1],
                                    ALU.mult).then_inc(S["kept_ready"], 1)

                def fix(i, q, s, at):
                    dve.wait_ge(S["taken"], i + 1)
                    dve.wait_ge(S["kept_ready"], i + 1)
                    V.tensor_tensor(c.acc[:, :, bass.ds(at, 1)], kept[:, s % 2, :].unsqueeze(2),
                                    first[:, ring(q, s), :].unsqueeze(2), ALU.add).then_inc(S["fixed"], 1)

                def batch(b, q, ahead, more=False):
                    steps = prep(b + 1, 1 - q) if ahead else {}
                    if more:
                        dve.wait_ge(gathered[q], (b + 2 - q) * 8 * TPB)
                        index(b + 2, q)
                    for s in range(TPB):
                        i = b * TPB + s
                        if s % 8 == 0:
                            at = nc.values_load_multi_w_load_instructions(
                                c.base[0:1, bass.ds(i, min(8, TPB - s))], engines=DVE_ONLY, min_val=0, max_val=N,
                                skip_runtime_bounds_check_because="a node's number")[1]
                        to = (q, s + LEAD) if s + LEAD < TPB else (1 - q, s + LEAD - TPB)
                        scales = ahead or s + LEAD < TPB
                        take(i, q, s)
                        keep(i, q, s, at[s % 8])
                        if scales:
                            make_window(i + LEAD, *to)
                        fix(i, q, s, at[s % 8])
                        if scales:
                            if s == TPB - LEAD:
                                dve.wait_ge(S["w_ready"], 2 * b + 4)
                            scale(*to)
                        if s in steps:
                            steps[s]()

                index(0, 0)
                index(1, 1)
                dve.wait_ge(moved, 32)
                dve.wait_ge(row_in, 16)
                for h in range(HEADS):
                    V.tensor_tensor_scan(spread[:, h, :], c.not_start[:], er_at[:, :, h],
                                         first_row[:, D + HEADS + h:D + HEADS + h + 1],
                                         ALU.mult, ALU.add).then_inc(scanned, 1)
                if layer == 1:
                    V.memset(c.acc[:], 0.0).then_inc(S["psum_zero"], 1)
                V.memset(carried[:, 0:1], -BIG).then_inc(S["psum_zero"], 1)
                for r in range(RING):
                    V.memset(p_part[r][:], 0.0).then_inc(S["psum_zero"], 1)
                dve.wait_ge(S["psum_zero"], ZEROED)
                dve.sem_inc(S["fixed"], 1)
                for _, step in sorted(prep(0, 0).items()):
                    step()
                dve.wait_ge(S["w_ready"], 2)
                for s in range(LEAD):
                    make_window(s, 0, s)
                    scale(0, s)
                with dve.Fori(0, PAIRS - 1) as k:
                    batch(2 * k, 0, True, more=True)
                    batch(2 * k + 1, 1, True, more=True)
                batch(NB - 2, 0, True)
                batch(NB - 1, 1, False)

            @block.scalar
            def _(act):
                A = nc.scalar.activation

                def prep(b, q):
                    def pick():
                        act.wait_ge(gathered[q], (b + 2 - q) * 8 * TPB)
                        A(el[:].rearrange("p (t h) -> p t h", h=HEADS), rows[q][:, :, D:D + HEADS],
                          ACT.Copy).then_inc(S["el_ready"], 1)

                    def probs():
                        act.wait_ge(S["down_ready"], b + 3)
                        A(prob[:], down[:], ACT.Exp).then_inc(S["exp_done"], 1)
                        A(fade[:], full_max[:, 0:1], ACT.Exp, bias=carry[:], scale=-1.0).then_inc(S["fade_done"], 1)

                    def copy_out():
                        act.wait_ge(S["w_done"], b + 1)
                        A(wt[q][:], p_w[:, 0:BP], ACT.Copy).then_inc(S["w_ready"], 1)
                        act.wait_ge(S["fadeT_done"], b + 1)
                        A(fades[q][:].rearrange("p a t -> p (a t)"), p_fade[:, 0:3 * TPB],
                          ACT.Copy).then_inc(S["w_ready"], 1)
                    return {PREP: pick, PREP + 16: probs, PREP + 19: copy_out}

                def batch(b, q, ahead):
                    steps = prep(b + 1, 1 - q) if ahead else {}
                    for s in range(TPB):
                        i = b * TPB + s
                        if s % 8 == 0:
                            at = nc.values_load_multi_w_load_instructions(
                                c.base[0:1, bass.ds(i, min(8, TPB - s))], engines=ACT_ONLY, min_val=0, max_val=N,
                                skip_runtime_bounds_check_because="a node's number")[1]
                        act.wait_ge(S["taken"], i + 1)
                        act.wait_ge(S["copied"], i + RING)
                        A(c.acc[:, :, bass.ds(at[s % 8] + 1, P - 1)],
                          p_part[ring(q, s)][:, 0:3 * P].rearrange("p (a n) -> p a n", a=3)[:, :, 1:P],
                          ACT.Copy).then_inc(S["copied"], 1)
                        if s in steps:
                            steps[s]()

                act.sem_inc(S["copied"], RING)
                for _, step in sorted(prep(0, 0).items()):
                    step()
                with act.Fori(0, PAIRS - 1) as k:
                    batch(2 * k, 0, True)
                    batch(2 * k + 1, 1, True)
                batch(NB - 2, 0, True)
                batch(NB - 1, 1, False)

            @block.tensor
            def _(pe):
                M, T = nc.tensor.matmul, nc.tensor.transpose

                def prep(b, q):
                    def eT():
                        pe.wait_ge(S["el_ready"], b + 1)
                        pe.nop(nofuse=True)
                        T(p_e[0:BP, 0:P], el[:], c.ident[:]).then_inc(S["eT_done"], 1)

                    def last():
                        pe.wait_ge(S["last_ready"], b + 1)
                        pe.nop(nofuse=True)
                        M(p_carry[0:HEADS, 0:TPB], c.is_head[0:BP, :], last_max[:], start=True,
                          stop=True).then_inc(S["last_done"], 1)

                    def bring():
                        pe.wait_ge(S["brought_ready"], b + 1)
                        pe.nop(nofuse=True)
                        M(p_carry[0:BP, 64:64 + TPB], c.head_parts[:], brought[:], start=True,
                          stop=True).then_inc(S["brought_done"], 1)

                    def turn():
                        pe.wait_ge(S["exp_done"], b + 1)
                        pe.nop(nofuse=True)
                        T(p_w[:, 0:BP], prob[:], c.ident[0:BP, 0:BP]).then_inc(S["w_done"], 1)

                    def fades_():
                        pe.wait_ge(S["fade_ready"], b + 1)
                        pe.nop(nofuse=True)
                        for a in range(3):
                            m = M(p_fade[:, a * TPB:(a + 1) * TPB], c.to_rows[0:BP, a, :], fade_t[:], start=True, stop=True)
                        m.then_inc(S["fadeT_done"], 1)
                    return {PREP + 3: eT, PREP + 10: last, PREP + 13: bring, PREP + 18: turn, PREP + 19: fades_}

                def batch(b, q, ahead):
                    steps = prep(b + 1, 1 - q) if ahead else {}
                    for s in range(TPB):
                        i = b * TPB + s
                        r = ring(q, s)
                        pe.wait_ge(S["scaled_ready"], i + RESERVED + 1)
                        pe.wait_ge(S["copied"], i + 1)
                        for a in range(2):
                            M(p_part[r][:, a * P:(a + 1) * P], scaled[:, r, a * P:(a + 1) * P], window[:, r, :],
                              start=True, stop=True)
                        M(p_part[r][0:HEADS, 2 * P:3 * P], wt[q][:, HEADS * s:HEADS * s + HEADS], window[:, r, :],
                          start=True, stop=True).then_inc(S["mm_done"], 1)
                        if s in steps:
                            steps[s]()

                pe.sem_inc(S["mm_done"], RING)
                pe.sem_inc(S["scaled_ready"], RESERVED)
                pe.wait_ge(S["psum_zero"], ZEROED)
                for _, step in sorted(prep(0, 0).items()):
                    step()
                with pe.Fori(0, PAIRS - 1) as k:
                    batch(2 * k, 0, True)
                    batch(2 * k + 1, 1, True)
                batch(NB - 2, 0, True)
                batch(NB - 1, 1, False)


def end_of_layer(c, ctx, tag, block_bias):
    nc = c.nc

    def sb(name, shape):
        return ctx.enter_context(nc.sbuf_tensor(f"{name}_{tag}", shape, F32))

    flat = sb("flat", [P, NT * HEADS])
    inv_now = [sb(f"inv_now{i}", [HEADS, P]) for i in range(2)]
    avg = [sb(f"avg{i}", [P, 2, P]) for i in range(2)]
    hT = [sb(f"hT{i}", [P, 2, P]) for i in range(2)]
    p_inv = [ctx.enter_context(nc.psum_tensor(f"p_inv{i}_{tag}", [P, 512], F32)) for i in range(2)]
    moved, inv_ready, inv_picked, inv_done, avg_ready, hT_ready = sems(
        nc, ctx, *(f"{n}_{tag}" for n in ("moved", "inv_ready", "inv_picked", "inv_done", "avg_ready", "hT_ready")))

    def move_sums(sp):
        sums = c.acc[0:HEADS, 2, 0:NT * P]
        by_head, by_part = c.d["weight_sums"], c.d["weight_sums"].rearrange("h (a n) -> (h a) n", a=P // HEADS)
        sp.dma_start(by_head, sums).then_inc(moved, 16)
        sp.wait_ge(moved, 16)
        sp.dma_start(flat[:], by_part).then_inc(moved, 16)
        sp.wait_ge(inv_ready, 2)
        sp.dma_start(by_part, flat[:]).then_inc(moved, 16)
        sp.wait_ge(moved, 48)
        sp.dma_start(sums, by_head).then_inc(moved, 16)

    def invert(dve):
        dve.wait_ge(moved, 32)
        nc.vector.tensor_scalar(flat[:], flat[:], 1e-9, None, ALU.max).then_inc(inv_ready, 1)
        dve.wait_ge(inv_ready, 1)
        nc.vector.reciprocal(flat[:], flat[:]).then_inc(inv_ready, 1)

    def pick(act, j, q):
        if isinstance(j, int) and j == 0:
            act.wait_ge(moved, 64)
        nc.scalar.activation(inv_now[q][:], c.acc[0:HEADS, 2, bass.ds(j * P, P)], ACT.Copy).then_inc(inv_picked, 1)

    def spread(pe, j, q):
        pe.wait_ge(inv_picked, j + 1)
        for a in range(2):
            m = nc.tensor.matmul(p_inv[q][:, a * P:(a + 1) * P], c.head_rows[:, a * P:(a + 1) * P],
                                 inv_now[q][:], start=True, stop=True)
        m.then_inc(inv_done, 1)

    def average(dve, j, q):
        dve.wait_ge(inv_done, j + 1)
        nc.vector.tensor_tensor(avg[q][:], c.acc[:, 0:2, bass.ds(j * P, P)],
                                p_inv[q][:, 0:2 * P].rearrange("p (a n) -> p a n", a=2), ALU.mult).then_inc(avg_ready, 1)

    def relu(act, j, q):
        act.wait_ge(avg_ready, j + 1)
        for a in range(2):
            i = nc.scalar.activation(hT[q][:, a, :], avg[q][:, a, :], ACT.Relu,
                                     bias=c.gat_b[:, block_bias, a:a + 1])
        i.then_inc(hT_ready, 1)
    def ends(act):
        pick(act, 0, 0)
        with act.Fori(0, (NT - 1) // 2) as k:
            pick(act, 2 * k + 1, 1)
            relu(act, 2 * k, 0)
            pick(act, 2 * k + 2, 0)
            relu(act, 2 * k + 1, 1)
        relu(act, NT - 1, 0)
    return hT, hT_ready, move_sums, invert, spread, average, ends


def second_features(c):
    nc, d = c.nc, c.d
    with ExitStack() as ctx:
        fe = [ctx.enter_context(nc.sbuf_tensor(f"fe2_{i}", [P, ROW], F32)) for i in range(2)]
        start_i = [ctx.enter_context(nc.sbuf_tensor(f"start2_{i}", [P, 1], I32)) for i in range(2)]
        p_fe = [ctx.enter_context(nc.psum_tensor(f"p_fe2_{i}", [P, 512], F32)) for i in range(2)]
        hT, hT_ready, move_sums, invert, spread, average, ends = end_of_layer(c, ctx, "one", 0)
        stored = sems(nc, ctx, "fe2_stored0", "fe2_stored1")
        scattered = sems(nc, ctx, "er2_scattered0", "er2_scattered1")
        fe_done, fe_ready = sems(nc, ctx, "fe2_done", "fe2_ready")

        with nc.Block() as block:
            @block.sync
            def _(sp):
                def store(j, q):
                    sp.wait_ge(fe_ready, j + 1)
                    sp.dma_start(d["table2"][bass.ds(j * P, P), :], fe[q][:]).then_inc(stored[q], 16)
                move_sums(sp)
                over_tiles(sp, store)
                for q in range(2):
                    sp.wait_ge(stored[q], 16 * len(range(q, NT, 2)))

            @block.gpsimd
            def _(pool):
                def scatter(j, q, n=P):
                    pool.wait_ge(fe_ready, j + 1)
                    pool.nop(nofuse=True)
                    nc.gpsimd.indirect_dma_start(
                        out=d["er_start2"], out_offset=bass.IndirectOffsetOnAxis(ap=start_i[q][0:n, :], axis=0),
                        in_=fe[q][0:n, D + HEADS:ROW], in_offset=None).then_inc(scattered[q], 16)
                with pool.Fori(0, (NT - 1) // 2) as k:
                    scatter(2 * k, 0)
                    scatter(2 * k + 1, 1)
                scatter(NT - 1, 0, TAIL)
                for q in range(2):
                    pool.wait_ge(scattered[q], 16 * len(range(q, NT, 2)))

            @block.vector
            def _(dve):
                def features(j, q):
                    if not (isinstance(j, int) and j < 2):
                        dve.wait_ge(stored[q], (j - q) * 8)
                        dve.wait_ge(scattered[q], (j - q) * 8)
                    nc.vector.tensor_copy(start_i[q][:], c.start[:, bass.ds(j, 1)])
                    dve.wait_ge(fe_done, j + 1)
                    nc.vector.tensor_copy(fe[q][:], p_fe[q][:, 0:ROW]).then_inc(fe_ready, 1)

                def tile(j, q, ahead=True):
                    if ahead:
                        average(dve, j + 1, 1 - q)
                    features(j, q)
                invert(dve)
                average(dve, 0, 0)
                tile(0, 0)
                tile(1, 1)
                with dve.Fori(1, (NT - 1) // 2) as k:
                    tile(2 * k, 0)
                    tile(2 * k + 1, 1)
                tile(NT - 1, 0, ahead=False)

            @block.scalar
            def _(act):
                ends(act)

            @block.tensor
            def _(pe):
                def features(j, q):
                    pe.wait_ge(hT_ready, j + 1)
                    for k in range(2):
                        m = nc.tensor.matmul(p_fe[q][:, 0:ROW], hT[q][:, k, :], c.gext2[:, k, :], start=k == 0, stop=k == 1)
                    m.then_inc(fe_done, 1)
                spread(pe, 0, 0)
                with pe.Fori(0, (NT - 1) // 2) as k:
                    spread(pe, 2 * k + 1, 1)
                    features(2 * k, 0)
                    spread(pe, 2 * k + 2, 0)
                    features(2 * k + 1, 1)
                features(NT - 1, 0)


def join(c):
    nc, d = c.nc, c.d
    with ExitStack() as ctx:
        def two(name, shape):
            return [ctx.enter_context(nc.sbuf_tensor(f"{name}{i}", shape, F32)) for i in range(2)]

        x = two("jx", [P, D])
        x2 = two("jx2", [P, D])
        st = two("jst", [P, 8])
        p_h = [ctx.enter_context(nc.psum_tensor(f"p_h{i}", [P, 512], F32)) for i in range(2)]
        hT, hT_ready, move_sums, invert, spread, average, ends = end_of_layer(c, ctx, "two", 1)
        in_ = sems(nc, ctx, "jx_in0", "jx_in1")
        stored = sems(nc, ctx, "x2_stored0", "x2_stored1")
        h_done, x2_ready, stat, var_ready, kept, std_ready = sems(
            nc, ctx, "h_done", "x2_ready", "stat", "jvar_ready", "var_kept", "jstd_ready")

        with nc.Block() as block:
            @block.sync
            def _(sp):
                def load(j, q, n=P):
                    sp.dma_start(x[q][0:n, :], d["x"][bass.ds(j * P, n), :]).then_inc(in_[q], 16)

                def store(j, q):
                    sp.wait_ge(x2_ready, j + 1)
                    sp.dma_start(d["x2"][bass.ds(j * P, P), :], x2[q][:]).then_inc(stored[q], 16)

                load(0, 0)
                load(1, 1)
                move_sums(sp)
                with sp.Fori(0, (NT - 3) // 2) as k:
                    for q in range(2):
                        store(2 * k + q, q)
                        load(2 * k + 2 + q, q)
                store(NT - 3, 0)
                load(NT - 1, 0, TAIL)
                store(NT - 2, 1)
                store(NT - 1, 0)
                for q in range(2):
                    sp.wait_ge(stored[q], 16 * len(range(q, NT, 2)))

            @block.vector
            def _(dve):
                V = nc.vector

                def add(j, q):
                    s = st[q]
                    if not (isinstance(j, int) and j < 2):
                        dve.wait_ge(stored[q], (j - q) * 8)
                    dve.wait_ge(in_[q], (j - q) * 8 + 16)
                    dve.wait_ge(h_done, j + 1)
                    V.tensor_tensor(x2[q][:], p_h[q][:, 0:D], x[q][:], ALU.add).then_inc(x2_ready, 1)

                def variance(j, q):
                    s = st[q]
                    dve.wait_ge(x2_ready, j + 1)
                    V.bn_stats(s[:, 0:6], x2[q][:]).then_inc(stat, 1)
                    dve.wait_ge(stat, j + 1)
                    dve.nop(nofuse=True)
                    V.bn_aggr(s[:, 6:8], s[:, 0:6]).then_inc(var_ready, 1)
                    dve.wait_ge(var_ready, j + 1)
                    V.tensor_copy(c.mean[:, bass.ds(j, 1)], s[:, 6:7])
                    V.tensor_copy(c.rstd[:, bass.ds(j, 1)], s[:, 7:8]).then_inc(kept, 1)

                def tile(j, q, ahead=True):
                    add(j, q)
                    if ahead:
                        average(dve, j + 1, 1 - q)
                    variance(j, q)
                invert(dve)
                average(dve, 0, 0)
                tile(0, 0)
                tile(1, 1)
                with dve.Fori(1, (NT - 1) // 2) as k:
                    tile(2 * k, 0)
                    tile(2 * k + 1, 1)
                tile(NT - 1, 0, ahead=False)
                dve.wait_ge(std_ready, 1)
                V.reciprocal(c.rstd[:], c.rstd[:])

            @block.scalar
            def _(act):
                ends(act)
                act.wait_ge(kept, NT)
                nc.scalar.activation(c.rstd[:], c.rstd[:], ACT.Sqrt, bias=c.eps[:]).then_inc(std_ready, 1)

            @block.tensor
            def _(pe):
                def turn(j, q):
                    pe.wait_ge(hT_ready, j + 1)
                    for k in range(2):
                        t = nc.tensor.transpose(p_h[q][:, k * P:(k + 1) * P], hT[q][:, k, :], c.ident[:])
                    t.then_inc(h_done, 1)
                spread(pe, 0, 0)
                with pe.Fori(0, (NT - 1) // 2) as k:
                    spread(pe, 2 * k + 1, 1)
                    turn(2 * k, 0)
                    spread(pe, 2 * k + 2, 0)
                    turn(2 * k + 1, 1)
                turn(NT - 1, 0)


def slice_block(c):
    nc, d = c.nc, c.d
    with ExitStack() as ctx:
        def sb(name, shape, dt=F32):
            return ctx.enter_context(nc.sbuf_tensor(name, shape, dt))

        def two(name, shape):
            return [sb(f"{name}{i}", shape) for i in range(2)]

        x2 = sb("x2", [P, NT, D])
        swT = sb("swT", [P, 4, NT * P])
        vp = sb("vp", [P, 4, D])
        with ExitStack() as inner:
            ctx_outer, ctx_in = ctx, inner
            p_sum = [inner.enter_context(nc.psum_tensor(f"p_sum{i}", [P, 512], F32)) for i in range(4)]
            bank = [inner.enter_context(nc.psum_tensor(f"bank{i}", [P, 512], F32)) for i in range(4)]
            slice_weights(c, x2, swT, p_sum, bank)
            slice_attention(c, vp, p_sum, bank)
        output(c, x2, swT, vp)


def slice_weights(c, x2, swT, p_sum, bank):
    nc, d = c.nc, c.d
    with ExitStack() as ctx:
        def two(name, shape):
            return [ctx.enter_context(nc.sbuf_tensor(f"{name}{i}", shape, F32)) for i in range(2)]

        xn = [ctx.enter_context(nc.sbuf_tensor(f"sxn{i}", [P, D + 1], F32)) for i in range(4)]
        xnT = two("sxnT", [P, 2, P])
        logit = two("logit", [P, SH, SG])
        top = two("top", [P, SH])
        low = two("low", [P, SH, SG])
        ex = two("ex", [P, SH, SG])
        total = two("total", [P, SH])
        inv = two("sinv", [P, SH])
        sw = two("sw", [P, INNER])
        p_xT, p_l, p_t = bank[0], bank[1:3], bank[3]
        in_ = sems(nc, ctx, "x2_in0", "x2_in1")
        (ones, xn_ready, xT_done, xT_ready, l_done, logit_ready, top_ready, low_ready, ex_ready, total_ready, inv_ready,
         sw_ready, t_done, swT_ready) = sems(
            nc, ctx, "ones", "sxn_ready", "sxT_done", "sxT_ready", "l_done", "logit_ready", "top_ready", "low_ready",
            "ex_ready", "total_ready", "sinv_ready", "sw_ready", "t_done", "swT_ready")

        def wide(v):
            return v.unsqueeze(2).broadcast_to([P, SH, SG])

        with nc.Block() as block:
            @block.sync
            def _(sp):
                def load(j, q):
                    if not (isinstance(j, int) and j < 2):
                        sp.wait_ge(in_[q], (j - q) * 8)
                    sp.dma_start(x2[:, bass.ds(j, 1), :].rearrange("p a n -> p (a n)"),
                                 d["x2"][bass.ds(j * P, P), :]).then_inc(in_[q], 16)
                load(0, 0)
                load(1, 1)
                with sp.Fori(1, (NT - 1) // 2) as k:
                    load(2 * k, 0)
                    load(2 * k + 1, 1)
                load(NT - 1, 0)
                for q in range(2):
                    sp.wait_ge(in_[q], 16 * len(range(q, NT, 2)))

            @block.vector
            def _(dve):
                V = nc.vector

                def norm(j, r):
                    q = r % 2
                    dve.wait_ge(in_[q], (j - q) * 8 + 16)
                    V.tensor_scalar(xn[r][:, 0:D], x2[:, bass.ds(j, 1), :].rearrange("p a n -> p (a n)"),
                                    c.mean[:, bass.ds(j, 1)], c.rstd[:, bass.ds(j, 1)], ALU.subtract,
                                    ALU.mult).then_inc(xn_ready, 1)

                def biased(j, q):
                    dve.wait_ge(l_done, j + 1)
                    V.tensor_tensor(logit[q][:].rearrange("p h g -> p (h g)"), p_l[q][:], c.wc_bias[:],
                                    ALU.add).then_inc(logit_ready, 1)
                    dve.wait_ge(logit_ready, j + 1)
                    V.tensor_reduce(top[q][:], logit[q][:], AX.X, ALU.max).then_inc(top_ready, 1)

                def sums(j, q):
                    dve.wait_ge(ex_ready, j + 1)
                    V.tensor_reduce(total[q][:], ex[q][:], AX.X, ALU.add).then_inc(total_ready, 1)
                    dve.wait_ge(total_ready, j + 1)
                    V.reciprocal(inv[q][:], total[q][:]).then_inc(inv_ready, 1)

                def tile(j, r, ahead=4):
                    sums(j, r % 2)
                    if ahead > 3:
                        if not (isinstance(j, int) and j == 0):
                            dve.wait_ge(t_done, j)
                        norm(j + 3, (r + 3) % 4)
                    if ahead > 2:
                        biased(j + 2, r % 2)

                for r in range(4):
                    i = V.memset(xn[r][:, D:D + 1], 1.0)
                i.then_inc(ones, 1)
                for j in range(3):
                    norm(j, j)
                biased(0, 0)
                biased(1, 1)
                for j in range(4):
                    tile(j, j)
                with dve.Fori(1, NT // 4 - 1) as k:
                    for r in range(4):
                        tile(4 * k + r, r)
                for j in range(NT - 5, NT):
                    tile(j, j % 4, ahead=NT - j)

            @block.gpsimd
            def _(pool):
                def lower(j, q):
                    pool.wait_ge(top_ready, j + 1)
                    nc.gpsimd.tensor_tensor(low[q][:], logit[q][:], wide(top[q][:]), ALU.subtract).then_inc(low_ready, 1)

                def weigh(j, q):
                    pool.wait_ge(inv_ready, j + 1)
                    nc.gpsimd.tensor_tensor(sw[q][:].rearrange("p (h g) -> p h g", h=SH), ex[q][:], wide(inv[q][:]),
                                            ALU.mult).then_inc(sw_ready, 1)
                lower(0, 0)
                lower(1, 1)
                with pool.Fori(0, (NT - 3) // 2) as k:
                    for q in range(2):
                        weigh(2 * k + q, q)
                        lower(2 * k + q + 2, q)
                weigh(NT - 3, 0)
                lower(NT - 1, 0)
                weigh(NT - 2, 1)
                weigh(NT - 1, 0)

            @block.scalar
            def _(act):
                A = nc.scalar.activation

                def copy_x(j, q):
                    act.wait_ge(xT_done, j + 1)
                    A(xnT[q][:].rearrange("p k n -> p (k n)"), p_xT[:, 0:D], ACT.Copy).then_inc(xT_ready, 1)

                def exp(j, q):
                    act.wait_ge(low_ready, j + 1)
                    A(ex[q][:], low[q][:], ACT.Exp).then_inc(ex_ready, 1)

                def keep(j, q):
                    act.wait_ge(t_done, j + 1)
                    A(swT[:, :, bass.ds(j * P, P)], p_t[:].rearrange("p (k n) -> p k n", k=4),
                      ACT.Copy).then_inc(swT_ready, 1)

                def tile(j, q, ahead=4):
                    if ahead > 3:
                        copy_x(j + 3, 1 - q)
                    keep(j, q)
                    if ahead > 2:
                        exp(j + 2, q)
                for j in range(3):
                    copy_x(j, j % 2)
                exp(0, 0)
                exp(1, 1)
                with act.Fori(0, (NT - 3) // 2) as k:
                    tile(2 * k, 0)
                    tile(2 * k + 1, 1)
                for j in range(NT - 3, NT):
                    tile(j, j % 2, ahead=NT - j)

            @block.tensor
            def _(pe):
                M, T = nc.tensor.matmul, nc.tensor.transpose

                def turn_x(j, r):
                    pe.wait_ge(xn_ready, j + 1)
                    if not (isinstance(j, int) and j == 0):
                        pe.wait_ge(xT_ready, j)
                    for k in range(2):
                        t = T(p_xT[:, k * P:(k + 1) * P], xn[r][:, k * P:(k + 1) * P], c.ident[:])
                    t.then_inc(xT_done, 1)

                def logits(j, q):
                    pe.wait_ge(xT_ready, j + 1)
                    if not (isinstance(j, int) and j < 2):
                        pe.wait_ge(logit_ready, j - 1)
                    for k in range(2):
                        m = M(p_l[q][:], xnT[q][:, k, :], c.wc[:, k, :], start=k == 0, stop=k == 1)
                    m.then_inc(l_done, 1)

                def slices(j, r, first=False, last=False):
                    pe.wait_ge(sw_ready, j + 1)
                    q = r % 2
                    n = TAIL if last else P
                    for s in range(4):
                        M(p_sum[s][:, 0:D + 1], sw[q][0:n, s * P:(s + 1) * P], xn[r][0:n, :], start=first, stop=last)
                    if not first:
                        pe.wait_ge(swT_ready, j)
                    for s in range(4):
                        t = T(p_t[:, s * P:(s + 1) * P], sw[q][:, s * P:(s + 1) * P], c.ident[:])
                    t.then_inc(t_done, 1)

                def tile(j, r, ahead=4):
                    if ahead > 2:
                        logits(j + 2, r % 2)
                    if ahead > 3:
                        turn_x(j + 3, (r + 3) % 4)
                    slices(j, r, first=isinstance(j, int) and j == 0, last=ahead == 1)
                pe.wait_ge(ones, 1)
                turn_x(0, 0)
                turn_x(1, 1)
                logits(0, 0)
                turn_x(2, 2)
                logits(1, 1)
                for j in range(4):
                    tile(j, j)
                with pe.Fori(1, NT // 4 - 1) as k:
                    for r in range(4):
                        tile(4 * k + r, r)
                for j in range(NT - 5, NT):
                    tile(j, j % 4, ahead=NT - j)


def slice_attention(c, vp, p_sum, bank):
    nc, d = c.nc, c.d
    with ExitStack() as ctx:
        def sb(name, shape, dt=F32):
            return ctx.enter_context(nc.sbuf_tensor(name, shape, dt))

        wfx = sb("wfx", [P, 2, INNER])
        bfx = sb("bfx", [1, INNER])
        wq, wk, wv = (sb(n, [SD, SD]) for n in ("wq", "wk", "wv"))
        wo = sb("wo", [SD, SH, D])
        soft = sb("soft", [P, 4, 1])
        inv = sb("ainv", [P, 4, 1])
        mean = sb("amean", [P, 4, D + 1])
        meanT = sb("ameanT", [P, 2, INNER])
        share = sb("share", [1, INNER])
        tokT, qT, kT, v, lg, ex, pr, prT, oT = (sb(n, [SD, INNER]) for n in
                                                ("tokT", "qT", "kT", "v", "lg", "aex", "pr", "prT", "oT"))
        top, tot, itot = (sb(n, [SG, SH]) for n in ("atop", "atot", "aitot"))
        loaded, v_step, p_step, exp_done = sems(nc, ctx, "a_loaded", "a_v", "a_p", "a_exp")

        DV = ["soft", "inv", "mean", "meanT", "share", "tokT", "qT", "kT", "v", "top", "low", "tot", "itot", "pr",
              "prT", "oT", "vp"]
        PE = ["meanT", "tokT", "qT", "kT", "v", "lg", "prT", "oT", "vp"]

        def dv(n):
            return DV.index(n) + 1

        def pp(n):
            return PE.index(n) + 1

        def heads(t):
            return t[:].rearrange("p (h g) -> p h g", h=SH)

        with nc.Block() as block:
            @block.sync
            def _(sp):
                for k in range(2):
                    sp.dma_start(wfx[:, k, :], d["W_fx"][k * P:(k + 1) * P, :]).then_inc(loaded, 16)
                sp.dma_start(bfx[:], d["b_fx"].unsqueeze(0)).then_inc(loaded, 16)
                for t, n in ((wq, "W_q"), (wk, "W_k"), (wv, "W_v")):
                    sp.dma_start(t[:], d[n]).then_inc(loaded, 16)
                sp.dma_start(wo[:], d["W_out"].rearrange("(h c) n -> c h n", c=SD)).then_inc(loaded, 16)

            @block.vector
            def _(dve):
                V = nc.vector

                def step(name, ins):
                    ins.then_inc(v_step, 1)
                    dve.wait_ge(v_step, dv(name))

                for s in range(4):
                    i = V.tensor_scalar(soft[:, s, :], p_sum[s][:, D:D + 1], 1e-5, None, ALU.add)
                step("soft", i)
                step("inv", V.reciprocal(inv[:, :, 0], soft[:, :, 0]))
                for s in range(4):
                    i = V.tensor_scalar(mean[:, s, :], p_sum[s][:, 0:D + 1], inv[:, s, :], None, ALU.mult)
                step("mean", i)
                dve.wait_ge(p_step, pp("meanT"))
                V.tensor_copy(meanT[:, 0, :], bank[0][:])
                step("meanT", V.tensor_copy(meanT[:, 1, :], bank[1][:]))
                step("share", V.tensor_copy(share[:], bank[2][0:1, :]))
                for name, t, b in (("tokT", tokT, 3), ("qT", qT, 0), ("kT", kT, 1), ("v", v, 2)):
                    dve.wait_ge(p_step, pp(name))
                    step(name, V.tensor_copy(t[:], bank[b][0:SD, :]))
                dve.wait_ge(p_step, pp("lg"))
                step("top", V.tensor_reduce(top[:], bank[3][0:SD, :].rearrange("p (h g) -> p h g", h=SH), AX.X, ALU.max))
                step("low", V.tensor_tensor(heads(lg), bank[3][0:SD, :].rearrange("p (h g) -> p h g", h=SH),
                                            top[:].unsqueeze(2).broadcast_to([SG, SH, SG]), ALU.subtract))
                dve.wait_ge(exp_done, 1)
                step("tot", V.tensor_reduce(tot[:], heads(ex), AX.X, ALU.add))
                step("itot", V.reciprocal(itot[:], tot[:]))
                step("pr", V.tensor_tensor(heads(pr), heads(ex), itot[:].unsqueeze(2).broadcast_to([SG, SH, SG]), ALU.mult))
                dve.wait_ge(p_step, pp("prT"))
                step("prT", V.tensor_copy(prT[:], bank[0][0:SD, :]))
                dve.wait_ge(p_step, pp("oT"))
                step("oT", V.tensor_copy(oT[:], bank[1][0:SD, :]))
                dve.wait_ge(p_step, pp("vp"))
                for h in range(SH):
                    i = V.tensor_copy(vp[64 * (h % 2):64 * (h % 2) + 64, h // 2, :],
                                      p_sum[h // 2][0:SG, (h % 2) * D:(h % 2 + 1) * D])
                step("vp", i)

            @block.scalar
            def _(act):
                act.wait_ge(v_step, dv("low"))
                nc.scalar.activation(ex[:], lg[:], ACT.Exp, scale=float(SD) ** -0.5).then_inc(exp_done, 1)

            @block.tensor
            def _(pe):
                M, T = nc.tensor.matmul, nc.tensor.transpose
                at = [slice(h * SG, (h + 1) * SG) for h in range(SH)]
                pe.wait_ge(v_step, dv("mean"))
                for s in range(4):
                    for k in range(2):
                        T(bank[k][:, s * P:(s + 1) * P], mean[:, s, k * P:(k + 1) * P], c.ident[:])
                    i = T(bank[2][0:1, s * P:(s + 1) * P], mean[:, s, D:D + 1], c.ident[:])
                i.then_inc(p_step, 1)
                pe.wait_ge(loaded, 16 * 7)
                pe.wait_ge(v_step, dv("share"))
                for h in range(SH):
                    for k in range(2):
                        M(bank[3][0:SD, at[h]], wfx[:, k, at[h]], meanT[:, k, at[h]], start=k == 0, stop=False)
                    i = M(bank[3][0:SD, at[h]], bfx[:, at[h]], share[:, at[h]], start=False, stop=True)
                i.then_inc(p_step, 1)
                pe.wait_ge(v_step, dv("tokT"))
                M(bank[0][0:SD, :], wq[:], tokT[:], start=True, stop=True).then_inc(p_step, 1)
                M(bank[1][0:SD, :], wk[:], tokT[:], start=True, stop=True).then_inc(p_step, 1)
                for h in range(SH):
                    i = M(bank[2][0:SG, at[h]], tokT[:, at[h]], wv[:], start=True, stop=True)
                i.then_inc(p_step, 1)
                pe.wait_ge(v_step, dv("kT"))
                for h in range(SH):
                    i = M(bank[3][0:SG, at[h]], qT[:, at[h]], kT[:, at[h]], start=True, stop=True)
                i.then_inc(p_step, 1)
                pe.wait_ge(v_step, dv("pr"))
                for h in range(SH):
                    i = T(bank[0][0:SG, at[h]], pr[:, at[h]], c.ident[0:SG, 0:SG])
                i.then_inc(p_step, 1)
                pe.wait_ge(v_step, dv("prT"))
                for h in range(SH):
                    i = M(bank[1][0:SD, at[h]], v[:, at[h]], prT[:, at[h]], start=True, stop=True)
                i.then_inc(p_step, 1)
                pe.wait_ge(v_step, dv("oT"))
                for h in range(SH):
                    i = M(p_sum[h // 2][0:SG, (h % 2) * D:(h % 2 + 1) * D], oT[:, at[h]], wo[:, h, :], start=True, stop=True)
                i.then_inc(p_step, 1)


def output(c, x2, swT, vp):
    nc, d = c.nc, c.d
    with ExitStack() as ctx:
        def two(name, shape):
            return [ctx.enter_context(nc.sbuf_tensor(f"{name}{i}", shape, F32)) for i in range(2)]

        w = two("w_now", [P, 4, P])
        xb = two("xb", [P, D])
        y = two("y", [P, D])
        p_y = [ctx.enter_context(nc.psum_tensor(f"p_y{i}", [P, 512], F32)) for i in range(2)]
        w_ready, xb_ready, y_done, y_ready = sems(nc, ctx, "w_now_ready", "xb_ready", "y_done", "y_ready")
        stored = sems(nc, ctx, "y_stored0", "y_stored1")
        with nc.Block() as block:
            @block.scalar
            def _(act):
                def copy(j, q):
                    if not (isinstance(j, int) and j < 2):
                        act.wait_ge(y_done, j - 1)
                    nc.scalar.activation(w[q][:], swT[:, :, bass.ds(j * P, P)], ACT.Copy).then_inc(w_ready, 1)
                copy(0, 0)
                copy(1, 1)
                with act.Fori(1, (NT - 1) // 2) as k:
                    copy(2 * k, 0)
                    copy(2 * k + 1, 1)
                copy(NT - 1, 0)

            @block.gpsimd
            def _(pool):
                def add(j, q):
                    if not (isinstance(j, int) and j < 2):
                        pool.wait_ge(y_ready, j - 1)
                    nc.gpsimd.tensor_tensor(xb[q][:], x2[:, bass.ds(j, 1), :].rearrange("p a n -> p (a n)"), c.b_out[:],
                                            ALU.add).then_inc(xb_ready, 1)
                add(0, 0)
                add(1, 1)
                with pool.Fori(1, (NT - 1) // 2) as k:
                    add(2 * k, 0)
                    add(2 * k + 1, 1)
                add(NT - 1, 0)

            @block.tensor
            def _(pe):
                def mm(j, q):
                    pe.wait_ge(w_ready, j + 1)
                    if not (isinstance(j, int) and j < 2):
                        pe.wait_ge(y_ready, j - 1)
                    for s in range(4):
                        m = nc.tensor.matmul(p_y[q][:, 0:D], w[q][:, s, :], vp[:, s, :], start=s == 0, stop=s == 3)
                    m.then_inc(y_done, 1)
                mm(0, 0)
                mm(1, 1)
                with pe.Fori(1, (NT - 1) // 2) as k:
                    mm(2 * k, 0)
                    mm(2 * k + 1, 1)
                mm(NT - 1, 0)

            @block.vector
            def _(dve):
                def add(j, q):
                    if not (isinstance(j, int) and j < 2):
                        dve.wait_ge(stored[q], (j - q) * 8)
                    dve.wait_ge(xb_ready, j + 1)
                    dve.wait_ge(y_done, j + 1)
                    nc.vector.tensor_tensor(y[q][:], p_y[q][:, 0:D], xb[q][:], ALU.add).then_inc(y_ready, 1)
                add(0, 0)
                add(1, 1)
                with dve.Fori(1, (NT - 1) // 2) as k:
                    add(2 * k, 0)
                    add(2 * k + 1, 1)
                add(NT - 1, 0)

            @block.sync
            def _(sp):
                def store(j, q, n=P):
                    sp.wait_ge(y_ready, j + 1)
                    sp.dma_start(d["out"][bass.ds(j * P, n), :], y[q][0:n, :]).then_inc(stored[q], 16)
                with sp.Fori(0, (NT - 1) // 2) as k:
                    store(2 * k, 0)
                    store(2 * k + 1, 1)
                store(NT - 1, 0, TAIL)
                for q in range(2):
                    sp.wait_ge(stored[q], 16 * len(range(q, NT, 2)))


def build(nc, dram):
    with ExitStack() as ctx:
        c = Core(nc, ctx, dram)
        seq = dram["dst_seq"]
        dram["dst_over"] = bass.AP(seq.tensor, seq.offset, [[P, ET], [1, P + 2]])
        c.ident = c.sb("ident", [P, P])
        c.iota = c.sb("iota", [P, P])
        c.eps = c.sb("eps", [P, 1])
        c.wc = c.sb("wc", [P, 2, INNER])
        c.wc_bias = c.sb("wc_bias", [P, INNER])
        c.inv_temp = c.sb("inv_temp", [P, SH])
        c.b_out = c.sb("b_out", [P, D])
        c.mean = c.sb("mean", [P, NT])
        c.rstd = c.sb("rstd", [P, NT])
        c.start = c.sb("start", [P, NT])
        with ExitStack() as gnn:
            c.ctx = gnn
            c.idx = c.sb("idx", [P, ET], I32)
            c.rel = c.sb("rel", [P, ET])
            c.base = c.sb("base", [1, ET], I32)
            c.not_start = c.sb("not_start", [P, EPP])
            c.go_on = c.sb("go_on", [HEADS, ET])
            c.pass_on = c.sb("pass_on", [HEADS, ET])
            c.is_head = c.sb("is_head", [P, HEADS])
            c.is_tile = c.sb("is_tile", [P, TPB])
            c.to_rows = c.sb("to_rows", [P, 3, P])
            c.head_rows = c.sb("head_rows", [HEADS, D])
            c.head_parts = c.sb("head_parts", [HEADS, BP])
            c.gext2 = c.sb("gext2", [P, 2, ROW])
            c.gat_b = c.sb("gat_b", [P, 2, 2])
            with ExitStack() as enc:
                c.ctx = enc
                c.w1a = c.sb("w1a", [P, 2, FF])
                c.label_rows = c.sb("label_rows", [96, FF], BF16)
                c.klass = c.sb("klass", [P, 1])
                c.fused = c.sb("fused", [P, 8, ROW])
                c.bias1 = c.sb("bias1", [P, ROW])
                c.ln_g = c.sb("ln_g", [P, 8])
                c.ln_b = c.sb("ln_b", [P, 8])
                c.nid = c.sb("nid", [P, NT])
                c.base_bc = c.sb("base_bc", [P, ET])
                constants_and_weights(c)
                encode(c)
            c.ctx = gnn
            c.acc = c.sb("acc", [P, 3, NW])
            edges(c, 1)
            second_features(c)
            edges(c, 2)
            join(c)
        slice_block(c)


_GNN = ["emb", "le_W1", "le_b1", "ln_g", "ln_b", "le_W2", "le_b2", "W1", "al1", "ar1", "b1", "W2", "al2", "ar2", "b2"]
_FFN = ["W_fx", "b_fx", "W_x", "b_x", "W_slice", "b_slice", "W_q", "W_k", "W_v", "W_out", "b_out", "temperature"]
_OUT_OF_PLACE = {"emb": "embT", "le_W1": "le_W1T", "W_x": "W_xT"}


def kernel(**inputs):
    import numpy as np
    import concourse.bacc as bacc
    from concourse.bass_utils import run_bass_kernel_spmd

    pad = EP - E
    src, dst = np.asarray(inputs["src"]), np.asarray(inputs["dst"])
    arrays = {
        "x": inputs["x"],
        "src": np.concatenate([src, np.zeros(pad, src.dtype)]).reshape(ET, P),
        "dst": np.concatenate([dst, np.full(pad, N, dst.dtype)]).reshape(ET, P),
        "dst_seq": np.concatenate([np.full(1, -1, dst.dtype), dst, np.full(pad + 1, N, dst.dtype)]),
        "labels": np.concatenate([np.asarray(inputs["node_type_24"]), np.zeros(NT * P - N, np.int32)]),
    }
    for n in _GNN:
        arrays[_OUT_OF_PLACE.get(n, n)] = np.asarray(inputs["L0_gnn_" + n])
    for n in _FFN:
        arrays[_OUT_OF_PLACE.get(n, n)] = np.asarray(inputs["L0_ffn_" + n])
    for n in _OUT_OF_PLACE.values():
        arrays[n] = arrays[n].T
    arrays["W1T"], arrays["W2T"] = arrays["W1"].T, arrays["W2"].T
    arrays["temperature"] = arrays["temperature"].reshape(-1)
    arrays = {f"in_{n}": np.ascontiguousarray(a) for n, a in arrays.items()}

    nc = bacc.Bacc("TRN2", target_bir_lowering=False, num_devices=1)
    dram = {n[3:]: nc.dram_tensor(n, a.shape, mybir.dt.from_np(a.dtype), kind="ExternalInput").ap()
            for n, a in arrays.items()}
    for i in (1, 2):
        dram[f"table{i}"] = nc.dram_tensor(f"table{i}", [NT * P, ROW], F32, kind="Internal").ap()
        dram[f"er_start{i}"] = nc.dram_tensor(f"er_start{i}", [EP, HEADS], F32, kind="Internal").ap()
        dram[f"er_edge{i}"] = nc.dram_tensor(f"er_edge{i}", [HEADS, EP], F32, kind="Internal").ap()
    dram["weight_sums"] = nc.dram_tensor("weight_sums", [HEADS, NT * P], F32, kind="Internal").ap()
    dram["x2"] = nc.dram_tensor("x2_rows", [NT * P, D], F32, kind="Internal").ap()
    dram["out"] = nc.dram_tensor("out_0", [N, D], F32, kind="ExternalOutput").ap()
    build(nc, dram)
    return run_bass_kernel_spmd(nc, [arrays], core_ids=[0]).results[0]["out_0"]
```

```python
from contextlib import ExitStack

import concourse.bass as bass
from concourse import mybir

ALU = mybir.AluOpType
ACT = mybir.ActivationFunctionType
AX = mybir.AxisListType
F32 = mybir.dt.float32
BF16 = mybir.dt.bfloat16
I32 = mybir.dt.int32
DVE_ONLY = (mybir.EngineType.DVE,)
ACT_ONLY = (mybir.EngineType.Activation,)

P = 128
N, E, D = 6250, 106250, 256
HEADS, HID = 4, 64
CLASSES = 24
FF = 1024
NT = -(-N // P)
TAIL = N - (NT - 1) * P
TPB = 26
BP = TPB * HEADS
ET = 832
EP = ET * P
NB = ET // TPB
PAIRS = NB // 2
EPP = EP // P
ROW = D + 2 * HEADS
NW = NT * P + P
BIG = 1e30
LN_EPS = 1e-5
SLOPE = 0.2
RING = 4
SH, SD, SG = 8, 64, 64
INNER = SH * SD
RESERVED = 2 * TPB


class Core:

    def __init__(self, nc, ctx, dram):
        self.nc, self.ctx, self.d = nc, ctx, dram

    def sem(self, name):
        return self.ctx.enter_context(self.nc.semaphore(name))

    def sb(self, name, shape, dt=F32):
        return self.ctx.enter_context(self.nc.sbuf_tensor(name, shape, dt))


def sems(nc, ctx, *names):
    return [ctx.enter_context(nc.semaphore(n)) for n in names]


def known_below(j, n):
    return isinstance(j, int) and j < n


def a_tile(j):
    return not isinstance(j, int) or 0 <= j < NT


def staggered(eng, step):
    for j in range(-4, 1):
        step(j, j % 4)
    with eng.Fori(0, (NT - 5) // 4) as k:
        for r in range(1, 5):
            step(4 * k + r, r % 4)
    for j in range(NT - 4, NT):
        step(j, j % 4)


def by_four(eng, step):
    with eng.Fori(0, NT // 4) as k:
        for r in range(4):
            step(4 * k + r, r)
    step(NT - 1, 0)


def bcast_rows(ap, parts, n):
    return bass.AP(ap.tensor, ap.offset, [[0, parts], [1, n]])


def constants_and_weights(c):
    nc, d = c.nc, c.d
    with ExitStack() as ctx:
        def sb(name, shape, dt=F32):
            return ctx.enter_context(nc.sbuf_tensor(name, shape, dt))

        emb3 = sb("emb3", [P, 2, 3, 32])
        w1b = sb("w1b", [P, 2, FF])
        b1_bc = sb("b1_bc", [96, FF])
        table = sb("table", [96, FF])
        rest = sb("rest", [96, FF])
        parts = sb("parts", [96, 3, FF], BF16)
        gw = [sb(f"gw{i}", [P, 2, D]) for i in range(2)]
        attn = [sb(f"attn{i}", [P, 2, 2 * HEADS]) for i in range(2)]
        gext1 = sb("gext1", [P, 2, ROW])
        le2 = sb("le2", [P, 2, FF])
        le2_b = sb("le2_b", [P, 2])
        le2_bw = sb("le2_bw", [P, 2, P])
        wxT = sb("wxT", [SD, SH, D])
        wsl = sb("wsl", [SD, SG])
        bx = sb("bx", [SD, SH])
        bx_w = sb("bx_w", [SD, SH, P])
        bsl = sb("bsl", [P, SG])
        temp = sb("temp", [P, SH])
        src_i = sb("src_i", [P, 7, P], I32)
        dst_i = sb("dst_i", [P, 7, P], I32)
        src_f = sb("src_f", [P, 7, P])
        dst_f = sb("dst_f", [P, 7, P])
        rel_f = sb("rel_f", [P, 7, P])
        base_f = sb("base_f", [1, ET])
        ends = sb("ends", [HEADS, 3, ET], I32)
        same = sb("same", [HEADS, 3, ET])
        one_row = sb("one_row", [1, P])
        iota_i = sb("iota_i", [P, P], I32)
        nid_i = sb("nid_i", [P, NT + 1], I32)
        seq = sb("seq", [P, EPP + 1], I32)
        zeros = sb("zeros", [P, 2048])
        pm = [ctx.enter_context(nc.psum_tensor(f"pm{i}", [P, 512], F32)) for i in range(8)]

        (loaded, weights_in, attn_in, emb_in, pool_done, v_step, p_step, a_step, zeroed) = sems(
            nc, ctx, "loaded", "weights_in", "attn_in", "emb_in", "pool_done", "v_step", "p_step", "a_step", "zeroed")
        n_loaded, n_weights = [0], [0]
        v_at = {}

        PE = ["table", "attn1", "attn2", "fused0", "fused1", "fused2", "fused3", "fused4", "fused5", "fused6",
              "fused7", "bias1", "slices0", "slices1", "slice_bias", "base"] + [f"idx{g}" for g in range(7)]
        pe_at = {n: i + 1 for i, n in enumerate(PE)}

        with nc.Block() as block:
            @block.sync
            def _(sp):
                def weight(dst, src):
                    sp.dma_start(dst, src).then_inc(weights_in, 16)
                    n_weights[0] += 16

                def load(dst, src):
                    sp.dma_start(dst, src).then_inc(loaded, 16)
                    n_loaded[0] += 16

                with nc.allow_non_contiguous_dma(reason="short vectors"):
                    for k in range(2):
                        weight(w1b[:, k, :], d["le_W1T"][D + k * P:D + (k + 1) * P, :])
                    weight(b1_bc[:], bcast_rows(d["le_b1"], 96, FF))
                    for k in range(2):
                        for i in range(2):
                            weight(gw[i][:, k, :], d[f"W{i + 1}"][k * P:(k + 1) * P, :])
                            weight((gext1, c.gext2)[i][:, k, 0:D], d[f"W{i + 1}T"][k * P:(k + 1) * P, :])
                        weight(le2[:, k, :], d["le_W2"][k * P:(k + 1) * P, :])
                    weight(le2_b[:], d["le_b2"].rearrange("(k p) -> p k", p=P))
                    for k in range(2):
                        load(c.w1a[:, k, :], d["le_W1T"][k * P:(k + 1) * P, :])
                    load(c.ln_g[:], d["ln_g"].rearrange("(k p) -> p k", p=P))
                    load(c.ln_b[:], d["ln_b"].rearrange("(k p) -> p k", p=P))
                    for i in range(2):
                        load(c.gat_b[:, i, :], d[f"b{i + 1}"].rearrange("(k p) -> p k", p=P))
                    load(wxT[:], d["W_xT"].rearrange("(h c) n -> c h n", c=SD))
                    load(wsl[:], d["W_slice"])
                    load(bx[:], d["b_x"].rearrange("(h c) -> c h", c=SD))
                    load(bsl[:], bcast_rows(d["b_slice"], P, SG))
                    load(temp[:], bcast_rows(d["temperature"], P, SH))
                    load(c.b_out[:], bcast_rows(d["b_out"], P, D))
                    for g in range(7):
                        rows = min(P, ET - g * P)
                        load(src_i[0:rows, g, :], d["src"][g * P:g * P + rows, :])
                        load(dst_i[0:rows, g, :], d["dst"][g * P:g * P + rows, :])
                    dst_at = d["dst_seq"]
                    load(c.base[:], bass.AP(dst_at.tensor, dst_at.offset + 1, [[0, 1], [P, ET]]))
                    for i, at in enumerate((1, 0, P)):
                        load(ends[:, i, :], bass.AP(dst_at.tensor, dst_at.offset + at, [[0, HEADS], [P, ET]]))
                    load(c.first_id[:], bass.AP(dst_at.tensor, dst_at.offset + 1, [[EPP, P], [1, 1]]))
                    load(seq[:], bass.AP(dst_at.tensor, dst_at.offset, [[EPP, P], [1, EPP + 1]]))
                sp.wait_ge(v_step, 1)
                flat = EP * HEADS // P
                for e in (d["er_start1"], d["er_start2"]):
                    v = e.rearrange("(p a) h -> p (a h)", p=P)
                    for o in range(0, flat, 2048):
                        w = min(2048, flat - o)
                        sp.dma_start(v[:, o:o + w], zeros[:, 0:w]).then_inc(zeroed, 16)
                sp.wait_ge(zeroed, 16 * 2 * -(-flat // 2048))

            @block.scalar
            def _(act):
                with nc.allow_non_contiguous_dma(reason="short vectors"):
                    act.wait_ge(pool_done, 2)
                    for i in range(2):
                        for h in range(HEADS):
                            for j, a in enumerate(("al", "ar")):
                                lo = HID * (h % 2)
                                act.dma_start(attn[i][lo:lo + HID, h // 2, j * HEADS + h:j * HEADS + h + 1],
                                             d[f"{a}{i + 1}"][h, :].rearrange("(p o) -> p o", o=1)).then_inc(attn_in, 16)
                A = nc.scalar.activation
                for k in range(8):
                    act.wait_ge(p_step, pe_at[f"fused{k}"])
                    A(c.fused[:, k, :], pm[4 + k % 2][:, 0:ROW], ACT.Copy).then_inc(a_step, 1)
                act.wait_ge(p_step, pe_at["bias1"])
                A(c.bias1[:], pm[6][:, 0:ROW], ACT.Copy).then_inc(a_step, 1)
                act.wait_ge(p_step, pe_at["base"])
                A(c.base_bc[:, 0:512], pm[2][:], ACT.Copy)
                A(c.base_bc[:, 512:ET], pm[3][:, 0:ET - 512], ACT.Copy)

            @block.gpsimd
            def _(pool):
                nc.gpsimd.memset(emb3[:], 0.0).then_inc(pool_done, 1)
                nc.gpsimd.memset(attn[0][:], 0.0)
                nc.gpsimd.memset(attn[1][:], 0.0).then_inc(pool_done, 1)
                nc.gpsimd.memset(c.ident[:], 0.0).then_inc(pool_done, 1)
                pool.wait_ge(pool_done, 3)
                nc.gpsimd.affine_select(out=c.ident[:], in_=c.ident[:], compare_op=ALU.not_equal, fill=1.0, base=0,
                                        pattern=[[-1, P]], channel_multiplier=1).then_inc(pool_done, 1)
                nc.gpsimd.iota(iota_i[:], [[1, P]], base=0, channel_multiplier=0).then_inc(pool_done, 1)
                nc.gpsimd.iota(nid_i[:], [[P, NT + 1]], base=0, channel_multiplier=1).then_inc(pool_done, 1)
                with nc.allow_non_contiguous_dma(reason="short rows"):
                    for k in range(2):
                        for r in range(3):
                            pool.dma_start(emb3[:, k, r, 0:CLASSES], d["embT"][k * P:(k + 1) * P, :]).then_inc(emb_in, 16)

            @block.vector
            def _(dve):
                n = [0]

                def link(ins):
                    n[0] += 1
                    ins.then_inc(v_step, 1)
                    dve.wait_ge(v_step, n[0])

                V = nc.vector
                link(V.memset(zeros[:], 0.0))
                V.memset(c.eps[:], LN_EPS)
                V.memset(one_row[:], 1.0).then_inc(v_step, 1)
                n[0] += 1
                dve.wait_ge(pool_done, 6)
                link(V.tensor_copy(c.iota[:], iota_i[:]))
                link(V.tensor_copy(c.nid[:], nid_i[:, 0:NT]))
                link(V.tensor_copy(c.klass[:, 0:1], nid_i[:, 0:1]))
                for r in range(1, 3):
                    link(V.tensor_scalar(c.klass[32 * r:32 * r + 32, :], c.klass[32 * r:32 * r + 32, :], -32.0 * r,
                                         None, ALU.add))
                link(V.tensor_reduce(c.is_head[:], c.ident[:].rearrange("p (t h) -> p h t", h=HEADS), AX.X, ALU.add))
                link(V.tensor_reduce(c.is_tile[:], c.ident[:, 0:BP].rearrange("p (t h) -> p t h", h=HEADS), AX.X, ALU.add))
                link(V.memset(c.to_rows[:], 0.0))
                link(V.tensor_copy(c.to_rows[:, 0:2, :].rearrange("p a (b f) -> p (a b) f", b=2),
                                   c.is_head[:].unsqueeze(2).broadcast_to([P, HEADS, HID])))
                link(V.tensor_copy(c.to_rows[:, 2, 0:HEADS], c.is_head[:]))
                link(V.tensor_copy(c.head_rows[:].rearrange("p (h f) -> p h f", h=HEADS),
                                   c.ident[0:HEADS, 0:HEADS].unsqueeze(2).broadcast_to([HEADS, HEADS, HID])))
                link(V.tensor_copy(c.head_parts[:].rearrange("p (t h) -> p t h", h=HEADS),
                                   c.ident[0:HEADS, 0:HEADS].unsqueeze(1).broadcast_to([HEADS, TPB, HEADS])))
                v_at["consts"] = n[0]
                dve.wait_ge(weights_in, n_weights[0])
                link(V.tensor_copy(le2_bw[:], le2_b[:].unsqueeze(2).broadcast_to([P, 2, P])))
                for i, g in enumerate((gext1, c.gext2)):
                    dve.wait_ge(p_step, pe_at[f"attn{i + 1}"])
                    link(V.tensor_copy(g[:, :, D:ROW],
                                       pm[2 + i][:, 0:16].rearrange("p (k a) -> p k a", k=2)))
                    v_at[f"gext{i + 1}"] = n[0]
                dve.wait_ge(p_step, pe_at["table"])
                for h in range(2):
                    link(V.tensor_tensor(table[:, h * 512:(h + 1) * 512], pm[h][0:96, :],
                                         b1_bc[:, h * 512:(h + 1) * 512], ALU.add))
                link(V.tensor_copy(parts[:, 0, :], table[:]))
                link(V.tensor_tensor(rest[:], table[:], parts[:, 0, :], ALU.subtract))
                link(V.tensor_copy(parts[:, 1, :], rest[:]))
                link(V.tensor_tensor(table[:], rest[:], parts[:, 1, :], ALU.subtract))
                link(V.tensor_copy(parts[:, 2, :], table[:]))
                for rr in range(3):
                    link(V.tensor_copy(c.label_rows[32 * rr:32 * rr + 32, :], parts[32 * rr:32 * rr + 32, rr, :]))
                dve.wait_ge(loaded, n_loaded[0])
                link(V.tensor_copy(bx_w[:], bx[:].unsqueeze(2).broadcast_to([SD, SH, P])))
                link(V.tensor_copy(base_f[:], c.base[:]))
                v_at["base"] = n[0]
                for g in range(7):
                    rows = min(P, ET - g * P)
                    link(V.tensor_copy(src_f[0:rows, g, :], src_i[0:rows, g, :]))
                    link(V.tensor_copy(dst_f[0:rows, g, :], dst_i[0:rows, g, :]))
                    link(V.tensor_scalar(rel_f[0:rows, g, :], dst_f[0:rows, g, :], dst_f[0:rows, g, 0:1], None,
                                         ALU.subtract))
                    v_at[f"rel{g}"] = n[0]
                link(V.tensor_tensor(same[:, 0, :], ends[:, 0, :], ends[:, 1, :], ALU.is_equal))
                link(V.tensor_tensor(same[:, 1, :], ends[:, 0, :], ends[:, 2, :], ALU.is_equal))
                link(V.tensor_tensor(same[:, 2, :], same[:, 0, :], same[:, 1, :], ALU.mult))
                link(V.tensor_scalar(c.go_on[:], same[:, 0, :], -1.0, BIG, ALU.add, ALU.mult))
                link(V.tensor_scalar(c.pass_on[:], same[:, 2, :], -1.0, BIG, ALU.add, ALU.mult))
                link(V.tensor_tensor(c.not_start[:], seq[:, 1:EPP + 1], seq[:, 0:EPP], ALU.is_equal))
                link(V.tensor_scalar(temp[:], temp[:], 0.1, 5.0, ALU.max, ALU.min))
                link(V.reciprocal(c.inv_temp[:], temp[:]))
                inv = c.inv_temp[:].unsqueeze(2).broadcast_to([P, SH, SG])
                for k in range(2):
                    dve.wait_ge(p_step, pe_at[f"slices{k}"])
                    link(V.tensor_tensor(c.wc[:, k, :].rearrange("p (h g) -> p h g", h=SH),
                                         pm[k][:].rearrange("p (h g) -> p h g", h=SH), inv, ALU.mult))
                dve.wait_ge(p_step, pe_at["slice_bias"])
                cb = c.wc_bias[:].rearrange("p (h g) -> p h g", h=SH)
                link(V.tensor_tensor(cb, pm[7][:].rearrange("p (h g) -> p h g", h=SH),
                                     bsl[:].unsqueeze(1).broadcast_to([P, SH, SG]), ALU.add))
                link(V.tensor_tensor(cb, cb, inv, ALU.mult))
                for g in range(7):
                    rows = min(P, ET - g * P)
                    dve.wait_ge(p_step, pe_at[f"idx{g}"])
                    q = pm[4 + g % 2]
                    link(V.tensor_copy(c.idx[:, g * P:g * P + rows], q[:, 0:rows]))
                    link(V.tensor_copy(c.rel[:, g * P:g * P + rows], q[:, 256:256 + rows]))
                    v_at[f"idx{g}"] = n[0]

            @block.tensor
            def _(pe):
                M, T = nc.tensor.matmul, nc.tensor.transpose

                def done(ins):
                    ins.then_inc(p_step, 1)

                pe.wait_ge(emb_in, 16 * 6)
                pe.wait_ge(weights_in, n_weights[0])
                pe.wait_ge(v_step, v_at["consts"])
                for h in range(2):
                    for k in range(2):
                        m = M(pm[h][0:96, :], emb3[:, k].rearrange("p r q -> p (r q)"), w1b[:, k, h * 512:(h + 1) * 512],
                              start=k == 0, stop=k == 1)
                done(m)
                pe.wait_ge(attn_in, 16 * 16)
                for i in range(2):
                    for k in range(2):
                        for o in range(2):
                            m = M(pm[2 + i][:, 8 * k:8 * k + 8], gw[i][:, o, k * P:(k + 1) * P], attn[i][:, o, :],
                                  start=o == 0, stop=o == 1)
                    done(m)
                pe.wait_ge(v_step, v_at["gext1"])
                for k in range(8):
                    if k >= 2:
                        pe.wait_ge(a_step, k - 1)
                    for cc in range(2):
                        m = M(pm[4 + k % 2][:, 0:ROW], le2[:, cc, k * P:(k + 1) * P], gext1[:, cc, :],
                              start=cc == 0, stop=cc == 1)
                    done(m)
                for cc in range(2):
                    m = M(pm[6][:, 0:ROW], le2_bw[:, cc, :], gext1[:, cc, :], start=cc == 0, stop=cc == 1)
                done(m)
                pe.wait_ge(loaded, n_loaded[0])
                pe.wait_ge(v_step, v_at["base"])
                for k in range(2):
                    for h in range(SH):
                        m = M(pm[k][:, h * SG:(h + 1) * SG], wxT[:, h, k * P:(k + 1) * P], wsl[:], start=True, stop=True)
                    done(m)
                for h in range(SH):
                    m = M(pm[7][:, h * SG:(h + 1) * SG], bx_w[:, h, :], wsl[:], start=True, stop=True)
                done(m)
                M(pm[2][:], one_row[:], base_f[0:1, 0:512], start=True, stop=True)
                m = M(pm[3][:, 0:ET - 512], one_row[:], base_f[0:1, 512:ET], start=True, stop=True)
                done(m)
                for g in range(7):
                    rows = min(P, ET - g * P)
                    if g < 2:
                        pe.wait_ge(a_step, 9)
                        pe.wait_ge(v_step, v_at[f"rel{g}"])
                    else:
                        pe.wait_ge(v_step, max(v_at[f"idx{g - 2}"], v_at[f"rel{g}"]))
                    q = pm[4 + g % 2]
                    T(q[:, 0:rows], src_f[0:rows, g, :], c.ident[0:rows, 0:rows])
                    m = T(q[:, 256:256 + rows], rel_f[0:rows, g, :], c.ident[0:rows, 0:rows])
                    done(m)


def encode(c):
    nc, d = c.nc, c.d
    with ExitStack() as ctx:
        def sb(name, shape, dt=F32):
            return ctx.enter_context(nc.sbuf_tensor(name, shape, dt))

        x = [sb(f"x{i}", [P, D]) for i in range(2)]
        lab = [sb(f"lab{i}", [96, P], I32) for i in range(2)]
        hot = [sb(f"hot{i}", [96, P], BF16) for i in range(2)]
        xn = [sb(f"xn{i}", [P, D]) for i in range(2)]
        xnT = [sb(f"xnT{i}", [P, D]) for i in range(2)]
        zn = [sb(f"zn{i}", [P, FF]) for i in range(2)]
        yT = [sb(f"yT{i}", [P, FF]) for i in range(2)]
        fe = [sb(f"fe{i}", [P, ROW]) for i in range(2)]
        st = [sb(f"st{i}", [P, 32]) for i in range(2)]
        junk = sb("junk", [P, ET])
        tile_f = [sb(f"tile_f{i}", [P, 1]) for i in range(2)]
        tile_i = [sb(f"tile_i{i}", [P, 1], I32) for i in range(2)]
        rows = [sb(f"rows{i}", [P, P], I32) for i in range(2)]
        cnt = [sb(f"cnt{i}", [P, 1]) for i in range(2)]
        start_f = [sb(f"start_f{i}", [P, 1]) for i in range(2)]
        start_i = [sb(f"start_i{i}", [P, 1], I32) for i in range(2)]
        p_xT = ctx.enter_context(nc.psum_tensor("p_xT", [P, 512], F32))
        p_z = [ctx.enter_context(nc.psum_tensor(f"p_z{i}", [P, 2, 512], F32)) for i in range(2)]
        p_zT = ctx.enter_context(nc.psum_tensor("p_zT", [P, 2, 512], F32))
        p_fe = ctx.enter_context(nc.psum_tensor("p_fe", [P, 512], F32))

        in_ = sems(nc, ctx, "x_in0", "x_in1")
        stored = sems(nc, ctx, "fe_stored0", "fe_stored1")
        scattered = sems(nc, ctx, "er_scattered0", "er_scattered1")
        found = sems(nc, ctx, "rows_in0", "rows_in1")
        (chain, xn_ready, hot_ready, z_half, xT_done, xT_ready, z_done, var_x, std_x, var_z, std_z, scale_z, zn_ready,
         zT_done, yT_ready, fe_done, fe_ready, tile_ready, start_ready) = sems(
            nc, ctx, "chain", "xn_ready", "hot_ready", "z_half", "xT_done", "xT_ready", "z_done", "var_x", "std_x",
            "var_z", "std_z", "scale_z", "zn_ready", "zT_done", "yT_ready", "fe_done", "fe_ready", "tile_ready",
            "start_ready")
        free_x, counted = sems(nc, ctx, "free_x", "counted")

        with nc.Block() as block:
            @block.sync
            def _(sp):
                def store(j, q):
                    sp.wait_ge(fe_ready, j + 1)
                    sp.dma_start(d["table1"][bass.ds(j * P, P), :], fe[q][:]).then_inc(stored[q], 16)

                def load(j, q, n=P):
                    sp.wait_ge(free_x, j + 1)
                    sp.dma_start(x[q][0:n, :], d["x"][bass.ds(j * P, n), :]).then_inc(in_[q], 16)
                    at = d["labels"]
                    sp.dma_start(lab[q][:], at[bass.ds(j * P, P)].unsqueeze(0).broadcast_to([96, P])).then_inc(in_[q], 16)

                sp.sem_inc(free_x, 2)
                for j in range(3):
                    load(j, j % 2)
                with sp.Fori(0, (NT - 5) // 2) as k:
                    load(2 * k + 3, 1)
                    store(2 * k, 0)
                    load(2 * k + 4, 0)
                    store(2 * k + 1, 1)
                load(NT - 2, 1)
                store(NT - 5, 0)
                load(NT - 1, 0, TAIL)
                for j in range(NT - 4, NT):
                    store(j, j % 2)
                for q in range(2):
                    sp.wait_ge(stored[q], 16 * len(range(q, NT, 2)))

            @block.gpsimd
            def _(pool):
                def fetch(j, q):
                    pool.wait_ge(tile_ready, j + 1)
                    pool.nop(nofuse=True)
                    nc.gpsimd.indirect_dma_start(
                        out=rows[q][:], out_offset=None, in_=d["dst"],
                        in_offset=bass.IndirectOffsetOnAxis(ap=tile_i[q][:], axis=0)).then_inc(found[q], 16)

                def scatter(j, q, n=P):
                    pool.wait_ge(fe_ready, j + 1)
                    pool.wait_ge(start_ready, j + 1)
                    pool.nop(nofuse=True)
                    nc.gpsimd.indirect_dma_start(
                        out=d["er_start1"], out_offset=bass.IndirectOffsetOnAxis(ap=start_i[q][0:n, :], axis=0),
                        in_=fe[q][0:n, D + HEADS:ROW], in_offset=None).then_inc(scattered[q], 16)

                fetch(0, 0)
                fetch(1, 1)
                with pool.Fori(0, (NT - 3) // 2) as k:
                    fetch(2 * k + 2, 0)
                    scatter(2 * k, 0)
                    fetch(2 * k + 3, 1)
                    scatter(2 * k + 1, 1)
                fetch(NT - 1, 0)
                scatter(NT - 3, 0)
                scatter(NT - 2, 1)
                scatter(NT - 1, 0, TAIL)
                for q in range(2):
                    pool.wait_ge(scattered[q], 16 * len(range(q, NT, 2)))

            @block.vector
            def _(dve):
                V = nc.vector

                def stats_x(j, q):
                    dve.wait_ge(in_[q], 16 * (2 * (j // 2) + 2) if isinstance(j, int) else (j + 2 - q) * 16)
                    s = st[q]
                    V.bn_stats(s[:, 0:6], x[q][:]).then_inc(chain, 1)
                    V.tensor_scalar(hot[q][:], lab[q][:], c.klass[0:96, :], None, ALU.is_equal).then_inc(hot_ready, 1)
                    dve.wait_ge(chain, 4 * j + 1)
                    dve.nop(nofuse=True)
                    V.bn_aggr(s[:, 6:8], s[:, 0:6]).then_inc(var_x, 1)
                    V.tensor_scalar(junk[:], c.base_bc[:], c.nid[:, bass.ds(j, 1)], 0.0, ALU.is_lt, ALU.add,
                                    accum_out=tile_f[q][:]).then_inc(chain, 1)
                    dve.wait_ge(chain, 4 * j + 2)
                    V.tensor_scalar(tile_f[q][:], tile_f[q][:], -1.0, 0.0, ALU.add, ALU.max).then_inc(chain, 1)
                    dve.wait_ge(chain, 4 * j + 3)
                    V.tensor_copy(tile_i[q][:], tile_f[q][:]).then_inc(tile_ready, 1)

                def norm_x(j, q):
                    s = st[q]
                    dve.wait_ge(std_x, j + 1)
                    V.reciprocal(s[:, 9:10], s[:, 8:9]).then_inc(chain, 1)
                    dve.wait_ge(chain, 4 * j + 4)
                    V.tensor_scalar(xn[q][:], x[q][:], s[:, 6:7], s[:, 9:10], ALU.subtract,
                                    ALU.mult).then_inc(xn_ready, 1)
                    dve.wait_ge(xn_ready, j + 1)
                    dve.sem_inc(free_x, 1)

                def norm_z(j, q):
                    s = st[q]
                    dve.wait_ge(z_done, j + 1)
                    V.bn_stats(s[:, 10:16], p_z[q][:, 0, :])
                    V.bn_stats(s[:, 16:22], p_z[q][:, 1, :]).then_inc(z_half, 1)
                    dve.wait_ge(z_half, 2 * j + 1)
                    dve.nop(nofuse=True)
                    V.bn_aggr(s[:, 22:24], s[:, 10:22]).then_inc(var_z, 1)
                    dve.wait_ge(std_z, j + 1)
                    V.reciprocal(s[:, 25:26], s[:, 24:25]).then_inc(z_half, 1)
                    dve.wait_ge(z_half, 2 * j + 2)
                    V.scalar_tensor_tensor(out=s[:, 26:27], in0=s[:, 22:23], scalar=-1.0, in1=s[:, 25:26],
                                           op0=ALU.mult, op1=ALU.mult).then_inc(scale_z, 1)
                    dve.wait_ge(scale_z, j + 1)
                    V.tensor_scalar(zn[q][:, 0:512], p_z[q][:, 0, :], s[:, 25:26], s[:, 26:27], ALU.mult,
                                    ALU.add).then_inc(zn_ready, 1)

                def edge_start(j, q):
                    if not known_below(j, 2):
                        dve.wait_ge(scattered[q], (j - q) * 8)
                    dve.wait_ge(found[q], 16 * (j // 2 + 1) if isinstance(j, int) else (j + 2 - q) * 8)
                    V.tensor_scalar(junk[:, 0:P], rows[q][:], c.nid[:, bass.ds(j, 1)], 0.0, ALU.is_lt, ALU.add,
                                    accum_out=cnt[q][:]).then_inc(counted, 1)
                    dve.wait_ge(counted, 2 * j + 1)
                    V.scalar_tensor_tensor(out=start_f[q][:], in0=tile_f[q][:], scalar=float(P), in1=cnt[q][:],
                                           op0=ALU.mult, op1=ALU.add).then_inc(counted, 1)
                    dve.wait_ge(counted, 2 * j + 2)
                    V.tensor_copy(start_i[q][:], start_f[q][:]).then_inc(start_ready, 1)
                    V.tensor_copy(c.start[:, bass.ds(j, 1)], start_f[q][:])

                def features(j, q):
                    if not known_below(j, 2):
                        dve.wait_ge(stored[q], (j - q) * 8)
                        dve.wait_ge(scattered[q], (j - q) * 8)
                    dve.wait_ge(fe_done, j + 1)
                    V.tensor_tensor(fe[q][:], p_fe[:, 0:ROW], c.bias1[:], ALU.add).then_inc(fe_ready, 1)

                def tile(j, q, ahead=True):
                    norm_z(j, q)
                    edge_start(j, q)
                    if ahead:
                        stats_x(j + 2, q)
                    if not known_below(j, 1):
                        features(j - 1, 1 - q)
                    if ahead:
                        norm_x(j + 2, q)

                for j in range(2):
                    stats_x(j, j)
                    norm_x(j, j)
                for j in range(3):
                    tile(j, j % 2)
                with dve.Fori(1, (NT - 3) // 2) as k:
                    tile(2 * k + 1, 1)
                    tile(2 * k + 2, 0)
                tile(NT - 2, 1, ahead=False)
                tile(NT - 1, 0, ahead=False)
                features(NT - 1, 0)

            @block.scalar
            def _(act):
                A = nc.scalar.activation

                def std(j, q):
                    s = st[q]
                    act.wait_ge(var_x, j + 1)
                    A(s[:, 8:9], s[:, 7:8], ACT.Sqrt, bias=c.eps[:]).then_inc(std_x, 1)

                def copy_x(j, q):
                    act.wait_ge(xT_done, j + 1)
                    A(xnT[q][:], p_xT[:, 0:D], ACT.Copy).then_inc(xT_ready, 1)

                def mid(j, q):
                    s = st[q]
                    act.wait_ge(var_z, j + 1)
                    A(s[:, 24:25], s[:, 23:24], ACT.Sqrt, bias=c.eps[:]).then_inc(std_z, 1)
                    act.wait_ge(scale_z, j + 1)
                    A(zn[q][:, 512:1024], p_z[q][:, 1, :], ACT.Identity, bias=s[:, 26:27],
                      scale=s[:, 25:26]).then_inc(zn_ready, 1)

                def rise(j, q, h):
                    act.wait_ge(zT_done, 2 * j + h + 1)
                    for i in range(4):
                        k = 4 * h + i
                        a = A(yT[q][:, k * P:(k + 1) * P], p_zT[:, h, i * P:(i + 1) * P], ACT.Relu,
                              bias=c.ln_b[:, k:k + 1], scale=c.ln_g[:, k:k + 1])
                    a.then_inc(yT_ready, 1)

                def tile(j, q, ahead=True):
                    mid(j, q)
                    rise(j, q, 0)
                    if ahead:
                        std(j + 2, q)
                    rise(j, q, 1)
                    if ahead:
                        copy_x(j + 2, q)

                for j in range(2):
                    std(j, j)
                    copy_x(j, j)
                with act.Fori(0, (NT - 3) // 2) as k:
                    tile(2 * k, 0)
                    tile(2 * k + 1, 1)
                tile(NT - 3, 0)
                tile(NT - 2, 1, ahead=False)
                tile(NT - 1, 0, ahead=False)

            @block.tensor
            def _(pe):
                M, T = nc.tensor.matmul, nc.tensor.transpose

                def xT(j, q):
                    pe.wait_ge(xn_ready, j + 1)
                    for k in range(2):
                        t = T(p_xT[:, k * P:(k + 1) * P], xn[q][:, k * P:(k + 1) * P], c.ident[:])
                    t.then_inc(xT_done, 1)

                def z(j, q):
                    pe.wait_ge(xT_ready, j + 1)
                    pe.wait_ge(hot_ready, j + 1)
                    for h in range(2):
                        cols = slice(h * 512, (h + 1) * 512)
                        for k in range(2):
                            M(p_z[q][:, h, :], xnT[q][:, k * P:(k + 1) * P], c.w1a[:, k, cols], start=k == 0, stop=False)
                        m = M(p_z[q][:, h, :], hot[q][:], c.label_rows[:, cols], start=False, stop=True)
                    m.then_inc(z_done, 1)

                def zT(j, q):
                    pe.wait_ge(zn_ready, 2 * j + 2)
                    for h in range(2):
                        for i in range(4):
                            k = 4 * h + i
                            t = T(p_zT[:, h, i * P:(i + 1) * P], zn[q][:, k * P:(k + 1) * P], c.ident[:])
                        t.then_inc(zT_done, 1)

                def fe_mm(j, q):
                    pe.wait_ge(yT_ready, 2 * j + 2)
                    if not known_below(j, 1):
                        pe.wait_ge(fe_ready, j)
                    for k in range(8):
                        m = M(p_fe[:, 0:ROW], yT[q][:, k * P:(k + 1) * P], c.fused[:, k, :], start=k == 0, stop=k == 7)
                    m.then_inc(fe_done, 1)

                def tile(j, q, ahead=2):
                    zT(j, q)
                    if ahead > 0:
                        z(j + 1, 1 - q)
                    if ahead > 1:
                        xT(j + 2, q)
                    fe_mm(j, q)

                xT(0, 0)
                z(0, 0)
                xT(1, 1)
                for j in range(3):
                    tile(j, j % 2)
                with pe.Fori(1, (NT - 3) // 2) as k:
                    tile(2 * k + 1, 1)
                    tile(2 * k + 2, 0)
                tile(NT - 2, 1, ahead=1)
                tile(NT - 1, 0, ahead=0)


def edges(c, layer):
    nc, d = c.nc, c.d
    with ExitStack() as ctx:
        def sb(name, shape, dt=F32):
            return ctx.enter_context(nc.sbuf_tensor(f"{name}_{layer}", shape, dt))

        def two(name, shape, dt=F32):
            return [sb(f"{name}{i}", shape, dt) for i in range(2)]

        rows = two("rows", [P, TPB, ROW])
        scaled = sb("scaled", [P, RING, D])
        window = sb("window", [P, RING, P])
        idx_now = two("idx_now", [P, TPB], I32)
        er = two("er_now", [BP, P])
        el = sb("el", [P, BP])
        dst_i = two("dst_i", [BP, P + 2], I32)
        cut = sb("cut", [BP, P + 1])
        fst = sb("fst", [BP, P])
        e0 = sb("e0", [BP, P])
        e = sb("e", [BP, P])
        run_max = sb("run_max", [BP, P])
        node_max = sb("node_max", [BP, P])
        full_max = sb("full_max", [BP, P])
        down = sb("down", [BP, P])
        prob = sb("prob", [BP, P])
        last_max = sb("last_max", [BP, TPB])
        carried = sb("carried", [HEADS, NB * TPB + 1])
        brought = sb("brought", [HEADS, TPB])
        spread_junk = sb("spread_junk", [BP, TPB])
        carry = sb("carry", [BP, 1])
        fade = sb("fade", [BP, 1])
        fade_t = sb("fade_t", [BP, TPB])
        wt = two("wt", [P, BP])
        fades = two("fades", [P, 3, TPB])
        kept = sb("kept", [P, 2, 3])
        er_at = sb("er_at", [P, EPP, HEADS])
        spread = sb("spread", [P, HEADS, EPP])
        first_row = sb("first_row", [P, ROW])
        first = sb("first", [P, RING, 3])
        p_part = [ctx.enter_context(nc.psum_tensor(f"p_part{i}_{layer}", [P, 512], F32)) for i in range(RING)]
        p_e = ctx.enter_context(nc.psum_tensor(f"p_e_{layer}", [P, 512], F32))
        p_carry = ctx.enter_context(nc.psum_tensor(f"p_carry_{layer}", [P, 512], F32))
        p_w = ctx.enter_context(nc.psum_tensor(f"p_w_{layer}", [P, 512], F32))
        p_fade = ctx.enter_context(nc.psum_tensor(f"p_fade_{layer}", [P, 512], F32))

        names = ["idx_ready", "el_ready", "eT_done", "link", "last_ready", "last_done", "brought_ready",
                 "brought_done", "down_ready", "carry_ready", "exp_done", "fade_done", "fade_ready", "w_done",
                 "fadeT_done", "w_ready", "scaled_ready", "mm_done", "kept_ready", "taken", "fixed",
                 "copied", "psum_zero"]
        S = dict(zip(names, sems(nc, ctx, *(f"{n}_{layer}" for n in names))))
        moved, row_in, scanned = sems(nc, ctx, *(f"{n}_{layer}" for n in ("er_moved", "row_in", "scanned")))
        gathered = sems(nc, ctx, *(f"gathered{i}_{layer}" for i in range(2)))
        loaded = sems(nc, ctx, *(f"batch_in{i}_{layer}" for i in range(2)))

        PREP = TPB - 23
        ZEROED = RING + (2 if layer == 1 else 1)
        LEAD = RING - 1

        def ring(q, s):
            return (q * TPB + s) % RING

        with nc.Block() as block:
            @block.sync
            def _(sp):
                def load(b, q):
                    sp.wait_ge(S["down_ready"], b + 1)
                    ee, dd = d[f"er_edge{layer}"], d["dst_seq"]
                    sp.dma_start(er[q][:], ee.rearrange("h (b t e) -> b t h e", t=TPB, e=P)[bass.ds(b, 1)].rearrange(
                        "b t h e -> (b t) h e")).then_inc(loaded[q], 16)
                    sp.dma_start(dst_i[q][:], d["dst_over"][bass.ds(b * TPB, TPB), :].unsqueeze(1).broadcast_to(
                        [TPB, HEADS, P + 2])).then_inc(loaded[q], 16)

                sp.dma_start(er_at[:], d[f"er_start{layer}"].rearrange("(p a) h -> p a h", p=P)).then_inc(moved, 16)
                for h in range(HEADS):
                    sp.wait_ge(scanned, h + 1)
                    sp.dma_start(d[f"er_edge{layer}"][h].rearrange("(p a) -> p a", p=P), spread[:, h, :]).then_inc(moved, 16)
                sp.wait_ge(moved, 16 * (1 + HEADS))
                sp.sem_inc(S["down_ready"], 2)
                with sp.Fori(0, PAIRS) as k:
                    load(2 * k, 0)
                    load(2 * k + 1, 1)

            @block.gpsimd
            def _(pool):
                nc.gpsimd.indirect_dma_start(
                    out=first_row[:], out_offset=None, in_=d[f"table{layer}"],
                    in_offset=bass.IndirectOffsetOnAxis(ap=c.first_id[:], axis=0)).then_inc(row_in, 16)
                with pool.Fori(0, PAIRS) as k:
                    for q in range(2):
                        b = 2 * k + q
                        pool.wait_ge(S["idx_ready"], b + 1)
                        for s in range(TPB):
                            if s % 4 == 0:
                                pool.wait_ge(S["scaled_ready"], b * TPB + s + 4)
                            pool.nop(nofuse=True)
                            nc.gpsimd.indirect_dma_start(
                                out=rows[q][:, s, :], out_offset=None, in_=d[f"table{layer}"],
                                in_offset=bass.IndirectOffsetOnAxis(ap=idx_now[q][:, s:s + 1], axis=0)
                            ).then_inc(gathered[q], 16)

            @block.vector
            def _(dve):
                V = nc.vector
                LINKS = 7

                def index(b, q):
                    V.tensor_copy(idx_now[q][:], c.idx[:, bass.ds(b * TPB, TPB)]).then_inc(S["idx_ready"], 1)

                def prep(b, q):
                    def links(k):
                        dve.wait_ge(S["link"], b * LINKS + k)

                    def borders():
                        dve.wait_ge(loaded[q], (b + 2 - q) * 16)
                        V.tensor_tensor(cut[:], dst_i[q][:, 1:P + 2], dst_i[q][:, 0:P + 1],
                                        ALU.not_equal).then_inc(S["link"], 1)
                        V.tensor_scalar(fst[:], dst_i[q][:, 1:P + 1], dst_i[q][:, 1:2], -BIG, ALU.not_equal, ALU.mult)

                    def sum_():
                        links(1)
                        V.tensor_scalar(cut[:], cut[:], -BIG, None, ALU.mult).then_inc(S["link"], 1)
                        dve.wait_ge(S["eT_done"], b + 1)
                        V.tensor_tensor(e0[:], p_e[0:BP, 0:P], er[q][:], ALU.add).then_inc(S["link"], 1)

                    def leak():
                        links(3)
                        V.scalar_tensor_tensor(out=e[:], in0=e0[:], scalar=SLOPE, in1=e0[:], op0=ALU.mult,
                                               op1=ALU.max).then_inc(S["link"], 1)

                    def forth():
                        links(4)
                        V.tensor_tensor_scan(run_max[:], cut[:, 0:P], e[:], -BIG, ALU.add, ALU.max).then_inc(S["link"], 1)

                    def back():
                        links(5)
                        V.tensor_tensor_scan(node_max[:, ::-1], cut[:, :0:-1], run_max[:, ::-1], -BIG, ALU.add,
                                             ALU.max).then_inc(S["link"], 1)

                    def last():
                        links(6)
                        V.tensor_scalar(last_max[:], c.is_tile[0:BP, :], node_max[:, P - 1:P], None,
                                        ALU.mult).then_inc(S["last_ready"], 1)

                    def carries():
                        dve.wait_ge(S["last_done"], b + 1)
                        V.tensor_tensor_scan(carried[:, bass.ds(b * TPB + 1, TPB)], c.pass_on[:, bass.ds(b * TPB, TPB)],
                                             p_carry[0:HEADS, 0:TPB], carried[:, bass.ds(b * TPB, 1)], ALU.add,
                                             ALU.max).then_inc(S["link"], 1)

                    def bring():
                        links(7)
                        V.tensor_tensor(brought[:], carried[:, bass.ds(b * TPB, TPB)], c.go_on[:, bass.ds(b * TPB, TPB)],
                                        ALU.add).then_inc(S["brought_ready"], 1)

                    def own():
                        dve.wait_ge(S["brought_done"], b + 1)
                        V.tensor_tensor_reduce(spread_junk[:], p_carry[0:BP, 64:64 + TPB], c.is_tile[0:BP, :], 1.0, 0.0,
                                               ALU.mult, ALU.add, carry[:]).then_inc(S["carry_ready"], 1)

                    def full():
                        dve.wait_ge(S["carry_ready"], 2 * b + 1)
                        V.scalar_tensor_tensor(out=full_max[:], in0=fst[:], scalar=carry[:], in1=node_max[:],
                                               op0=ALU.add, op1=ALU.max).then_inc(S["carry_ready"], 1)

                    def shift():
                        dve.wait_ge(S["carry_ready"], 2 * b + 2)
                        V.tensor_tensor(down[:], e[:], full_max[:], ALU.subtract).then_inc(S["down_ready"], 1)

                    def fade_():
                        dve.wait_ge(S["fade_done"], b + 1)
                        V.tensor_scalar(fade_t[:], c.is_tile[0:BP, :], fade[:], None, ALU.mult).then_inc(S["fade_ready"], 1)

                    return {PREP + 1: borders, PREP + 3: sum_, PREP + 4: leak, PREP + 5: forth, PREP + 6: back,
                            PREP + 7: last, PREP + 10: carries, PREP + 11: bring, PREP + 13: own, PREP + 14: full,
                            PREP + 15: shift, PREP + 17: fade_}

                def make_window(i, q, s):
                    dve.wait_ge(S["mm_done"], i + 1)
                    V.tensor_scalar(window[:, ring(q, s), :], c.iota[:], c.rel[:, bass.ds(i, 1)], None, ALU.is_equal)

                def scale(q, s):
                    V.tensor_tensor(scaled[:, ring(q, s), :].rearrange("p (h f) -> p h f", h=HEADS),
                                    rows[q][:, s, 0:D].rearrange("p (h f) -> p h f", h=HEADS),
                                    wt[q][:, HEADS * s:HEADS * s + HEADS].unsqueeze(2).broadcast_to([P, HEADS, HID]),
                                    ALU.mult).then_inc(S["scaled_ready"], 1)

                def take(i, q, s):
                    dve.wait_ge(S["mm_done"], i + RING + 1)
                    V.tensor_copy(first[:, ring(q, s), :].unsqueeze(2), p_part[ring(q, s)][:, 0:3 * P].rearrange(
                        "p (a n) -> p a n", a=3)[:, :, 0:1]).then_inc(S["taken"], 1)

                def keep(i, q, s, at):
                    dve.wait_ge(S["copied"], i + RING)
                    dve.wait_ge(S["fixed"], i + 1)
                    V.tensor_tensor(kept[:, s % 2, :].unsqueeze(2), c.acc[:, :, bass.ds(at, 1)], fades[q][:, :, s:s + 1],
                                    ALU.mult).then_inc(S["kept_ready"], 1)

                def fix(i, q, s, at):
                    dve.wait_ge(S["taken"], i + 1)
                    dve.wait_ge(S["kept_ready"], i + 1)
                    V.tensor_tensor(c.acc[:, :, bass.ds(at, 1)], kept[:, s % 2, :].unsqueeze(2),
                                    first[:, ring(q, s), :].unsqueeze(2), ALU.add).then_inc(S["fixed"], 1)

                def batch(b, q, ahead, more=False):
                    steps = prep(b + 1, 1 - q) if ahead else {}
                    if more:
                        dve.wait_ge(gathered[q], (b + 2 - q) * 8 * TPB)
                        index(b + 2, q)
                    for s in range(TPB):
                        i = b * TPB + s
                        if s % 8 == 0:
                            at = nc.values_load_multi_w_load_instructions(
                                c.base[0:1, bass.ds(i, min(8, TPB - s))], engines=DVE_ONLY, min_val=0, max_val=N,
                                skip_runtime_bounds_check_because="a node's number")[1]
                        to = (q, s + LEAD) if s + LEAD < TPB else (1 - q, s + LEAD - TPB)
                        scales = ahead or s + LEAD < TPB
                        take(i, q, s)
                        keep(i, q, s, at[s % 8])
                        if scales:
                            make_window(i + LEAD, *to)
                        fix(i, q, s, at[s % 8])
                        if scales:
                            if s == TPB - LEAD:
                                dve.wait_ge(S["w_ready"], 2 * b + 4)
                            scale(*to)
                        if s in steps:
                            steps[s]()

                index(0, 0)
                index(1, 1)
                dve.wait_ge(moved, 16)
                dve.wait_ge(row_in, 16)
                for h in range(HEADS):
                    V.tensor_tensor_scan(spread[:, h, :], c.not_start[:], er_at[:, :, h],
                                         first_row[:, D + HEADS + h:D + HEADS + h + 1],
                                         ALU.mult, ALU.add).then_inc(scanned, 1)
                if layer == 1:
                    V.memset(c.acc[:], 0.0).then_inc(S["psum_zero"], 1)
                V.memset(carried[:, 0:1], -BIG).then_inc(S["psum_zero"], 1)
                for r in range(RING):
                    V.memset(p_part[r][:], 0.0).then_inc(S["psum_zero"], 1)
                dve.wait_ge(S["psum_zero"], ZEROED)
                dve.sem_inc(S["fixed"], 1)
                for _, step in sorted(prep(0, 0).items()):
                    step()
                dve.wait_ge(S["w_ready"], 2)
                for s in range(LEAD):
                    make_window(s, 0, s)
                    scale(0, s)
                with dve.Fori(0, PAIRS - 1) as k:
                    batch(2 * k, 0, True, more=True)
                    batch(2 * k + 1, 1, True, more=True)
                batch(NB - 2, 0, True)
                batch(NB - 1, 1, False)

            @block.scalar
            def _(act):
                A = nc.scalar.activation

                def prep(b, q):
                    def pick():
                        act.wait_ge(gathered[q], (b + 2 - q) * 8 * TPB)
                        A(el[:].rearrange("p (t h) -> p t h", h=HEADS), rows[q][:, :, D:D + HEADS],
                          ACT.Copy).then_inc(S["el_ready"], 1)

                    def probs():
                        act.wait_ge(S["down_ready"], b + 3)
                        A(prob[:], down[:], ACT.Exp).then_inc(S["exp_done"], 1)
                        A(fade[:], full_max[:, 0:1], ACT.Exp, bias=carry[:], scale=-1.0).then_inc(S["fade_done"], 1)

                    def copy_out():
                        act.wait_ge(S["w_done"], b + 1)
                        A(wt[q][:], p_w[:, 0:BP], ACT.Copy).then_inc(S["w_ready"], 1)
                        act.wait_ge(S["fadeT_done"], b + 1)
                        A(fades[q][:].rearrange("p a t -> p (a t)"), p_fade[:, 0:3 * TPB],
                          ACT.Copy).then_inc(S["w_ready"], 1)
                    return {PREP: pick, PREP + 16: probs, PREP + 19: copy_out}

                def batch(b, q, ahead):
                    steps = prep(b + 1, 1 - q) if ahead else {}
                    for s in range(TPB):
                        i = b * TPB + s
                        if s % 8 == 0:
                            at = nc.values_load_multi_w_load_instructions(
                                c.base[0:1, bass.ds(i, min(8, TPB - s))], engines=ACT_ONLY, min_val=0, max_val=N,
                                skip_runtime_bounds_check_because="a node's number")[1]
                        act.wait_ge(S["taken"], i + 1)
                        act.wait_ge(S["copied"], i + RING)
                        A(c.acc[:, :, bass.ds(at[s % 8] + 1, P - 1)],
                          p_part[ring(q, s)][:, 0:3 * P].rearrange("p (a n) -> p a n", a=3)[:, :, 1:P],
                          ACT.Copy).then_inc(S["copied"], 1)
                        if s in steps:
                            steps[s]()

                act.sem_inc(S["copied"], RING)
                for _, step in sorted(prep(0, 0).items()):
                    step()
                with act.Fori(0, PAIRS - 1) as k:
                    batch(2 * k, 0, True)
                    batch(2 * k + 1, 1, True)
                batch(NB - 2, 0, True)
                batch(NB - 1, 1, False)

            @block.tensor
            def _(pe):
                M, T = nc.tensor.matmul, nc.tensor.transpose

                def prep(b, q):
                    def eT():
                        pe.wait_ge(S["el_ready"], b + 1)
                        pe.nop(nofuse=True)
                        T(p_e[0:BP, 0:P], el[:], c.ident[:]).then_inc(S["eT_done"], 1)

                    def last():
                        pe.wait_ge(S["last_ready"], b + 1)
                        pe.nop(nofuse=True)
                        M(p_carry[0:HEADS, 0:TPB], c.is_head[0:BP, :], last_max[:], start=True,
                          stop=True).then_inc(S["last_done"], 1)

                    def bring():
                        pe.wait_ge(S["brought_ready"], b + 1)
                        pe.nop(nofuse=True)
                        M(p_carry[0:BP, 64:64 + TPB], c.head_parts[:], brought[:], start=True,
                          stop=True).then_inc(S["brought_done"], 1)

                    def turn():
                        pe.wait_ge(S["exp_done"], b + 1)
                        pe.nop(nofuse=True)
                        T(p_w[:, 0:BP], prob[:], c.ident[0:BP, 0:BP]).then_inc(S["w_done"], 1)

                    def fades_():
                        pe.wait_ge(S["fade_ready"], b + 1)
                        pe.nop(nofuse=True)
                        for a in range(3):
                            m = M(p_fade[:, a * TPB:(a + 1) * TPB], c.to_rows[0:BP, a, :], fade_t[:], start=True, stop=True)
                        m.then_inc(S["fadeT_done"], 1)
                    return {PREP + 3: eT, PREP + 10: last, PREP + 13: bring, PREP + 18: turn, PREP + 19: fades_}

                def batch(b, q, ahead):
                    steps = prep(b + 1, 1 - q) if ahead else {}
                    for s in range(TPB):
                        i = b * TPB + s
                        r = ring(q, s)
                        pe.wait_ge(S["scaled_ready"], i + RESERVED + 1)
                        pe.wait_ge(S["copied"], i + 1)
                        for a in range(2):
                            M(p_part[r][:, a * P:(a + 1) * P], scaled[:, r, a * P:(a + 1) * P], window[:, r, :],
                              start=True, stop=True)
                        M(p_part[r][0:HEADS, 2 * P:3 * P], wt[q][:, HEADS * s:HEADS * s + HEADS], window[:, r, :],
                          start=True, stop=True).then_inc(S["mm_done"], 1)
                        if s in steps:
                            steps[s]()

                pe.sem_inc(S["mm_done"], RING)
                pe.sem_inc(S["scaled_ready"], RESERVED)
                pe.wait_ge(S["psum_zero"], ZEROED)
                for _, step in sorted(prep(0, 0).items()):
                    step()
                with pe.Fori(0, PAIRS - 1) as k:
                    batch(2 * k, 0, True)
                    batch(2 * k + 1, 1, True)
                batch(NB - 2, 0, True)
                batch(NB - 1, 1, False)


def end_of_layer(c, ctx, tag, block_bias):
    nc = c.nc

    def sb(name, shape):
        return ctx.enter_context(nc.sbuf_tensor(f"{name}_{tag}", shape, F32))

    flat = sb("flat", [P, NT * HEADS])
    inv_now = [sb(f"inv_now{i}", [HEADS, P]) for i in range(4)]
    avg = [sb(f"avg{i}", [P, 2, P]) for i in range(4)]
    hT = [sb(f"hT{i}", [P, 2, P]) for i in range(4)]
    p_inv = [ctx.enter_context(nc.psum_tensor(f"p_inv{i}_{tag}", [P, 512], F32)) for i in range(4)]
    moved, inv_ready, inv_picked, inv_done, avg_ready, hT_ready, hT_used = sems(
        nc, ctx, *(f"{n}_{tag}" for n in ("moved", "inv_ready", "inv_picked", "inv_done", "avg_ready", "hT_ready",
                                          "hT_used")))

    def move_sums(sp):
        sums = c.acc[0:HEADS, 2, 0:NT * P]
        by_head, by_part = c.d["weight_sums"], c.d["weight_sums"].rearrange("h (a n) -> (h a) n", a=P // HEADS)
        sp.dma_start(by_head, sums).then_inc(moved, 16)
        sp.wait_ge(moved, 16)
        sp.dma_start(flat[:], by_part).then_inc(moved, 16)
        sp.wait_ge(inv_ready, 2)
        sp.dma_start(by_part, flat[:]).then_inc(moved, 16)
        sp.wait_ge(moved, 48)
        sp.dma_start(sums, by_head).then_inc(moved, 16)

    def invert(dve):
        dve.wait_ge(moved, 32)
        nc.vector.tensor_scalar(flat[:], flat[:], 1e-9, None, ALU.max).then_inc(inv_ready, 1)
        dve.wait_ge(inv_ready, 1)
        nc.vector.reciprocal(flat[:], flat[:]).then_inc(inv_ready, 1)

    def pick(act, j, q):
        if known_below(j, 1):
            act.wait_ge(moved, 64)
        if not known_below(j, 4):
            act.wait_ge(inv_done, j - 3)
        nc.scalar.activation(inv_now[q][:], c.acc[0:HEADS, 2, bass.ds(j * P, P)], ACT.Copy).then_inc(inv_picked, 1)

    def spread(pe, j, q):
        pe.wait_ge(inv_picked, j + 1)
        if not known_below(j, 4):
            pe.wait_ge(avg_ready, j - 3)
        for a in range(2):
            m = nc.tensor.matmul(p_inv[q][:, a * P:(a + 1) * P], c.head_rows[:, a * P:(a + 1) * P],
                                 inv_now[q][:], start=True, stop=True)
        m.then_inc(inv_done, 1)

    def average(dve, j, q):
        dve.wait_ge(inv_done, j + 1)
        if not known_below(j, 4):
            dve.wait_ge(hT_ready, j - 3)
        nc.vector.tensor_tensor(avg[q][:], c.acc[:, 0:2, bass.ds(j * P, P)],
                                p_inv[q][:, 0:2 * P].rearrange("p (a n) -> p a n", a=2), ALU.mult).then_inc(avg_ready, 1)

    def relu(act, j, q):
        act.wait_ge(avg_ready, j + 1)
        if not known_below(j, 4):
            act.wait_ge(hT_used, j - 3)
        for a in range(2):
            i = nc.scalar.activation(hT[q][:, a, :], avg[q][:, a, :], ACT.Relu,
                                     bias=c.gat_b[:, block_bias, a:a + 1])
        i.then_inc(hT_ready, 1)

    def ends(act, j, r):
        if a_tile(j + 4):
            pick(act, j + 4, r)
        if a_tile(j + 2):
            relu(act, j + 2, (r + 2) % 4)
    return hT, hT_ready, hT_used, move_sums, invert, spread, average, ends


def second_features(c):
    nc, d = c.nc, c.d
    with ExitStack() as ctx:
        fe = [ctx.enter_context(nc.sbuf_tensor(f"fe2_{i}", [P, ROW], F32)) for i in range(4)]
        start_i = [ctx.enter_context(nc.sbuf_tensor(f"start2_{i}", [P, 1], I32)) for i in range(4)]
        p_fe = [ctx.enter_context(nc.psum_tensor(f"p_fe2_{i}", [P, 512], F32)) for i in range(2)]
        hT, hT_ready, hT_used, move_sums, invert, spread, average, ends = end_of_layer(c, ctx, "one", 0)
        stored = sems(nc, ctx, *(f"fe2_stored{i}" for i in range(4)))
        scattered = sems(nc, ctx, *(f"er2_scattered{i}" for i in range(4)))
        fe_ready, = sems(nc, ctx, "fe2_ready")

        with nc.Block() as block:
            @block.sync
            def _(sp):
                def store(j, r):
                    sp.wait_ge(fe_ready, j + 1)
                    sp.dma_start(d["table2"][bass.ds(j * P, P), :], fe[r][:]).then_inc(stored[r], 16)
                move_sums(sp)
                by_four(sp, store)
                for r in range(4):
                    sp.wait_ge(stored[r], 16 * len(range(r, NT, 4)))

            @block.gpsimd
            def _(pool):
                def scatter(j, r, n=P):
                    pool.wait_ge(fe_ready, j + 1)
                    pool.nop(nofuse=True)
                    nc.gpsimd.indirect_dma_start(
                        out=d["er_start2"], out_offset=bass.IndirectOffsetOnAxis(ap=start_i[r][0:n, :], axis=0),
                        in_=fe[r][0:n, D + HEADS:ROW], in_offset=None).then_inc(scattered[r], 16)
                by_four(pool, lambda j, r: scatter(j, r, TAIL if known_below(j, NT) else P))
                for r in range(4):
                    pool.wait_ge(scattered[r], 16 * len(range(r, NT, 4)))

            @block.vector
            def _(dve):
                def features(j, r):
                    if not known_below(j, 4):
                        dve.wait_ge(stored[r], (j - r) * 4)
                        dve.wait_ge(scattered[r], (j - r) * 4)
                    nc.vector.tensor_copy(start_i[r][:], c.start[:, bass.ds(j, 1)])
                    dve.wait_ge(hT_used, j + 1)
                    nc.vector.tensor_copy(fe[r][:], p_fe[r % 2][:, 0:ROW]).then_inc(fe_ready, 1)

                def tile(j, r):
                    if a_tile(j + 2):
                        average(dve, j + 2, (r + 2) % 4)
                    if a_tile(j):
                        features(j, r)
                invert(dve)
                staggered(dve, tile)

            @block.scalar
            def _(act):
                staggered(act, lambda j, r: ends(act, j, r))

            @block.tensor
            def _(pe):
                def features(j, r):
                    q = r % 2
                    pe.wait_ge(hT_ready, j + 1)
                    if not known_below(j, 2):
                        pe.wait_ge(fe_ready, j - 1)
                    for k in range(2):
                        m = nc.tensor.matmul(p_fe[q][:, 0:ROW], hT[r][:, k, :], c.gext2[:, k, :], start=k == 0, stop=k == 1)
                    m.then_inc(hT_used, 1)

                def tile(j, r):
                    if a_tile(j + 1):
                        features(j + 1, (r + 1) % 4)
                    if a_tile(j + 4):
                        spread(pe, j + 4, r)
                staggered(pe, tile)


def join(c):
    nc, d = c.nc, c.d
    with ExitStack() as ctx:
        def four(name, shape):
            return [ctx.enter_context(nc.sbuf_tensor(f"{name}{i}", shape, F32)) for i in range(4)]

        x = four("jx", [P, D])
        x2 = four("jx2", [P, D])
        st = four("jst", [P, 8])
        p_h = [ctx.enter_context(nc.psum_tensor(f"p_h{i}", [P, 512], F32)) for i in range(2)]
        hT, hT_ready, hT_used, move_sums, invert, spread, average, ends = end_of_layer(c, ctx, "two", 1)
        moved_x = sems(nc, ctx, *(f"x_moved{i}" for i in range(4)))
        x2_ready, stat, var_ready, kept, std_ready = sems(
            nc, ctx, "x2_ready", "stat", "jvar_ready", "var_kept", "jstd_ready")

        with nc.Block() as block:
            @block.sync
            def _(sp):
                def load(j, r, n=P):
                    sp.dma_start(x[r][0:n, :], d["x"][bass.ds(j * P, n), :]).then_inc(moved_x[r], 16)

                def store(j, r):
                    sp.wait_ge(x2_ready, j + 1)
                    sp.dma_start(d["x2"][bass.ds(j * P, P), :], x2[r][:]).then_inc(moved_x[r], 16)

                for j in range(4):
                    load(j, j)
                move_sums(sp)
                with sp.Fori(0, NT // 4 - 1) as k:
                    for r in range(4):
                        store(4 * k + r, r)
                        load(4 * k + 4 + r, r)
                store(NT - 5, 0)
                load(NT - 1, 0, TAIL)
                for j in range(NT - 4, NT):
                    store(j, j % 4)
                for r in range(4):
                    sp.wait_ge(moved_x[r], 32 * len(range(r, NT, 4)))

            @block.vector
            def _(dve):
                V = nc.vector

                def add(j, r):
                    dve.wait_ge(moved_x[r], (j - r) * 8 + 16)
                    dve.wait_ge(hT_used, j + 1)
                    V.tensor_tensor(x2[r][:], p_h[r % 2][:, 0:D], x[r][:], ALU.add).then_inc(x2_ready, 1)

                def stats(j, r):
                    dve.wait_ge(x2_ready, j + 1)
                    V.bn_stats(st[r][:, 0:6], x2[r][:]).then_inc(stat, 1)

                def variance(j, r):
                    dve.wait_ge(stat, j + 1)
                    dve.nop(nofuse=True)
                    V.bn_aggr(st[r][:, 6:8], st[r][:, 0:6]).then_inc(var_ready, 1)

                def keep(j, r):
                    dve.wait_ge(var_ready, j + 1)
                    V.tensor_copy(c.mean_rstd[:, bass.ds(j, 1), :].rearrange("p a n -> p (a n)"),
                                  st[r][:, 6:8]).then_inc(kept, 1)

                def tile(j, r):
                    if a_tile(j):
                        add(j, r)
                    if a_tile(j - 1):
                        variance(j - 1, (r + 3) % 4)
                    if a_tile(j + 2):
                        average(dve, j + 2, (r + 2) % 4)
                    if a_tile(j - 1):
                        keep(j - 1, (r + 3) % 4)
                    if a_tile(j):
                        stats(j, r)
                invert(dve)
                staggered(dve, tile)
                variance(NT - 1, 0)
                keep(NT - 1, 0)
                dve.wait_ge(std_ready, 1)
                V.reciprocal(c.mean_rstd[:, :, 1:2], c.mean_rstd[:, :, 1:2])

            @block.scalar
            def _(act):
                staggered(act, lambda j, r: ends(act, j, r))
                act.wait_ge(kept, NT)
                nc.scalar.activation(c.mean_rstd[:, :, 1:2], c.mean_rstd[:, :, 1:2], ACT.Sqrt, bias=c.eps[:]).then_inc(std_ready, 1)

            @block.tensor
            def _(pe):
                def turn(j, r):
                    q = r % 2
                    pe.wait_ge(hT_ready, j + 1)
                    if not known_below(j, 2):
                        pe.wait_ge(x2_ready, j - 1)
                    for k in range(2):
                        t = nc.tensor.transpose(p_h[q][:, k * P:(k + 1) * P], hT[r][:, k, :], c.ident[:])
                    t.then_inc(hT_used, 1)

                def tile(j, r):
                    if a_tile(j + 1):
                        turn(j + 1, (r + 1) % 4)
                    if a_tile(j + 4):
                        spread(pe, j + 4, r)
                staggered(pe, tile)


def slice_block(c):
    nc, d = c.nc, c.d
    with ExitStack() as ctx:
        def sb(name, shape, dt=F32):
            return ctx.enter_context(nc.sbuf_tensor(name, shape, dt))

        def two(name, shape):
            return [sb(f"{name}{i}", shape) for i in range(2)]

        x2 = sb("x2", [P, NT, D])
        swT = sb("swT", [P, 4, NT * P])
        vp = sb("vp", [P, 4, D])
        with ExitStack() as inner:
            ctx_outer, ctx_in = ctx, inner
            p_sum = [inner.enter_context(nc.psum_tensor(f"p_sum{i}", [P, 512], F32)) for i in range(4)]
            bank = [inner.enter_context(nc.psum_tensor(f"bank{i}", [P, 512], F32)) for i in range(4)]
            slice_weights(c, x2, swT, p_sum, bank)
            slice_attention(c, vp, p_sum, bank)
        output(c, x2, swT, vp)


def slice_weights(c, x2, swT, p_sum, bank):
    nc, d = c.nc, c.d
    with ExitStack() as ctx:
        def two(name, shape):
            return [ctx.enter_context(nc.sbuf_tensor(f"{name}{i}", shape, F32)) for i in range(2)]

        xn = [ctx.enter_context(nc.sbuf_tensor(f"sxn{i}", [P, D + 1], F32)) for i in range(4)]
        xnT = two("sxnT", [P, 2, P])
        logit = two("logit", [P, SH, SG])
        top = two("top", [P, SH])
        low = two("low", [P, SH, SG])
        ex = two("ex", [P, SH, SG])
        total = two("total", [P, SH])
        inv = two("sinv", [P, SH])
        sw = two("sw", [P, INNER])
        p_xT, p_l, p_t = bank[0], bank[1:3], bank[3]
        in_ = sems(nc, ctx, "x2_in0", "x2_in1")
        (ones, xn_ready, xT_done, xT_ready, l_done, logit_ready, top_ready, low_ready, ex_ready, total_ready, inv_ready,
         sw_ready, t_done, swT_ready) = sems(
            nc, ctx, "ones", "sxn_ready", "sxT_done", "sxT_ready", "l_done", "logit_ready", "top_ready", "low_ready",
            "ex_ready", "total_ready", "sinv_ready", "sw_ready", "t_done", "swT_ready")

        def wide(v):
            return v.unsqueeze(2).broadcast_to([P, SH, SG])

        with nc.Block() as block:
            @block.sync
            def _(sp):
                def load(j, q):
                    if not known_below(j, 2):
                        sp.wait_ge(in_[q], (j - q) * 8)
                    sp.dma_start(x2[:, bass.ds(j, 1), :].rearrange("p a n -> p (a n)"),
                                 d["x2"][bass.ds(j * P, P), :]).then_inc(in_[q], 16)
                load(0, 0)
                load(1, 1)
                with sp.Fori(1, (NT - 1) // 2) as k:
                    load(2 * k, 0)
                    load(2 * k + 1, 1)
                load(NT - 1, 0)
                for q in range(2):
                    sp.wait_ge(in_[q], 16 * len(range(q, NT, 2)))

            @block.vector
            def _(dve):
                V = nc.vector

                def norm(j, r):
                    q = r % 2
                    dve.wait_ge(in_[q], (j - q) * 8 + 16)
                    V.tensor_scalar(xn[r][:, 0:D], x2[:, bass.ds(j, 1), :].rearrange("p a n -> p (a n)"),
                                    *(c.mean_rstd[:, bass.ds(j, 1), i:i + 1].rearrange("p a n -> p (a n)")
                                      for i in range(2)), ALU.subtract,
                                    ALU.mult).then_inc(xn_ready, 1)

                def biased(j, q):
                    dve.wait_ge(l_done, j + 1)
                    V.tensor_tensor(logit[q][:].rearrange("p h g -> p (h g)"), p_l[q][:], c.wc_bias[:],
                                    ALU.add).then_inc(logit_ready, 1)
                    dve.wait_ge(logit_ready, j + 1)
                    V.tensor_reduce(top[q][:], logit[q][:], AX.X, ALU.max).then_inc(top_ready, 1)

                def sums(j, q):
                    dve.wait_ge(ex_ready, j + 1)
                    V.tensor_reduce(total[q][:], ex[q][:], AX.X, ALU.add).then_inc(total_ready, 1)
                    dve.wait_ge(total_ready, j + 1)
                    V.reciprocal(inv[q][:], total[q][:]).then_inc(inv_ready, 1)

                def tile(j, r, ahead=4):
                    sums(j, r % 2)
                    if ahead > 3:
                        if not known_below(j, 1):
                            dve.wait_ge(t_done, j)
                        norm(j + 3, (r + 3) % 4)
                    if ahead > 2:
                        biased(j + 2, r % 2)

                for r in range(4):
                    i = V.memset(xn[r][:, D:D + 1], 1.0)
                i.then_inc(ones, 1)
                for j in range(3):
                    norm(j, j)
                biased(0, 0)
                biased(1, 1)
                for j in range(4):
                    tile(j, j)
                with dve.Fori(1, NT // 4 - 1) as k:
                    for r in range(4):
                        tile(4 * k + r, r)
                for j in range(NT - 5, NT):
                    tile(j, j % 4, ahead=NT - j)

            @block.gpsimd
            def _(pool):
                def lower(j, q):
                    pool.wait_ge(top_ready, j + 1)
                    nc.gpsimd.tensor_tensor(low[q][:], logit[q][:], wide(top[q][:]), ALU.subtract).then_inc(low_ready, 1)

                def weigh(j, q):
                    pool.wait_ge(inv_ready, j + 1)
                    nc.gpsimd.tensor_tensor(sw[q][:].rearrange("p (h g) -> p h g", h=SH), ex[q][:], wide(inv[q][:]),
                                            ALU.mult).then_inc(sw_ready, 1)
                lower(0, 0)
                lower(1, 1)
                with pool.Fori(0, (NT - 3) // 2) as k:
                    for q in range(2):
                        weigh(2 * k + q, q)
                        lower(2 * k + q + 2, q)
                weigh(NT - 3, 0)
                lower(NT - 1, 0)
                weigh(NT - 2, 1)
                weigh(NT - 1, 0)

            @block.scalar
            def _(act):
                A = nc.scalar.activation

                def copy_x(j, q):
                    act.wait_ge(xT_done, j + 1)
                    A(xnT[q][:].rearrange("p k n -> p (k n)"), p_xT[:, 0:D], ACT.Copy).then_inc(xT_ready, 1)

                def exp(j, q):
                    act.wait_ge(low_ready, j + 1)
                    A(ex[q][:], low[q][:], ACT.Exp).then_inc(ex_ready, 1)

                def keep(j, q):
                    act.wait_ge(t_done, j + 1)
                    A(swT[:, :, bass.ds(j * P, P)], p_t[:].rearrange("p (k n) -> p k n", k=4),
                      ACT.Copy).then_inc(swT_ready, 1)

                def tile(j, q, ahead=4):
                    if ahead > 3:
                        copy_x(j + 3, 1 - q)
                    keep(j, q)
                    if ahead > 2:
                        exp(j + 2, q)
                for j in range(3):
                    copy_x(j, j % 2)
                exp(0, 0)
                exp(1, 1)
                with act.Fori(0, (NT - 3) // 2) as k:
                    tile(2 * k, 0)
                    tile(2 * k + 1, 1)
                for j in range(NT - 3, NT):
                    tile(j, j % 2, ahead=NT - j)

            @block.tensor
            def _(pe):
                M, T = nc.tensor.matmul, nc.tensor.transpose

                def turn_x(j, r):
                    pe.wait_ge(xn_ready, j + 1)
                    if not known_below(j, 1):
                        pe.wait_ge(xT_ready, j)
                    for k in range(2):
                        t = T(p_xT[:, k * P:(k + 1) * P], xn[r][:, k * P:(k + 1) * P], c.ident[:])
                    t.then_inc(xT_done, 1)

                def logits(j, q):
                    pe.wait_ge(xT_ready, j + 1)
                    if not known_below(j, 2):
                        pe.wait_ge(logit_ready, j - 1)
                    for k in range(2):
                        m = M(p_l[q][:], xnT[q][:, k, :], c.wc[:, k, :], start=k == 0, stop=k == 1)
                    m.then_inc(l_done, 1)

                def slices(j, r, first=False, last=False):
                    pe.wait_ge(sw_ready, j + 1)
                    q = r % 2
                    n = TAIL if last else P
                    for s in range(4):
                        M(p_sum[s][:, 0:D + 1], sw[q][0:n, s * P:(s + 1) * P], xn[r][0:n, :], start=first, stop=last)
                    if not first:
                        pe.wait_ge(swT_ready, j)
                    for s in range(4):
                        t = T(p_t[:, s * P:(s + 1) * P], sw[q][:, s * P:(s + 1) * P], c.ident[:])
                    t.then_inc(t_done, 1)

                def tile(j, r, ahead=4):
                    if ahead > 2:
                        logits(j + 2, r % 2)
                    if ahead > 3:
                        turn_x(j + 3, (r + 3) % 4)
                    slices(j, r, first=known_below(j, 1), last=ahead == 1)
                pe.wait_ge(ones, 1)
                turn_x(0, 0)
                turn_x(1, 1)
                logits(0, 0)
                turn_x(2, 2)
                logits(1, 1)
                for j in range(4):
                    tile(j, j)
                with pe.Fori(1, NT // 4 - 1) as k:
                    for r in range(4):
                        tile(4 * k + r, r)
                for j in range(NT - 5, NT):
                    tile(j, j % 4, ahead=NT - j)


def slice_attention(c, vp, p_sum, bank):
    nc, d = c.nc, c.d
    with ExitStack() as ctx:
        def sb(name, shape, dt=F32):
            return ctx.enter_context(nc.sbuf_tensor(name, shape, dt))

        wfx = sb("wfx", [P, 2, INNER])
        bfx = sb("bfx", [1, INNER])
        wq, wk, wv = (sb(n, [SD, SD]) for n in ("wq", "wk", "wv"))
        wo = sb("wo", [SD, SH, D])
        soft = sb("soft", [P, 4, 1])
        inv = sb("ainv", [P, 4, 1])
        mean = sb("amean", [P, 4, D + 1])
        meanT = sb("ameanT", [P, 2, INNER])
        share = sb("share", [1, INNER])
        tokT, qT, kT, v, lg, ex, pr, prT, oT = (sb(n, [SD, INNER]) for n in
                                                ("tokT", "qT", "kT", "v", "lg", "aex", "pr", "prT", "oT"))
        top, tot, itot = (sb(n, [SG, SH]) for n in ("atop", "atot", "aitot"))
        loaded, v_step, p_step, exp_done = sems(nc, ctx, "a_loaded", "a_v", "a_p", "a_exp")

        DV = ["soft", "inv", "mean", "meanT", "share", "tokT", "qT", "kT", "v", "top", "low", "tot", "itot", "pr",
              "prT", "oT", "vp"]
        PE = ["meanT", "tokT", "qT", "kT", "v", "lg", "prT", "oT", "vp"]

        def dv(n):
            return DV.index(n) + 1

        def pp(n):
            return PE.index(n) + 1

        def heads(t):
            return t[:].rearrange("p (h g) -> p h g", h=SH)

        with nc.Block() as block:
            @block.sync
            def _(sp):
                for k in range(2):
                    sp.dma_start(wfx[:, k, :], d["W_fx"][k * P:(k + 1) * P, :]).then_inc(loaded, 16)
                sp.dma_start(bfx[:], d["b_fx"].unsqueeze(0)).then_inc(loaded, 16)
                for t, n in ((wq, "W_q"), (wk, "W_k"), (wv, "W_v")):
                    sp.dma_start(t[:], d[n]).then_inc(loaded, 16)
                sp.dma_start(wo[:], d["W_out"].rearrange("(h c) n -> c h n", c=SD)).then_inc(loaded, 16)

            @block.vector
            def _(dve):
                V = nc.vector

                def step(name, ins):
                    ins.then_inc(v_step, 1)
                    dve.wait_ge(v_step, dv(name))

                for s in range(4):
                    i = V.tensor_scalar(soft[:, s, :], p_sum[s][:, D:D + 1], 1e-5, None, ALU.add)
                step("soft", i)
                step("inv", V.reciprocal(inv[:, :, 0], soft[:, :, 0]))
                for s in range(4):
                    i = V.tensor_scalar(mean[:, s, :], p_sum[s][:, 0:D + 1], inv[:, s, :], None, ALU.mult)
                step("mean", i)
                dve.wait_ge(p_step, pp("meanT"))
                V.tensor_copy(meanT[:, 0, :], bank[0][:])
                step("meanT", V.tensor_copy(meanT[:, 1, :], bank[1][:]))
                step("share", V.tensor_copy(share[:], bank[2][0:1, :]))
                for name, t, b in (("tokT", tokT, 3), ("qT", qT, 0), ("kT", kT, 1), ("v", v, 2)):
                    dve.wait_ge(p_step, pp(name))
                    step(name, V.tensor_copy(t[:], bank[b][0:SD, :]))
                dve.wait_ge(p_step, pp("lg"))
                step("top", V.tensor_reduce(top[:], bank[3][0:SD, :].rearrange("p (h g) -> p h g", h=SH), AX.X, ALU.max))
                step("low", V.tensor_tensor(heads(lg), bank[3][0:SD, :].rearrange("p (h g) -> p h g", h=SH),
                                            top[:].unsqueeze(2).broadcast_to([SG, SH, SG]), ALU.subtract))
                dve.wait_ge(exp_done, 1)
                step("tot", V.tensor_reduce(tot[:], heads(ex), AX.X, ALU.add))
                step("itot", V.reciprocal(itot[:], tot[:]))
                step("pr", V.tensor_tensor(heads(pr), heads(ex), itot[:].unsqueeze(2).broadcast_to([SG, SH, SG]), ALU.mult))
                dve.wait_ge(p_step, pp("prT"))
                step("prT", V.tensor_copy(prT[:], bank[0][0:SD, :]))
                dve.wait_ge(p_step, pp("oT"))
                step("oT", V.tensor_copy(oT[:], bank[1][0:SD, :]))
                dve.wait_ge(p_step, pp("vp"))
                for h in range(SH):
                    i = V.tensor_copy(vp[64 * (h % 2):64 * (h % 2) + 64, h // 2, :],
                                      p_sum[h // 2][0:SG, (h % 2) * D:(h % 2 + 1) * D])
                step("vp", i)

            @block.scalar
            def _(act):
                act.wait_ge(v_step, dv("low"))
                nc.scalar.activation(ex[:], lg[:], ACT.Exp, scale=float(SD) ** -0.5).then_inc(exp_done, 1)

            @block.tensor
            def _(pe):
                M, T = nc.tensor.matmul, nc.tensor.transpose
                at = [slice(h * SG, (h + 1) * SG) for h in range(SH)]
                pe.wait_ge(v_step, dv("mean"))
                for s in range(4):
                    for k in range(2):
                        T(bank[k][:, s * P:(s + 1) * P], mean[:, s, k * P:(k + 1) * P], c.ident[:])
                    i = T(bank[2][0:1, s * P:(s + 1) * P], mean[:, s, D:D + 1], c.ident[:])
                i.then_inc(p_step, 1)
                pe.wait_ge(loaded, 16 * 7)
                pe.wait_ge(v_step, dv("share"))
                for h in range(SH):
                    for k in range(2):
                        M(bank[3][0:SD, at[h]], wfx[:, k, at[h]], meanT[:, k, at[h]], start=k == 0, stop=False)
                    i = M(bank[3][0:SD, at[h]], bfx[:, at[h]], share[:, at[h]], start=False, stop=True)
                i.then_inc(p_step, 1)
                pe.wait_ge(v_step, dv("tokT"))
                M(bank[0][0:SD, :], wq[:], tokT[:], start=True, stop=True).then_inc(p_step, 1)
                M(bank[1][0:SD, :], wk[:], tokT[:], start=True, stop=True).then_inc(p_step, 1)
                for h in range(SH):
                    i = M(bank[2][0:SG, at[h]], tokT[:, at[h]], wv[:], start=True, stop=True)
                i.then_inc(p_step, 1)
                pe.wait_ge(v_step, dv("kT"))
                for h in range(SH):
                    i = M(bank[3][0:SG, at[h]], qT[:, at[h]], kT[:, at[h]], start=True, stop=True)
                i.then_inc(p_step, 1)
                pe.wait_ge(v_step, dv("pr"))
                for h in range(SH):
                    i = T(bank[0][0:SG, at[h]], pr[:, at[h]], c.ident[0:SG, 0:SG])
                i.then_inc(p_step, 1)
                pe.wait_ge(v_step, dv("prT"))
                for h in range(SH):
                    i = M(bank[1][0:SD, at[h]], v[:, at[h]], prT[:, at[h]], start=True, stop=True)
                i.then_inc(p_step, 1)
                pe.wait_ge(v_step, dv("oT"))
                for h in range(SH):
                    i = M(p_sum[h // 2][0:SG, (h % 2) * D:(h % 2 + 1) * D], oT[:, at[h]], wo[:, h, :], start=True, stop=True)
                i.then_inc(p_step, 1)


def output(c, x2, swT, vp):
    nc, d = c.nc, c.d
    with ExitStack() as ctx:
        def two(name, shape):
            return [ctx.enter_context(nc.sbuf_tensor(f"{name}{i}", shape, F32)) for i in range(2)]

        w = two("w_now", [P, 4, P])
        xb = two("xb", [P, D])
        y = two("y", [P, D])
        p_y = [ctx.enter_context(nc.psum_tensor(f"p_y{i}", [P, 512], F32)) for i in range(2)]
        w_ready, xb_ready, y_done, y_ready = sems(nc, ctx, "w_now_ready", "xb_ready", "y_done", "y_ready")
        stored = sems(nc, ctx, "y_stored0", "y_stored1")
        with nc.Block() as block:
            @block.scalar
            def _(act):
                def copy(j, q):
                    if not known_below(j, 2):
                        act.wait_ge(y_done, j - 1)
                    nc.scalar.activation(w[q][:], swT[:, :, bass.ds(j * P, P)], ACT.Copy).then_inc(w_ready, 1)
                copy(0, 0)
                copy(1, 1)
                with act.Fori(1, (NT - 1) // 2) as k:
                    copy(2 * k, 0)
                    copy(2 * k + 1, 1)
                copy(NT - 1, 0)

            @block.gpsimd
            def _(pool):
                def add(j, q):
                    if not known_below(j, 2):
                        pool.wait_ge(y_ready, j - 1)
                    nc.gpsimd.tensor_tensor(xb[q][:], x2[:, bass.ds(j, 1), :].rearrange("p a n -> p (a n)"), c.b_out[:],
                                            ALU.add).then_inc(xb_ready, 1)
                add(0, 0)
                add(1, 1)
                with pool.Fori(1, (NT - 1) // 2) as k:
                    add(2 * k, 0)
                    add(2 * k + 1, 1)
                add(NT - 1, 0)

            @block.tensor
            def _(pe):
                def mm(j, q):
                    pe.wait_ge(w_ready, j + 1)
                    if not known_below(j, 2):
                        pe.wait_ge(y_ready, j - 1)
                    for s in range(4):
                        m = nc.tensor.matmul(p_y[q][:, 0:D], w[q][:, s, :], vp[:, s, :], start=s == 0, stop=s == 3)
                    m.then_inc(y_done, 1)
                mm(0, 0)
                mm(1, 1)
                with pe.Fori(1, (NT - 1) // 2) as k:
                    mm(2 * k, 0)
                    mm(2 * k + 1, 1)
                mm(NT - 1, 0)

            @block.vector
            def _(dve):
                def add(j, q):
                    if not known_below(j, 2):
                        dve.wait_ge(stored[q], (j - q) * 8)
                    dve.wait_ge(xb_ready, j + 1)
                    dve.wait_ge(y_done, j + 1)
                    nc.vector.tensor_tensor(y[q][:], p_y[q][:, 0:D], xb[q][:], ALU.add).then_inc(y_ready, 1)
                add(0, 0)
                add(1, 1)
                with dve.Fori(1, (NT - 1) // 2) as k:
                    add(2 * k, 0)
                    add(2 * k + 1, 1)
                add(NT - 1, 0)

            @block.sync
            def _(sp):
                def store(j, q, n=P):
                    sp.wait_ge(y_ready, j + 1)
                    sp.dma_start(d["out"][bass.ds(j * P, n), :], y[q][0:n, :]).then_inc(stored[q], 16)
                with sp.Fori(0, (NT - 1) // 2) as k:
                    store(2 * k, 0)
                    store(2 * k + 1, 1)
                store(NT - 1, 0, TAIL)
                for q in range(2):
                    sp.wait_ge(stored[q], 16 * len(range(q, NT, 2)))


def build(nc, dram):
    with ExitStack() as ctx:
        c = Core(nc, ctx, dram)
        seq = dram["dst_seq"]
        dram["dst_over"] = bass.AP(seq.tensor, seq.offset, [[P, ET], [1, P + 2]])
        c.ident = c.sb("ident", [P, P])
        c.iota = c.sb("iota", [P, P])
        c.eps = c.sb("eps", [P, 1])
        c.wc = c.sb("wc", [P, 2, INNER])
        c.wc_bias = c.sb("wc_bias", [P, INNER])
        c.inv_temp = c.sb("inv_temp", [P, SH])
        c.b_out = c.sb("b_out", [P, D])
        c.mean_rstd = c.sb("mean_rstd", [P, NT, 2])
        c.start = c.sb("start", [P, NT])
        with ExitStack() as gnn:
            c.ctx = gnn
            c.idx = c.sb("idx", [P, ET], I32)
            c.rel = c.sb("rel", [P, ET])
            c.first_id = c.sb("first_id", [P, 1], I32)
            c.base = c.sb("base", [1, ET], I32)
            c.not_start = c.sb("not_start", [P, EPP])
            c.go_on = c.sb("go_on", [HEADS, ET])
            c.pass_on = c.sb("pass_on", [HEADS, ET])
            c.is_head = c.sb("is_head", [P, HEADS])
            c.is_tile = c.sb("is_tile", [P, TPB])
            c.to_rows = c.sb("to_rows", [P, 3, P])
            c.head_rows = c.sb("head_rows", [HEADS, D])
            c.head_parts = c.sb("head_parts", [HEADS, BP])
            c.gext2 = c.sb("gext2", [P, 2, ROW])
            c.gat_b = c.sb("gat_b", [P, 2, 2])
            with ExitStack() as enc:
                c.ctx = enc
                c.w1a = c.sb("w1a", [P, 2, FF])
                c.label_rows = c.sb("label_rows", [96, FF], BF16)
                c.klass = c.sb("klass", [P, 1])
                c.fused = c.sb("fused", [P, 8, ROW])
                c.bias1 = c.sb("bias1", [P, ROW])
                c.ln_g = c.sb("ln_g", [P, 8])
                c.ln_b = c.sb("ln_b", [P, 8])
                c.nid = c.sb("nid", [P, NT])
                c.base_bc = c.sb("base_bc", [P, ET])
                constants_and_weights(c)
                encode(c)
            c.ctx = gnn
            c.acc = c.sb("acc", [P, 3, NW])
            edges(c, 1)
            second_features(c)
            edges(c, 2)
            join(c)
        slice_block(c)


_GNN = ["emb", "le_W1", "le_b1", "ln_g", "ln_b", "le_W2", "le_b2", "W1", "al1", "ar1", "b1", "W2", "al2", "ar2", "b2"]
_FFN = ["W_fx", "b_fx", "W_x", "b_x", "W_slice", "b_slice", "W_q", "W_k", "W_v", "W_out", "b_out", "temperature"]
_OUT_OF_PLACE = {"emb": "embT", "le_W1": "le_W1T", "W_x": "W_xT"}


def kernel(**inputs):
    import numpy as np
    import concourse.bacc as bacc
    from concourse.bass_utils import run_bass_kernel_spmd

    pad = EP - E
    src, dst = np.asarray(inputs["src"]), np.asarray(inputs["dst"])
    arrays = {
        "x": inputs["x"],
        "src": np.concatenate([src, np.zeros(pad, src.dtype)]).reshape(ET, P),
        "dst": np.concatenate([dst, np.full(pad, N, dst.dtype)]).reshape(ET, P),
        "dst_seq": np.concatenate([np.full(1, -1, dst.dtype), dst, np.full(pad + 1, N, dst.dtype)]),
        "labels": np.concatenate([np.asarray(inputs["node_type_24"]), np.zeros(NT * P - N, np.int32)]),
    }
    for n in _GNN:
        arrays[_OUT_OF_PLACE.get(n, n)] = np.asarray(inputs["L0_gnn_" + n])
    for n in _FFN:
        arrays[_OUT_OF_PLACE.get(n, n)] = np.asarray(inputs["L0_ffn_" + n])
    for n in _OUT_OF_PLACE.values():
        arrays[n] = arrays[n].T
    arrays["W1T"], arrays["W2T"] = arrays["W1"].T, arrays["W2"].T
    arrays["temperature"] = arrays["temperature"].reshape(-1)
    arrays = {f"in_{n}": np.ascontiguousarray(a) for n, a in arrays.items()}

    nc = bacc.Bacc("TRN2", target_bir_lowering=False, num_devices=1)
    dram = {n[3:]: nc.dram_tensor(n, a.shape, mybir.dt.from_np(a.dtype), kind="ExternalInput").ap()
            for n, a in arrays.items()}
    for i in (1, 2):
        dram[f"table{i}"] = nc.dram_tensor(f"table{i}", [NT * P, ROW], F32, kind="Internal").ap()
        dram[f"er_start{i}"] = nc.dram_tensor(f"er_start{i}", [EP, HEADS], F32, kind="Internal").ap()
        dram[f"er_edge{i}"] = nc.dram_tensor(f"er_edge{i}", [HEADS, EP], F32, kind="Internal").ap()
    dram["weight_sums"] = nc.dram_tensor("weight_sums", [HEADS, NT * P], F32, kind="Internal").ap()
    dram["x2"] = nc.dram_tensor("x2_rows", [NT * P, D], F32, kind="Internal").ap()
    dram["out"] = nc.dram_tensor("out_0", [N, D], F32, kind="ExternalOutput").ap()
    build(nc, dram)
    return run_bass_kernel_spmd(nc, [arrays], core_ids=[0]).results[0]["out_0"]
```
